# Optimizing a Trainium2 kernel written in Bass

```python
import numpy as np
import jax
import jax.numpy as jnp

def _softmax(x, axis=-1):
    return jax.nn.softmax(x, axis=axis)

def _gelu(x):
    return jax.nn.gelu(x, approximate=True)

def _silu(x):
    return jax.nn.silu(x)

def _sigmoid(x):
    return jax.nn.sigmoid(x)

def _layernorm(x, axis=-1, eps=1e-05):
    m = jnp.mean(x, axis=axis, keepdims=True)
    v = jnp.var(x, axis=axis, keepdims=True)
    return (x - m) / jnp.sqrt(v + eps)

def _scatter_add(tgt, idx, src, axis=0):
    return tgt.at[idx].add(src)

def _segment_sum(src, seg, n):
    return jax.ops.segment_sum(src, seg, n)
kernel_name = 'mk_decoder_postln_d1_seqx_r4_fe458a'

def setup_inputs(seed: int=0):
    np.random.seed(seed)
    _w = jnp.asarray

    def _rec_inputs():
        import jax
        import jax.numpy as jnp
        _rk = jax.random.key(seed)
        x = 7.22e-05 + 1 * jax.random.normal(jax.random.fold_in(_rk, 1), (4, 1024, 256), jnp.float32)
        _lenS = 1024 - jax.random.randint(jax.random.fold_in(_rk, 7), (4,), 0, max(1, 1024 // 4) + 1, jnp.int32)
        _lenS2 = 77 - jax.random.randint(jax.random.fold_in(_rk, 8), (4,), 0, max(1, 77 // 4) + 1, jnp.int32)
        _ctx_1024P = jax.random.normal(jax.random.fold_in(_rk, 11), (4, 16, 256), jnp.float32)
        _ctx_1024c = jax.random.dirichlet(jax.random.fold_in(_rk, 511), 0.3 * jnp.ones((16,), jnp.float32), (4, 77))
        _ctx_1024t = jnp.einsum('bsk,bkd->bsd', _ctx_1024c, _ctx_1024P)
        _ctx_1024t = _ctx_1024t * jax.lax.rsqrt(jnp.mean(jnp.square(_ctx_1024t)) + 1e-12) * 0.953939
        ctx_1024 = 4.13588e-05 + 0.999923 * (_ctx_1024t + 0.3 * jax.random.normal(jax.random.fold_in(_rk, 611), (4, 77, 256), jnp.float32))
        return (x, ctx_1024, _lenS2)
    x, ctx_1024, _lenS2 = _rec_inputs()

    def _L0_attn_setup():
        import jax, jax.numpy as jnp
        import numpy as np
        D = 256
        H = 4
        DK = D
        DV = 2 * D
        HK = DK // H
        HV = DV // H
        KCONV = 4
        EPS = 1e-05
        CHUNK = 64

        def causal_conv_silu(x, w):
            B, T, C = x.shape
            K = w.shape[1]
            xp = jnp.pad(x, ((0, 0), (K - 1, 0), (0, 0)))
            y = sum((xp[:, i:i + T, :] * w[:, i] for i in range(K)))
            return jax.nn.silu(y)

        def l2norm(x):
            return x * jax.lax.rsqrt(jnp.sum(x * x, -1, keepdims=True) + 1e-06)

        def _step(S, inp):
            q_t, k_t, v_t, g_t, b_t = inp
            S = S * jnp.exp(g_t)[..., None, None]
            v_eff = (v_t - jnp.einsum('bhk,bhkv->bhv', k_t, S)) * b_t[..., None]
            S = S + k_t[..., None] * v_eff[..., None, :]
            o_t = jnp.einsum('bhk,bhkv->bhv', q_t, S)
            return (S, o_t)

        @jax.checkpoint
        def _chunk(S, ch):
            return jax.lax.scan(_step, S, ch)

        def _forward(x, ln_w, ln_b, Wq, Wk, Wv, conv_q, conv_k, conv_v, Wb, Wa, A_log, dt_bias, Wg, norm_w, Wo):
            B, T, _ = x.shape
            mu = jnp.mean(x, -1, keepdims=True)
            var = jnp.mean((x - mu) ** 2, -1, keepdims=True)
            normed = (x - mu) * jax.lax.rsqrt(var + EPS) * ln_w + ln_b
            q = causal_conv_silu(normed @ Wq, conv_q)
            k = causal_conv_silu(normed @ Wk, conv_k)
            v = causal_conv_silu(normed @ Wv, conv_v)
            beta = jax.nn.sigmoid(normed @ Wb)
            g = -jnp.exp(A_log) * jax.nn.softplus(normed @ Wa + dt_bias)
            q = l2norm(q.reshape(B, T, H, HK)) * HK ** (-0.5)
            k = l2norm(k.reshape(B, T, H, HK))
            v = v.reshape(B, T, H, HV)
            nc = T // CHUNK

            def to_chunks(a):
                return jnp.moveaxis(a, 1, 0).reshape((nc, CHUNK, B) + a.shape[2:])
            qc, kc, vc, gc, bc = map(to_chunks, (q, k, v, g, beta))
            S0 = jnp.zeros((B, H, HK, HV), x.dtype)
            _, o = jax.lax.scan(_chunk, S0, (qc, kc, vc, gc, bc))
            o = jnp.moveaxis(o.reshape(T, B, H, HV), 0, 1)
            g_out = (normed @ Wg).reshape(B, T, H, HV)
            o = o * jax.lax.rsqrt(jnp.mean(o * o, -1, keepdims=True) + EPS) * norm_w
            o = o * g_out * jax.nn.sigmoid(g_out)
            return x + o.reshape(B, T, DV) @ Wo
        key = jax.random.key(seed)
        ks = jax.random.split(key, 16)
        B, T = (4, 512)
        p = lambda k, shape, s=0.02: jax.random.normal(k, shape, jnp.float32) * s
        return {'x': jax.random.normal(ks[0], (B, T, D), jnp.float32), 'ln_w': jnp.ones((D,), jnp.float32), 'ln_b': jnp.zeros((D,), jnp.float32), 'Wq': p(ks[1], (D, DK)), 'Wk': p(ks[2], (D, DK)), 'Wv': p(ks[3], (D, DV)), 'conv_q': p(ks[4], (DK, KCONV), 0.1), 'conv_k': p(ks[5], (DK, KCONV), 0.1), 'conv_v': p(ks[6], (DV, KCONV), 0.1), 'Wb': p(ks[7], (D, H)), 'Wa': p(ks[8], (D, H)), 'A_log': jnp.log(jax.random.uniform(ks[9], (H,), jnp.float32, 1.0, 16.0)), 'dt_bias': jnp.log(jnp.expm1(jax.random.uniform(ks[10], (H,), jnp.float32, 0.001, 0.1))), 'Wg': p(ks[11], (D, DV)), 'norm_w': jnp.ones((HV,), jnp.float32), 'Wo': p(ks[12], (DV, D))}
    _L0_attn_all = _L0_attn_setup()
    _L0_attn_in = {k: v for k, v in _L0_attn_all.items() if k in ('ln_w', 'ln_b', 'Wq', 'Wk', 'Wv', 'conv_q', 'conv_k', 'conv_v', 'Wb', 'Wa', 'A_log', 'dt_bias', 'Wg', 'norm_w', 'Wo')}
    del _L0_attn_all

    def _L0_xattn_setup():
        import jax, jax.numpy as jnp
        import numpy as np
        DIM, HEADS, HEAD_DIM = (256, 16, 64)
        B, L, S = (4, 512, 512)
        EPS = 1e-05
        NEG_INF = -1000000000.0

        def rms_norm(x, w):
            var = jnp.mean(jnp.square(x), axis=-1, keepdims=True)
            return x * jax.lax.rsqrt(var + EPS) * w
        key = jax.random.key(seed)
        ks = jax.random.split(key, 9)
        hd = HEADS * HEAD_DIM
        scale = 1.0 / np.sqrt(DIM)
        return {'q': jax.random.normal(ks[0], (B, L, DIM), dtype=jnp.float32), 'kv': jax.random.normal(ks[1], (B, S, DIM), dtype=jnp.float32), 'x_seqlens': jax.random.randint(ks[2], (B,), 1, S + 1, dtype=jnp.int32), 'Wq': jax.random.normal(ks[3], (DIM, hd), dtype=jnp.float32) * scale, 'Wk': jax.random.normal(ks[4], (DIM, hd), dtype=jnp.float32) * scale, 'Wv': jax.random.normal(ks[5], (DIM, hd), dtype=jnp.float32) * scale, 'Wo': jax.random.normal(ks[6], (hd, DIM), dtype=jnp.float32) * (1.0 / np.sqrt(hd)), 'q_norm_w': jnp.ones((HEAD_DIM,), dtype=jnp.float32), 'k_norm_w': jnp.ones((HEAD_DIM,), dtype=jnp.float32)}
    _L0_xattn_all = _L0_xattn_setup()
    _L0_xattn_in = {k: v for k, v in _L0_xattn_all.items() if k in ('Wq', 'Wk', 'Wv', 'Wo', 'q_norm_w', 'k_norm_w')}
    del _L0_xattn_all

    def _L0_ffn_setup():
        import jax, jax.numpy as jnp
        import numpy as np
        D_MODEL, D_FF, N_EXPERTS, TOP_K = (256, 512, 8, 2)
        B, S = (2, 512)
        key = jax.random.key(seed)
        ks = jax.random.split(key, 6)
        sd = 1.0 / np.sqrt(D_MODEL)
        sf = 1.0 / np.sqrt(D_FF)
        return {'x': jax.random.normal(ks[0], (B, S, D_MODEL), jnp.float32), 'router_w': jax.random.normal(ks[1], (N_EXPERTS, D_MODEL), jnp.float32) * sd, 'gate_w': jax.random.normal(ks[2], (N_EXPERTS, D_MODEL, D_FF), jnp.float32) * sd, 'gate_b': jnp.zeros((N_EXPERTS, D_FF), jnp.float32), 'up_w': jax.random.normal(ks[3], (N_EXPERTS, D_MODEL, D_FF), jnp.float32) * sd, 'up_b': jnp.zeros((N_EXPERTS, D_FF), jnp.float32), 'down_w': jax.random.normal(ks[4], (N_EXPERTS, D_FF, D_MODEL), jnp.float32) * sf, 'down_b': jnp.zeros((N_EXPERTS, D_MODEL), jnp.float32)}
    _L0_ffn_all = _L0_ffn_setup()
    _L0_ffn_in = {k: v for k, v in _L0_ffn_all.items() if k in ('router_w', 'gate_w', 'gate_b', 'up_w', 'up_b', 'down_w', 'down_b')}
    del _L0_ffn_all
    return {'x': x, 'ctx_1024': ctx_1024, '_lenS2': _lenS2, 'L0_attn_ln_w': _L0_attn_in['ln_w'], 'L0_attn_ln_b': _L0_attn_in['ln_b'], 'L0_attn_Wq': _L0_attn_in['Wq'], 'L0_attn_Wk': _L0_attn_in['Wk'], 'L0_attn_Wv': _L0_attn_in['Wv'], 'L0_attn_conv_q': _L0_attn_in['conv_q'], 'L0_attn_conv_k': _L0_attn_in['conv_k'], 'L0_attn_conv_v': _L0_attn_in['conv_v'], 'L0_attn_Wb': _L0_attn_in['Wb'], 'L0_attn_Wa': _L0_attn_in['Wa'], 'L0_attn_A_log': _L0_attn_in['A_log'], 'L0_attn_dt_bias': _L0_attn_in['dt_bias'], 'L0_attn_Wg': _L0_attn_in['Wg'], 'L0_attn_norm_w': _L0_attn_in['norm_w'], 'L0_attn_Wo': _L0_attn_in['Wo'], 'L0_xattn_Wq': _L0_xattn_in['Wq'], 'L0_xattn_Wk': _L0_xattn_in['Wk'], 'L0_xattn_Wv': _L0_xattn_in['Wv'], 'L0_xattn_Wo': _L0_xattn_in['Wo'], 'L0_xattn_q_norm_w': _L0_xattn_in['q_norm_w'], 'L0_xattn_k_norm_w': _L0_xattn_in['k_norm_w'], 'L0_ffn_router_w': _L0_ffn_in['router_w'], 'L0_ffn_gate_w': _L0_ffn_in['gate_w'], 'L0_ffn_gate_b': _L0_ffn_in['gate_b'], 'L0_ffn_up_w': _L0_ffn_in['up_w'], 'L0_ffn_up_b': _L0_ffn_in['up_b'], 'L0_ffn_down_w': _L0_ffn_in['down_w'], 'L0_ffn_down_b': _L0_ffn_in['down_b']}

def reference(x, ctx_1024, _lenS2, L0_attn_ln_w, L0_attn_ln_b, L0_attn_Wq, L0_attn_Wk, L0_attn_Wv, L0_attn_conv_q, L0_attn_conv_k, L0_attn_conv_v, L0_attn_Wb, L0_attn_Wa, L0_attn_A_log, L0_attn_dt_bias, L0_attn_Wg, L0_attn_norm_w, L0_attn_Wo, L0_xattn_Wq, L0_xattn_Wk, L0_xattn_Wv, L0_xattn_Wo, L0_xattn_q_norm_w, L0_xattn_k_norm_w, L0_ffn_router_w, L0_ffn_gate_w, L0_ffn_gate_b, L0_ffn_up_w, L0_ffn_up_b, L0_ffn_down_w, L0_ffn_down_b):
    import jax
    import jax.numpy as jnp

    def _L0_attn_ref(x, ln_w, ln_b, Wq, Wk, Wv, conv_q, conv_k, conv_v, Wb, Wa, A_log, dt_bias, Wg, norm_w, Wo):
        import jax, jax.numpy as jnp
        import numpy as np
        D = 256
        H = 4
        DK = D
        DV = 2 * D
        HK = DK // H
        HV = DV // H
        KCONV = 4
        EPS = 1e-05
        CHUNK = 64

        def causal_conv_silu(x, w):
            B, T, C = x.shape
            K = w.shape[1]
            xp = jnp.pad(x, ((0, 0), (K - 1, 0), (0, 0)))
            y = sum((xp[:, i:i + T, :] * w[:, i] for i in range(K)))
            return jax.nn.silu(y)

        def l2norm(x):
            return x * jax.lax.rsqrt(jnp.sum(x * x, -1, keepdims=True) + 1e-06)

        def _step(S, inp):
            q_t, k_t, v_t, g_t, b_t = inp
            S = S * jnp.exp(g_t)[..., None, None]
            v_eff = (v_t - jnp.einsum('bhk,bhkv->bhv', k_t, S)) * b_t[..., None]
            S = S + k_t[..., None] * v_eff[..., None, :]
            o_t = jnp.einsum('bhk,bhkv->bhv', q_t, S)
            return (S, o_t)

        @jax.checkpoint
        def _chunk(S, ch):
            return jax.lax.scan(_step, S, ch)

        def _forward(x, ln_w, ln_b, Wq, Wk, Wv, conv_q, conv_k, conv_v, Wb, Wa, A_log, dt_bias, Wg, norm_w, Wo):
            B, T, _ = x.shape
            mu = jnp.mean(x, -1, keepdims=True)
            var = jnp.mean((x - mu) ** 2, -1, keepdims=True)
            normed = (x - mu) * jax.lax.rsqrt(var + EPS) * ln_w + ln_b
            q = causal_conv_silu(normed @ Wq, conv_q)
            k = causal_conv_silu(normed @ Wk, conv_k)
            v = causal_conv_silu(normed @ Wv, conv_v)
            beta = jax.nn.sigmoid(normed @ Wb)
            g = -jnp.exp(A_log) * jax.nn.softplus(normed @ Wa + dt_bias)
            q = l2norm(q.reshape(B, T, H, HK)) * HK ** (-0.5)
            k = l2norm(k.reshape(B, T, H, HK))
            v = v.reshape(B, T, H, HV)
            nc = T // CHUNK

            def to_chunks(a):
                return jnp.moveaxis(a, 1, 0).reshape((nc, CHUNK, B) + a.shape[2:])
            qc, kc, vc, gc, bc = map(to_chunks, (q, k, v, g, beta))
            S0 = jnp.zeros((B, H, HK, HV), x.dtype)
            _, o = jax.lax.scan(_chunk, S0, (qc, kc, vc, gc, bc))
            o = jnp.moveaxis(o.reshape(T, B, H, HV), 0, 1)
            g_out = (normed @ Wg).reshape(B, T, H, HV)
            o = o * jax.lax.rsqrt(jnp.mean(o * o, -1, keepdims=True) + EPS) * norm_w
            o = o * g_out * jax.nn.sigmoid(g_out)
            return x + o.reshape(B, T, DV) @ Wo
        return _forward(x, ln_w, ln_b, Wq, Wk, Wv, conv_q, conv_k, conv_v, Wb, Wa, A_log, dt_bias, Wg, norm_w, Wo)

    def _L0_xattn_ref(q, kv, x_seqlens, Wq, Wk, Wv, Wo, q_norm_w, k_norm_w):
        import jax, jax.numpy as jnp
        import numpy as np
        DIM, HEADS, HEAD_DIM = (256, 16, 64)
        B, L, S = (4, 512, 512)
        EPS = 1e-05
        NEG_INF = -1000000000.0

        def rms_norm(x, w):
            var = jnp.mean(jnp.square(x), axis=-1, keepdims=True)
            return x * jax.lax.rsqrt(var + EPS) * w
        b, l, _ = q.shape
        s = kv.shape[1]
        qh = (q @ Wq).reshape(b, l, HEADS, HEAD_DIM).transpose(0, 2, 1, 3)
        kh = (kv @ Wk).reshape(b, s, HEADS, HEAD_DIM).transpose(0, 2, 1, 3)
        vh = (kv @ Wv).reshape(b, s, HEADS, HEAD_DIM).transpose(0, 2, 1, 3)
        qh = rms_norm(qh, q_norm_w)
        kh = rms_norm(kh, k_norm_w)
        mask = (jnp.arange(s, dtype=jnp.int32)[None, :] < x_seqlens[:, None])[:, None, None, :]
        scores = jnp.einsum('bhld,bhsd->bhls', qh, kh) * (1.0 / np.sqrt(HEAD_DIM))
        scores = jnp.where(mask, scores, NEG_INF)
        attn = jax.nn.softmax(scores, axis=-1)
        o = jnp.einsum('bhls,bhsd->bhld', attn, vh)
        o = o.transpose(0, 2, 1, 3).reshape(b, l, HEADS * HEAD_DIM)
        return o @ Wo

    def _L0_ffn_ref(x, router_w, gate_w, gate_b, up_w, up_b, down_w, down_b):
        import jax, jax.numpy as jnp
        import numpy as np
        D_MODEL, D_FF, N_EXPERTS, TOP_K = (256, 512, 8, 2)
        B, S = (2, 512)
        b, s, d = x.shape
        xf = x.reshape(b * s, d)
        n = xf.shape[0]
        router_logits = xf @ router_w.T
        probs = jax.nn.softmax(router_logits, axis=-1)
        topv, topi = jax.lax.top_k(probs, TOP_K)
        mask = jnp.zeros_like(probs).at[jnp.arange(n)[:, None], topi].set(1.0)
        probs = probs * mask
        probs = probs / (probs.sum(axis=-1, keepdims=True) + 1e-09)
        g = jnp.einsum('nd,edf->nef', xf, gate_w) + gate_b
        u = jnp.einsum('nd,edf->nef', xf, up_w) + up_b
        h = jax.nn.silu(g) * u
        expert_out = jnp.einsum('nef,efd->ned', h, down_w) + down_b
        y = jnp.einsum('ne,ned->nd', probs, expert_out)
        return y.reshape(b, s, d)
    x = _layernorm(x + _L0_attn_ref(x, L0_attn_ln_w, L0_attn_ln_b, L0_attn_Wq, L0_attn_Wk, L0_attn_Wv, L0_attn_conv_q, L0_attn_conv_k, L0_attn_conv_v, L0_attn_Wb, L0_attn_Wa, L0_attn_A_log, L0_attn_dt_bias, L0_attn_Wg, L0_attn_norm_w, L0_attn_Wo), axis=-1)
    x = _layernorm(x + _L0_xattn_ref(x, ctx_1024, _lenS2, L0_xattn_Wq, L0_xattn_Wk, L0_xattn_Wv, L0_xattn_Wo, L0_xattn_q_norm_w, L0_xattn_k_norm_w), axis=-1)
    x = _layernorm(x + _L0_ffn_ref(x, L0_ffn_router_w, L0_ffn_gate_w, L0_ffn_gate_b, L0_ffn_up_w, L0_ffn_up_b, L0_ffn_down_w, L0_ffn_down_b), axis=-1)
    return x

_drawn_inputs = setup_inputs


def setup_inputs(seed=0):
    import zlib

    import numpy as np

    out = dict(_drawn_inputs(seed))
    spreads = {'L0_attn_ln_w': (1.0, 0.6),
     'L0_attn_ln_b': (0.0, 0.8),
     'L0_attn_norm_w': (1.0, 0.6),
     'L0_xattn_q_norm_w': (1.0, 0.2),
     'L0_xattn_k_norm_w': (1.0, 0.2),
     'L0_ffn_gate_b': (0.0, 0.1),
     'L0_ffn_up_b': (0.0, 0.1),
     'L0_ffn_down_b': (0.0, 0.1)}
    factors = {'L0_attn_Wq': 3.228,
     'L0_attn_Wk': 3.695,
     'L0_attn_Wv': 3.281,
     'L0_attn_conv_q': 3.483,
     'L0_attn_conv_k': 3.147,
     'L0_attn_conv_v': 3.232,
     'L0_attn_Wb': 8.0,
     'L0_attn_Wa': 8.0,
     'L0_attn_A_log': 7.654,
     'L0_attn_dt_bias': 7.289,
     'L0_attn_Wg': 3.061,
     'L0_attn_Wo': 3.493}
    for name, (base, spread) in spreads.items():
        noise = np.random.default_rng([zlib.crc32(name.encode()), seed]).standard_normal(out[name].shape)
        drawn = base * np.exp(spread * noise) if base else spread * noise
        out[name] = jnp.asarray(drawn.astype(out[name].dtype))
    for name, factor in factors.items():
        out[name] = (out[name] * factor).astype(out[name].dtype)
    return out
```

```python
from contextlib import ExitStack, contextmanager

import numpy as np

import concourse.bass as bass
from concourse import mybir

P = 128
F32 = mybir.dt.float32
I32 = mybir.dt.int32
ALU = mybir.AluOpType
ACT = mybir.ActivationFunctionType
AX_X = mybir.AxisListType.X

BATCH, SEQ, D = 4, 1024, 256
KD = D // P
TILES = BATCH * SEQ // P
BLK = 4
BT = BLK * P
BLOCKS = TILES // BLK
H, HK, HV, TAPS = 4, 64, 128, 4
DK, DV = H * HK, H * HV
QKV = 2 * DK + DV
CHUNKS = SEQ // P
EPS = 1e-5
NORM_EPS = 1e-6
DECAY_FLOOR = -200.0
XH, XD, CTX = 16, 64, 77
XW = XH * XD
NE, FF = 8, 512
FT = (TILES * P * 2) // P + NE - 1

C_ID, C_LE, C_GT, C_GE, C_ONE = 0, P, 2 * P, 3 * P, 4 * P
C_NM0 = 5 * P
C_LEV = 6 * P
LEVELS = 7
C_BLK = C_LEV + (LEVELS - 1) * P // 2
C_LT = C_BLK + 2
C_IOTA = C_LT + P
C_COL = C_IOTA + P
C_LOW = C_COL + 1
C_N = C_LOW + NE * NE


def constants():
    p, j = np.arange(P)[:, None], np.arange(P)[None, :]
    c = np.zeros((P, C_N), np.float32)
    c[:, C_ID:C_ID + P] = p == j
    c[:, C_LE:C_LE + P] = p <= j
    c[:, C_GT:C_GT + P] = p > j
    c[:, C_GE:C_GE + P] = p >= j
    c[:, C_ONE:C_ONE + P] = 1
    c[:, C_NM0:C_NM0 + P] = -1.0 * ((p // 2 == j // 2) & (p % 2 == 1) & (j % 2 == 0))
    for lev in range(1, LEVELS):
        s = 2 ** lev
        m = (p // (2 * s) == j // (2 * s)) & (p % (2 * s) < s) & (j % (2 * s) >= s)
        c[:, C_LEV + (lev - 1) * P // 2:C_LEV + lev * P // 2] = m[:, (np.arange(P) % (2 * s)) >= s]
    c[:, C_BLK:C_BLK + 2] = p // XD == np.arange(2)[None, :]
    c[:, C_LT:C_LT + P] = p < j
    c[:, C_IOTA:C_IOTA + P] = j
    c[:, C_COL:C_COL + 1] = p
    e = np.arange(NE)
    c[:, C_LOW:] = (e[None, :] < e[:, None]).reshape(1, -1)
    return c


@contextmanager
def stage_semaphores(nc):
    taken = []

    def sem(name):
        taken.append(nc.alloc_semaphore(name=name))
        return taken[-1]

    yield sem
    nc.clear_and_free_semaphores(taken)
    nc.all_engine_barrier()


def project_stage(nc, a, s):
    with ExitStack() as ctx:
        sb = lambda n, shape: ctx.enter_context(nc.sbuf_tensor(n, shape, F32))
        bank = lambda n: ctx.enter_context(nc.psum_tensor(n, [P, 512], F32))
        sem = ctx.enter_context(stage_semaphores(nc))

        NCT = QKV // P
        JOBS = NCT + BLK
        x_v = a["x"].rearrange("b (n t p) d -> (b n) p t d", t=BLK, p=P)
        tok_v = s["qkvg"].rearrange("(n t) p c -> n p t c", t=BLK)
        gb_v = s["gb"].rearrange("(n t) p c -> n p t c", t=BLK)

        con = sb("con1", [P, C_N])
        w_qkv = sb("w_qkv", [P, KD, QKV])
        w_gate = sb("w_gate", [P, KD, DV])
        w_ba = sb("w_ba", [P, KD, 2 * H])
        taps = sb("taps", [P, NCT, TAPS])
        ln_wb = sb("ln_wb", [P, 2, KD])
        head_row = sb("head_row", [P, 2, H])
        neg_rate = sb("neg_rate", [P, H])
        eps = sb("eps1", [P, 2])
        zeros = sb("zeros1", [P, NCT, TAPS - 1])
        xin = [sb(f"xin{b}", [P, BLK, D]) for b in range(2)]
        stats = sb("stats1", [P, BLK, 6])
        mv = sb("mv1", [P, BLK, 2])
        rstd = sb("rstd1", [P, BLK])
        xnT = [sb(f"xnT{b}", [P, KD, BT]) for b in range(2)]
        conv_in = sb("conv_in", [P, NCT, TAPS - 1 + BT])
        conv_y = [sb(f"conv_y{b}", [P, BT]) for b in range(2)]
        act_y = [sb(f"act_y{b}", [P, BT]) for b in range(2)]
        tok = [sb(f"tok{b}", [P, BLK, QKV]) for b in range(2)]
        gate = [sb(f"gate{b}", [P, BLK, DV]) for b in range(2)]
        sq = sb("sq1", [P, BLK, 2 * DK])
        ss = sb("ss1", [P, BLK, 2 * H])
        rn = sb("rn1", [P, BLK, 2 * H])
        ba = sb("ba1", [P, BLK, 2 * H])
        sm = sb("sm1", [P, 6, BLK, H])
        gb = [sb(f"gb{b}", [P, BLK, 2 * H]) for b in range(2)]

        ps_x = [bank(f"ps_x{c}") for c in range(KD)]
        ps_j = [bank(f"ps_j{c}") for c in range(2)]
        ps_t = [bank(f"ps_t{c}") for c in range(2)]
        ps_ba = bank("ps_ba")

        weights_in = sem("weights_in")
        x_in = [sem(f"x_in{b}") for b in range(2)]
        consts_set = sem("consts_set")
        rate_exp = sem("rate_exp")
        rate_neg = sem("rate_neg")
        stats_done = sem("stats_done")
        stats_seen = sem("stats_seen")
        var_done = sem("var_done")
        sd_done = sem("sd_done")
        rstd_done = sem("rstd_done")
        xn_done = sem("xn_done")
        xT_done = sem("xT_done")
        xnT_done = sem("xnT_done")
        proj_done = [sem(f"proj_done{b}") for b in range(2)]
        proj_taken = [sem(f"proj_taken{b}") for b in range(2)]
        ba_done = sem("ba_done")
        hist_set = sem("hist_set")
        conv_step = sem("conv_step")
        conv_done = sem("conv_done")
        silu_done = [sem(f"silu_done{b}") for b in range(2)]
        tokT_done = [sem(f"tokT_done{b}") for b in range(2)]
        tok_taken = [sem(f"tok_taken{b}") for b in range(2)]
        sq_done = sem("sq_done")
        ss_done = sem("ss_done")
        norm_sd = sem("norm_sd")
        norm_r = sem("norm_r")
        scaled = sem("scaled")
        beta_scaled = sem("beta_scaled")
        ba_sb = sem("ba_sb")
        z_abs = sem("z_abs")
        exps_done = sem("exps_done")
        soft = sem("soft")
        gb_done = sem("gb_done")
        tok_out = [sem(f"tok_out{b}") for b in range(2)]

        block = ctx.enter_context(nc.Block())

        def view_heads(t, lo, n, d):
            return t[:, :, lo:lo + n * d].rearrange("p t (h d) -> p t h d", d=d)

        @block.sync
        def _(sp):
            sp.dma_start(con[:], a["consts"]).then_inc(weights_in, 16)
            for k, w in enumerate((a["L0_attn_Wq"], a["L0_attn_Wk"], a["L0_attn_Wv"])):
                lo = (0, DK, 2 * DK)[k]
                sp.dma_start(w_qkv[:, :, lo:lo + w.shape[1]],
                             w.rearrange("(k p) n -> p k n", p=P)).then_inc(weights_in, 16)
            sp.dma_start(w_gate[:], a["L0_attn_Wg"].rearrange("(k p) n -> p k n", p=P)).then_inc(weights_in, 16)
            for k, w in enumerate((a["L0_attn_Wb"], a["L0_attn_Wa"])):
                sp.dma_start(w_ba[:, :, k * H:(k + 1) * H],
                             w.rearrange("(k p) n -> p k n", p=P)).then_inc(weights_in, 16)
            for k, w in enumerate((a["L0_attn_conv_q"], a["L0_attn_conv_k"], a["L0_attn_conv_v"])):
                lo, n = (0, DK // P, 2 * DK // P)[k], w.shape[0] // P
                sp.dma_start(taps[:, lo:lo + n, :],
                             w.rearrange("(m p) k -> p m k", p=P)).then_inc(weights_in, 16)
            for k, w in enumerate((a["L0_attn_ln_w"], a["L0_attn_ln_b"])):
                sp.dma_start(ln_wb[:, k, :], w.rearrange("(k p) -> p k", p=P), allow_slow_non_contiguous=True
                             ).then_inc(weights_in, 16)
            for k, w in enumerate((a["L0_attn_A_log"], a["L0_attn_dt_bias"])):
                sp.dma_start(head_row[:, k, :],
                             w.rearrange("(a h) -> a h", a=1).broadcast_to([P, H])).then_inc(weights_in, 16)
            sp.dma_start(xin[0][:], x_v[0]).then_inc(x_in[0], 16)
            with sp.Fori(0, BLOCKS // 2) as i:
                sp.wait_ge(xT_done, i * 2)
                sp.dma_start(xin[1][:], x_v[i * 2 + 1]).then_inc(x_in[1], 16)
                sp.wait_ge(xT_done, i * 2 + 1)
                sp.dma_start(xin[0][:], x_v[(i * 2 + 2) % BLOCKS]).then_inc(x_in[0], 16)
                for b in range(2):
                    n = i * 2 + b
                    sp.wait_ge(beta_scaled, n + 1)
                    sp.wait_ge(scaled, n + 1)
                    sp.wait_ge(tok_taken[0], n * (NCT // 2) + NCT // 2)
                    sp.wait_ge(tok_taken[1], n * (NCT // 2) + NCT // 2)
                    sp.dma_start(tok_v[n][:, :, 0:QKV], tok[b][:]).then_inc(tok_out[b], 16)
                    sp.wait_ge(proj_taken[0], n * (JOBS // 2) + JOBS // 2)
                    sp.wait_ge(proj_taken[1], n * (JOBS // 2) + JOBS // 2)
                    sp.dma_start(tok_v[n][:, :, QKV:QKV + DV], gate[b][:]).then_inc(tok_out[b], 16)
                    sp.wait_ge(gb_done, n * 2 + 2)
                    sp.dma_start(gb_v[n], gb[b][:]).then_inc(tok_out[b], 16)
            for b in range(2):
                sp.wait_ge(tok_out[b], 48 * (BLOCKS // 2))

        @block.gpsimd
        def _(pool):
            nc.gpsimd.memset(eps[:, 0:1], EPS).then_inc(consts_set, 1)
            nc.gpsimd.memset(eps[:, 1:2], NORM_EPS).then_inc(consts_set, 1)
            nc.gpsimd.memset(zeros[:], 0.0).then_inc(consts_set, 1)
            pool.wait_ge(consts_set, 3)
            with pool.Fori(0, BLOCKS // 2) as i:
                for b in range(2):
                    n = i * 2 + b
                    pool.wait_ge(conv_done, n * NCT)
                    if b == 0:
                        nc.gpsimd.tensor_tensor(conv_in[:, :, 0:TAPS - 1], zeros[:], zeros[:], ALU.add).then_inc(hist_set, 1)
                    else:
                        nc.gpsimd.tensor_tensor(conv_in[:, :, 0:TAPS - 1], conv_in[:, :, BT:BT + TAPS - 1], zeros[:],
                                                ALU.add).then_inc(hist_set, 1)
                    pool.wait_ge(tok_taken[0], n * (NCT // 2) + 2 * DK // P // 2)
                    pool.wait_ge(tok_taken[1], n * (NCT // 2) + 2 * DK // P // 2)
                    pool.wait_ge(ss_done, n)
                    nc.gpsimd.tensor_tensor(sq[:], tok[b][:, :, 0:2 * DK], tok[b][:, :, 0:2 * DK],
                                            ALU.mult).then_inc(sq_done, 1)
                    pool.wait_ge(norm_r, n * 2 + 2)
                    v = view_heads(tok[b], 0, 2 * H, HK)
                    nc.gpsimd.tensor_tensor(v, v, rn[:].unsqueeze(3).broadcast_to([P, BLK, 2 * H, HK]),
                                            ALU.mult).then_inc(scaled, 1)
                    pool.wait_ge(gb_done, n * 2 + 1)
                    pool.wait_ge(tok_taken[0], n * (NCT // 2) + NCT // 2)
                    pool.wait_ge(tok_taken[1], n * (NCT // 2) + NCT // 2)
                    v = view_heads(tok[b], 2 * DK, H, HV)
                    nc.gpsimd.tensor_tensor(v, v, gb[b][:, :, H:2 * H].unsqueeze(3).broadcast_to([P, BLK, H, HV]),
                                            ALU.mult).then_inc(beta_scaled, 1)

        @block.tensor
        def _(pe):
            pe.wait_ge(weights_in, 16 * 14)
            with pe.Fori(0, BLOCKS // 2) as i:
                for b in range(2):
                    n = i * 2 + b
                    pe.wait_ge(xn_done, n + 1)
                    pe.wait_ge(xnT_done, n * KD)
                    for c in range(KD):
                        for t in range(BLK):
                            mm = pe.transpose(ps_x[c][:, t * P:(t + 1) * P], xin[b][:, t, c * P:(c + 1) * P],
                                              con[:, C_ID:C_ID + P])
                    mm.then_inc(xT_done, 1)
                    pe.wait_ge(xnT_done, n * KD + KD)
                    pe.wait_ge(ba_sb, n)
                    for t in range(BLK):
                        for c in range(KD):
                            mm = pe.matmul(ps_ba[:, t * 2 * H:(t + 1) * 2 * H], xnT[b][:, c, t * P:(t + 1) * P],
                                           w_ba[:, c, :], start=c == 0, stop=c == KD - 1)
                    mm.then_inc(ba_done, 1)

                    def to_tokens(m):
                        pe.wait_ge(silu_done[m % 2], n * (NCT // 2) + m // 2 + 1)
                        pe.wait_ge(tok_taken[m % 2], n * (NCT // 2) + m // 2)
                        for t in range(BLK):
                            mm = pe.transpose(ps_t[m % 2][:, t * P:(t + 1) * P],
                                              act_y[m % 2][:, t * P:(t + 1) * P], con[:, C_ID:C_ID + P])
                        mm.then_inc(tokT_done[m % 2], 1)

                    for j in range(JOBS):
                        pe.wait_ge(proj_taken[j % 2], n * (JOBS // 2) + j // 2)
                        for c in range(KD):
                            if j < NCT:
                                mm = pe.matmul(ps_j[j % 2][:], w_qkv[:, c, j * P:(j + 1) * P], xnT[b][:, c, :],
                                               start=c == 0, stop=c == KD - 1)
                            else:
                                t = j - NCT
                                mm = pe.matmul(ps_j[j % 2][:], xnT[b][:, c, t * P:(t + 1) * P], w_gate[:, c, :],
                                               start=c == 0, stop=c == KD - 1)
                        mm.then_inc(proj_done[j % 2], 1)
                        if 2 <= j < NCT + 2:
                            to_tokens(j - 2)

        @block.scalar
        def _(act):
            act.wait_ge(weights_in, 16 * 14)
            act.wait_ge(consts_set, 3)
            nc.scalar.activation(neg_rate[:], head_row[:, 0, :], ACT.Exp).then_inc(rate_exp, 1)

            def block_sd(n):
                act.wait_ge(var_done, n + 1)
                act.wait_ge(xn_done, n)
                nc.scalar.activation(rstd[:], mv[:, :, 1], ACT.Sqrt, bias=eps[:, 0:1]).then_inc(sd_done, 1)

            block_sd(0)
            with act.Fori(0, BLOCKS // 2) as i:
                for b in range(2):
                    n = i * 2 + b
                    act.wait_ge(xT_done, n + 1)
                    for c in range(KD):
                        nc.scalar.activation(xnT[b][:, c, :], ps_x[c][:], ACT.Identity,
                                             bias=ln_wb[:, 1, c:c + 1],
                                             scale=ln_wb[:, 0, c:c + 1]).then_inc(xnT_done, 1)
                    act.wait_ge(hist_set, n + 1)

                    def silu(m):
                        act.wait_ge(conv_done, n * NCT + m + 1)
                        act.wait_ge(tokT_done[m % 2], n * (NCT // 2) + m // 2)
                        nc.scalar.activation(act_y[m % 2][:], conv_y[m % 2][:], ACT.Silu
                                             ).then_inc(silu_done[m % 2], 1)

                    def take_tokens(m):
                        act.wait_ge(tokT_done[m % 2], n * (NCT // 2) + m // 2 + 1)
                        if m == 0:
                            act.wait_ge(tok_out[b], i * 48)
                        nc.scalar.activation(tok[b][:, :, m * P:(m + 1) * P],
                                             ps_t[m % 2][:].rearrange("p (t c) -> p t c", t=BLK),
                                             ACT.Copy).then_inc(tok_taken[m % 2], 1)

                    for j in range(JOBS):
                        act.wait_ge(proj_done[j % 2], n * (JOBS // 2) + j // 2 + 1)
                        if j < NCT:
                            nc.scalar.activation(conv_in[:, j, TAPS - 1:TAPS - 1 + BT], ps_j[j % 2][:],
                                                 ACT.Copy).then_inc(proj_taken[j % 2], 1)
                        else:
                            nc.scalar.activation(gate[b][:, j - NCT, :], ps_j[j % 2][:], ACT.Silu
                                                 ).then_inc(proj_taken[j % 2], 1)
                        if 1 <= j < NCT + 1:
                            silu(j - 1)
                        if 3 <= j < NCT + 3:
                            take_tokens(j - 3)
                    block_sd(n + 1)
                    act.wait_ge(ss_done, n + 1)
                    nc.scalar.activation(rn[:], ss[:], ACT.Sqrt, bias=eps[:, 1:2]).then_inc(norm_sd, 1)
                    act.wait_ge(z_abs, n + 1)
                    nc.scalar.activation(sm[:, 0], ba[:, :, 0:H], ACT.Exp, scale=-1.0).then_inc(exps_done, 1)
                    nc.scalar.activation(sm[:, 2], sm[:, 1], ACT.Exp, scale=-1.0).then_inc(exps_done, 1)

        @block.vector
        def _(dve):
            dve.wait_ge(rate_exp, 1)
            nc.vector.tensor_scalar(neg_rate[:], neg_rate[:], -1.0, None, ALU.mult).then_inc(rate_neg, 1)
            dve.wait_ge(rate_neg, 1)

            def layer_norm(n, b, k):
                dve.wait_ge(x_in[b], k * 16 + 16)
                for t in range(BLK):
                    nc.vector.bn_stats(stats[:, t, :], xin[b][:, t, :]).then_inc(stats_done, 1)
                dve.wait_ge(stats_done, n * BLK + BLK)
                dve.wait_ge(sd_done, n)
                nc.vector.sem_inc(stats_seen, 1)
                for t in range(BLK):
                    ag = nc.vector.bn_aggr(mv[:, t, :], stats[:, t, :])
                ag.then_inc(var_done, 1)
                dve.wait_ge(sd_done, n + 1)
                nc.vector.reciprocal(rstd[:], rstd[:]).then_inc(rstd_done, 1)
                dve.wait_ge(rstd_done, n + 1)
                for t in range(BLK):
                    xn = nc.vector.tensor_scalar(xin[b][:, t, :], xin[b][:, t, :], mv[:, t, 0:1],
                                                 rstd[:, t:t + 1], ALU.subtract, ALU.mult)
                xn.then_inc(xn_done, 1)

            layer_norm(0, 0, 0)
            with dve.Fori(0, BLOCKS // 2) as i:
                for b in range(2):
                    n = i * 2 + b
                    dve.wait_ge(ba_done, n + 1)
                    nc.vector.tensor_copy(ba[:], ps_ba[:, 0:BLK * 2 * H].rearrange("p (t h) -> p t h", t=BLK)
                                          ).then_inc(ba_sb, 1)
                    dve.wait_ge(ba_sb, n + 1)
                    nc.vector.tensor_tensor(sm[:, 3], ba[:, :, H:2 * H],
                                            head_row[:, 1:2, :].broadcast_to([P, BLK, H]), ALU.add
                                            ).then_inc(soft, 1)
                    dve.wait_ge(soft, n * 16 + 1)
                    nc.vector.scalar_tensor_tensor(sm[:, 1], sm[:, 3], -1.0, sm[:, 3], ALU.mult, ALU.max
                                                   ).then_inc(z_abs, 1)
                    for m in range(NCT):
                        dve.wait_ge(proj_taken[m % 2], n * (JOBS // 2) + m // 2 + 1)
                        dve.wait_ge(silu_done[m % 2], n * (NCT // 2) + m // 2)
                        nc.vector.tensor_scalar(conv_y[m % 2][:], conv_in[:, m, 0:BT], taps[:, m, 0:1], None,
                                                ALU.mult).then_inc(conv_step, 1)
                        for k in range(1, TAPS):
                            dve.wait_ge(conv_step, (n * NCT + m) * (TAPS - 1) + k)
                            y = nc.vector.scalar_tensor_tensor(conv_y[m % 2][:], conv_in[:, m, k:k + BT],
                                                               taps[:, m, k:k + 1], conv_y[m % 2][:],
                                                               ALU.mult, ALU.add)
                            y.then_inc(conv_step if k < TAPS - 1 else conv_done, 1)
                        if m == 5:
                            dve.wait_ge(sq_done, n + 1)
                            dve.wait_ge(scaled, n)
                            nc.vector.tensor_reduce(ss[:], sq[:].rearrange("p t (h d) -> p t h d", d=HK), AX_X,
                                                    ALU.add).then_inc(ss_done, 1)
                    layer_norm(n + 1, 1 - b, i + b)
                    dve.wait_ge(norm_sd, n + 1)
                    nc.vector.reciprocal(rn[:], rn[:]).then_inc(norm_r, 1)
                    dve.wait_ge(norm_r, n * 2 + 1)
                    nc.vector.tensor_scalar(rn[:, :, 0:H], rn[:, :, 0:H], HK ** -0.5, None, ALU.mult
                                            ).then_inc(norm_r, 1)
                    step = [1]

                    def link(ins):
                        step[0] += 1
                        ins.then_inc(soft, 1)
                        dve.wait_ge(soft, n * 16 + step[0])

                    dve.wait_ge(exps_done, n * 2 + 2)
                    dve.wait_ge(tok_out[b], i * 48)
                    link(nc.vector.tensor_scalar(sm[:, 0], sm[:, 0], 1.0, None, ALU.add))
                    nc.vector.reciprocal(gb[b][:, :, H:2 * H], sm[:, 0]).then_inc(gb_done, 1)
                    link(nc.vector.tensor_scalar(sm[:, 4], sm[:, 2], 2.0, None, ALU.add))
                    link(nc.vector.reciprocal(sm[:, 4], sm[:, 4]))
                    link(nc.vector.tensor_tensor(sm[:, 4], sm[:, 4], sm[:, 2], ALU.mult))
                    link(nc.vector.tensor_tensor(sm[:, 5], sm[:, 4], sm[:, 4], ALU.mult))
                    link(nc.vector.tensor_scalar(sm[:, 2], sm[:, 5], 2.0 / 15, None, ALU.mult))
                    for k in (13, 11, 9, 7, 5, 3):
                        link(nc.vector.scalar_tensor_tensor(sm[:, 2], sm[:, 2], 2.0 / k, sm[:, 5], ALU.add,
                                                            ALU.mult))
                    link(nc.vector.scalar_tensor_tensor(sm[:, 2], sm[:, 2], 2.0, sm[:, 4], ALU.add, ALU.mult))
                    link(nc.vector.scalar_tensor_tensor(sm[:, 2], sm[:, 3], 0.0, sm[:, 2], ALU.max, ALU.add))
                    link(nc.vector.tensor_tensor(sm[:, 2], sm[:, 2],
                                                 neg_rate[:].unsqueeze(1).broadcast_to([P, BLK, H]), ALU.mult))
                    nc.vector.tensor_scalar(gb[b][:, :, 0:H], sm[:, 2], DECAY_FLOOR, None, ALU.max
                                            ).then_inc(gb_done, 1)
                    assert step[0] == 16


def delta_stage(nc, a, s):
    with ExitStack() as ctx:
        sb = lambda n, shape: ctx.enter_context(nc.sbuf_tensor(n, shape, F32))
        bank = lambda n: ctx.enter_context(nc.psum_tensor(n, [P, 512], F32))
        sem = ctx.enter_context(stage_semaphores(nc))
        G = range(BATCH)
        per = lambda n, shape: [sb(f"{n}{b}", shape) for b in G]

        con = sb("con2", [P, C_N])
        w_o = sb("w_o", [P, H, D])
        norm_w = sb("norm_w", [P, 1])
        eps = sb("eps2", [P, 1])
        qk = per("qk", [P, 2 * DK])
        vb = per("vb", [P, DV])
        gt = per("gt", [P, DV])
        gbt = per("gbt", [P, 2 * H])
        xr = per("xr", [P, D])
        gam = per("gam", [P, 3 * H])
        gC2 = per("gC2", [P, 2])
        nbg = per("nbg", [P, H])
        g_gt = per("g_gt", [P, H, P])
        E = per("E", [P, H, P])
        Em = per("Em", [P, H, P])
        Eb = per("Eb", [P, H, P])
        qg = per("qg", [P, DK])
        ke = per("ke", [P, DK])
        qkT = per("qkT", [P, 4, P])
        qgT = per("qgT", [P, 2, P])
        PT = per("PT", [P, H, P])
        Y = per("Y", [P, H, P])
        bb = per("bb", [P, H, P])
        u = per("u", [P, H, P])
        S = per("S", [P, 2, HV])
        ssum = per("ssum", [P, H])
        stats = per("stats2_", [P, 6])
        mv = per("mv2_", [P, 2])
        rstd = per("rstd2_", [P, 1])
        x1t = per("x1t", [P, D])
        X, Qs, Pm, Am, og, ogT = g_gt, E, Em, Eb, bb, u

        A = [bank(f"psA{b}") for b in G]
        B = [bank(f"psB{b}") for b in G]

        weights_in = sem("weights_in2")
        qk_in = [sem(f"qk_in{b}") for b in G]
        v_in = [sem(f"v_in{b}") for b in G]
        gx_in = [sem(f"gx_in{b}") for b in G]
        x1_out = [sem(f"x1_out{b}") for b in G]
        names = ("set_up g_gt_done cum_done gam_done D_done E_done Em_done Eb_done nbg_done qg_done ke_done "
                 "qkT_done qkT_sb qgT_done qgT_sb kkqk_done am_done pm_done x0_half x0_done pT_done pT_sb y0_done "
                 "y0_sb lev_q lev_qs lev_y lev_ys lev_x lev_xs ks_done bb_done u_done u_sb o_done s_done "
                 "sq_done rs_sd rs_done og_done ogT_done ogT_sb wo_done y_done st_done st_seen mv_done sd_done "
                 "r_done x1_done").split()
        (set_up, g_gt_done, cum_done, gam_done, D_done, E_done, Em_done, Eb_done, nbg_done, qg_done, ke_done,
         qkT_done, qkT_sb, qgT_done, qgT_sb, kkqk_done, am_done, pm_done, x0_half, x0_done, pT_done, pT_sb, y0_done,
         y0_sb, lev_q, lev_qs, lev_y, lev_ys, lev_x, lev_xs, ks_done, bb_done, u_done, u_sb, o_done, s_done,
         sq_done, rs_sd, rs_done, og_done, ogT_done, ogT_sb, wo_done, y_done, st_done, st_seen, mv_done, sd_done,
         r_done, x1_done) = [sem(f"d_{n}") for n in names]

        block = ctx.enter_context(nc.Block())
        MERGES = range(1, LEVELS)
        NL = LEVELS - 1
        head = lambda slot: 2 * (slot % 2) + slot // 2
        ident = con[:, C_ID:C_ID + P]
        rows = lambda slot: slice(HK * (slot // 2), HK * (slot // 2) + HK)
        by_slot = lambda t: t.rearrange("p (t r) -> p r t", r=2)
        mask4 = lambda lo: con[:, lo:lo + P].unsqueeze(1).broadcast_to([P, H, P])
        HP = P // 2
        right = lambda t, lev: t[:].rearrange("p k (m w j) -> p k m w j", w=2, j=2 ** lev)[:, :, :, 1, :]
        split = lambda t: t[:].rearrange("p (r t) j -> p r t j", r=2)

        @block.sync
        def _(sp):
            sp.dma_start(con[:], a["consts"]).then_inc(weights_in, 16)
            sp.dma_start(w_o[:], a["L0_attn_Wo"].rearrange("(h p) n -> p h n", p=P)).then_inc(weights_in, 16)
            sp.dma_start(norm_w[:], a["L0_attn_norm_w"].rearrange("(p a) -> p a", a=1)).then_inc(weights_in, 16)
            with sp.Fori(0, CHUNKS) as c:
                sp.wait_ge(Eb_done, c * BATCH)
                sp.wait_ge(ke_done, c * BATCH)
                sp.wait_ge(nbg_done, c * BATCH)
                sp.wait_ge(qkT_done, c * BATCH)
                for b in G:
                    sp.dma_start(gbt[b][:], s["gb"][c + b * CHUNKS]).then_inc(qk_in[b], 16)
                    sp.dma_start(qk[b][:], s["qkvg"][c + b * CHUNKS, :, 0:2 * DK]).then_inc(qk_in[b], 16)
                sp.wait_ge(bb_done, c * BATCH)
                for b in G:
                    sp.dma_start(vb[b][:], s["qkvg"][c + b * CHUNKS, :, 2 * DK:QKV]).then_inc(v_in[b], 16)
                sp.wait_ge(og_done, c * BATCH)
                sp.wait_ge(y_done, c * BATCH)
                for b in G:
                    sp.dma_start(gt[b][:], s["qkvg"][c + b * CHUNKS, :, QKV:QKV + DV]).then_inc(gx_in[b], 16)
                    sp.dma_start(xr[b][:], a["x"].rearrange("b (c p) d -> b c p d", p=P)[b, c]).then_inc(gx_in[b], 16)

        @block.gpsimd
        def _(pool):
            nc.gpsimd.memset(eps[:], EPS).then_inc(set_up, 1)
            for b in G:
                nc.gpsimd.memset(S[b][:], 0.0).then_inc(set_up, 1)
            pool.wait_ge(weights_in, 48)
            with pool.Fori(0, CHUNKS) as c:
                for b in G:
                    pool.wait_ge(qk_in[b], c * 32 + 32)
                    pool.wait_ge(lev_y, c * NL * BATCH)
                    nc.gpsimd.tensor_tensor(split(g_gt[b]),
                                            by_slot(gbt[b][:, 0:H]).unsqueeze(3).broadcast_to([P, 2, 2, P]),
                                            con[:, C_GT:C_GT + P].unsqueeze(1).unsqueeze(1).broadcast_to([P, 2, 2, P]), ALU.mult).then_inc(g_gt_done, 1)
                for b in G:
                    pool.wait_ge(gam_done, c * BATCH + b + 1)
                    pool.wait_ge(qgT_done, c * BATCH)
                    nc.gpsimd.tensor_tensor(qg[b][:].rearrange("p (h d) -> p h d", d=HK),
                                            qk[b][:, 0:DK].rearrange("p (h d) -> p h d", d=HK),
                                            gam[b][:, 0:H].unsqueeze(2).broadcast_to([P, H, HK]),
                                            ALU.mult).then_inc(qg_done, 1)
                for b in G:
                    pool.wait_ge(E_done, c * BATCH + b + 1)
                    pool.wait_ge(lev_q, c * NL * BATCH)
                    nc.gpsimd.tensor_tensor(split(Eb[b]), split(E[b]),
                                            by_slot(gbt[b][:, H:2 * H]).unsqueeze(3).broadcast_to([P, 2, 2, P]),
                                            ALU.mult).then_inc(Eb_done, 1)
                    pool.wait_ge(pT_done, c * BATCH)
                    nc.gpsimd.tensor_tensor(Em[b][:], E[b][:], mask4(C_GE), ALU.mult).then_inc(Em_done, 1)
                for b in G:
                    pool.wait_ge(am_done, c * BATCH + b + 1)
                    nc.gpsimd.tensor_tensor(X[b][:], Am[b][:], mask4(C_NM0), ALU.mult).then_inc(x0_half, 1)
                    pool.wait_ge(x0_half, c * BATCH + b + 1)
                    nc.gpsimd.tensor_tensor(X[b][:], X[b][:], mask4(C_ID), ALU.add).then_inc(x0_done, 1)
                for b in G:
                    pool.wait_ge(o_done, c * BATCH)
                    nc.gpsimd.tensor_tensor(ke[b][:].rearrange("p (h d) -> p h d", d=HK),
                                            qk[b][:, DK:2 * DK].rearrange("p (h d) -> p h d", d=HK),
                                            gam[b][:, H:2 * H].unsqueeze(2).broadcast_to([P, H, HK]),
                                            ALU.mult).then_inc(ke_done, 1)
                for b in G:
                    pool.wait_ge(x1_done, c * BATCH + b + 1)
                    pool.dma_start(s["x1"][c + b * CHUNKS], x1t[b][:]).then_inc(x1_out[b], 16)
            for b in G:
                pool.wait_ge(x1_out[b], 16 * CHUNKS)

        @block.tensor
        def _(pe):
            pe.wait_ge(weights_in, 48)
            pe.wait_ge(set_up, 1 + BATCH)
            with pe.Fori(0, CHUNKS) as c:
                at = lambda b: c * BATCH + b + 1
                for b in G:
                    pe.wait_ge(g_gt_done, at(b))
                    pe.wait_ge(ogT_sb, c * BATCH)
                    pe.wait_ge(y_done, c * BATCH)
                    for k, lo in enumerate((C_LE, C_GT, C_ONE)):
                        mm = pe.matmul(A[b][:, k * H:(k + 1) * H], con[:, lo:lo + P], gbt[b][:, 0:H],
                                       start=True, stop=True)
                    mm.then_inc(cum_done, 1)
                    pe.matmul(B[b][:], con[:, C_LE:C_LE + P], g_gt[b][:], start=True, stop=True).then_inc(D_done, 1)
                for b in G:
                    pe.wait_ge(gam_done, at(b))
                    for k in range(4):
                        mm = pe.transpose(A[b][:, k * P:(k + 1) * P], qk[b][:, k * P:(k + 1) * P], ident)
                    mm.then_inc(qkT_done, 1)
                for b in G:
                    pe.wait_ge(E_done, at(b))
                    pe.wait_ge(qg_done, at(b))
                    for k in range(2):
                        mm = pe.transpose(B[b][:, k * P:(k + 1) * P], qg[b][:, k * P:(k + 1) * P], ident)
                    mm.then_inc(qgT_done, 1)
                for b in G:
                    pe.wait_ge(qkT_sb, at(b))
                    pe.wait_ge(qgT_sb, at(b))
                    for w in (2, 0):
                        for t in range(2):
                            for r, bk in enumerate((A[b], B[b])):
                                lo = (t if w else 2 + t) * P
                                mm = pe.matmul(bk[:, lo:lo + P], qkT[b][rows(2 * r), w + t, :],
                                               qkT[b][rows(2 * r), 2 + t, :], start=True, stop=True)
                    mm.then_inc(kkqk_done, 1)
                for b in G:
                    pe.wait_ge(pm_done, at(b))
                    for k in range(H):
                        mm = pe.transpose(B[b][:, k * P:(k + 1) * P], Pm[b][:, k, :], ident)
                    mm.then_inc(pT_done, 1)
                for b in G:
                    pe.wait_ge(x0_done, at(b))
                    for k in range(H):
                        mm = pe.transpose(A[b][:, k * P:(k + 1) * P], X[b][:, k, :], ident)
                    mm.then_inc(y0_done, 1)
                for lev in MERGES:
                    lat = lambda b, lev=lev: (c * NL + (lev - 1)) * BATCH + b + 1
                    for b in G:
                        if lev == 1:
                            pe.wait_ge(y0_sb, at(b))
                        else:
                            pe.wait_ge(lev_ys, lat(b) - BATCH)
                            pe.wait_ge(lev_xs, (c * (NL - 1) + (lev - 2)) * BATCH + b + 1)
                        for k in range(H):
                            mm = pe.matmul(A[b][:, k * HP:(k + 1) * HP], Am[b][:, k, :], right(Y[b], lev)[:, k],
                                           start=True, stop=True)
                        mm.then_inc(lev_q, 1)
                    for b in G:
                        pe.wait_ge(lev_qs, lat(b))
                        if lev == 1:
                            pe.wait_ge(pT_sb, at(b))
                        for k in range(H):
                            mm = pe.matmul(B[b][:, k * HP:(k + 1) * HP], X[b][:, k, :], Qs[b][:, k, 0:HP],
                                           start=True, stop=True)
                        mm.then_inc(lev_y, 1)
                    if lev < NL:
                        for b in G:
                            pe.wait_ge(lev_ys, lat(b))
                            for k in range(H):
                                mm = pe.transpose(A[b][:, k * P:(k + 1) * P], Y[b][:, k, :], ident)
                            mm.then_inc(lev_x, 1)
                for b in G:
                    pe.wait_ge(lev_ys, (c + 1) * NL * BATCH - BATCH + b + 1)
                    pe.wait_ge(s_done, c * BATCH)
                    for t in range(2):
                        for r, bk in enumerate((A[b], B[b])):
                            mm = pe.matmul(bk[:, t * P:(t + 1) * P], qkT[b][rows(2 * r), 2 + t, :],
                                           S[b][rows(2 * r), t, :], start=True, stop=True)
                    mm.then_inc(ks_done, 1)
                for b in G:
                    pe.wait_ge(bb_done, at(b))
                    for k in range(H):
                        mm = pe.matmul(A[b][:, k * P:(k + 1) * P], Y[b][:, k, :], bb[b][:, k, :],
                                       start=True, stop=True)
                    mm.then_inc(u_done, 1)
                for b in G:
                    pe.wait_ge(u_sb, at(b))
                    pe.wait_ge(ke_done, at(b))
                    for t in range(2):
                        for r, bk in enumerate((A[b], B[b])):
                            pe.matmul(bk[:, t * P:(t + 1) * P], qgT[b][rows(2 * r), t, :],
                                      S[b][rows(2 * r), t, :], start=True, stop=False)
                            pe.matmul(bk[:, t * P:(t + 1) * P], PT[b][:, 2 * r + t, :], u[b][:, 2 * r + t, :],
                                      start=False, stop=True)
                    for t in range(2):
                        for r in range(2):
                            h = 2 * t + r
                            mm = pe.matmul(B[b][rows(2 * r), 2 * P + t * P:2 * P + (t + 1) * P],
                                           ke[b][:, h * HK:(h + 1) * HK], u[b][:, 2 * r + t, :],
                                           start=True, stop=True)
                    mm.then_inc(o_done, 1)
                for b in G:
                    pe.wait_ge(og_done, at(b))
                    for k in range(H):
                        mm = pe.transpose(A[b][:, k * P:(k + 1) * P], og[b][:, k, :], ident)
                    mm.then_inc(ogT_done, 1)
                for b in G:
                    pe.wait_ge(ogT_sb, at(b))
                    for k in range(H):
                        mm = pe.matmul(B[b][:, 0:D], ogT[b][:, k, :], w_o[:, head(k), :],
                                       start=k == 0, stop=k == H - 1)
                    mm.then_inc(wo_done, 1)

        @block.scalar
        def _(act):
            act.wait_ge(weights_in, 48)
            act.wait_ge(set_up, 1 + BATCH)
            with act.Fori(0, CHUNKS) as c:
                at = lambda b: c * BATCH + b + 1
                flat = lambda t: t[:].rearrange("p k j -> p (k j)")
                for b in G:
                    act.wait_ge(cum_done, at(b))
                    act.wait_ge(ke_done, c * BATCH)
                    act.wait_ge(s_done, c * BATCH)
                    nc.scalar.activation(gam[b][:], A[b][:, 0:3 * H], ACT.Exp)
                    tot = A[b][:, 2 * H:3 * H].rearrange("p (t r) -> p r t", r=2)
                    for r in range(2):
                        e = nc.scalar.activation(gC2[b][rows(2 * r), :], tot[rows(2 * r), r, :], ACT.Exp)
                    e.then_inc(gam_done, 1)
                for b in G:
                    act.wait_ge(D_done, at(b))
                    nc.scalar.activation(flat(E[b]), B[b][:], ACT.Exp).then_inc(E_done, 1)
                for b in G:
                    act.wait_ge(qkT_done, at(b))
                    nc.scalar.activation(flat(qkT[b]), A[b][:], ACT.Copy).then_inc(qkT_sb, 1)
                for b in G:
                    act.wait_ge(qgT_done, at(b))
                    nc.scalar.activation(flat(qgT[b]), B[b][:, 0:2 * P], ACT.Copy).then_inc(qgT_sb, 1)
                for b in G:
                    act.wait_ge(pT_done, at(b))
                    nc.scalar.activation(flat(PT[b]), B[b][:], ACT.Copy).then_inc(pT_sb, 1)
                for b in G:
                    act.wait_ge(y0_done, at(b))
                    nc.scalar.activation(flat(Y[b]), A[b][:], ACT.Copy).then_inc(y0_sb, 1)
                for lev in range(1, NL):
                    for b in G:
                        act.wait_ge(lev_x, (c * (NL - 1) + (lev - 1)) * BATCH + b + 1)
                        nc.scalar.activation(flat(X[b]), A[b][:], ACT.Copy).then_inc(lev_xs, 1)
                for b in G:
                    act.wait_ge(u_done, at(b))
                    nc.scalar.activation(flat(u[b]), A[b][:], ACT.Copy).then_inc(u_sb, 1)
                for b in G:
                    act.wait_ge(o_done, at(b))
                    act.wait_ge(s_done, at(b))
                    for k in range(H):
                        bk = (A, B)[k // 2][b]
                        q = nc.scalar.activation(og[b][:, k, :], bk[:, (k % 2) * P:(k % 2 + 1) * P], ACT.Square,
                                                 accum_out=ssum[b][:, k:k + 1])
                    q.then_inc(sq_done, 1)
                for b in G:
                    act.wait_ge(sq_done, at(b))
                    nc.scalar.activation(ssum[b][:], ssum[b][:], ACT.Sqrt, bias=eps[:, 0:1], scale=1.0 / HV
                                         ).then_inc(rs_sd, 1)
                for b in G:
                    act.wait_ge(ogT_done, at(b))
                    nc.scalar.activation(flat(ogT[b]), A[b][:], ACT.Copy, scale=norm_w[:, 0:1]).then_inc(ogT_sb, 1)
                for b in G:
                    act.wait_ge(mv_done, at(b))
                    nc.scalar.activation(rstd[b][:], mv[b][:, 1:2], ACT.Sqrt, bias=eps[:, 0:1]).then_inc(sd_done, 1)

        @block.vector
        def _(dve):
            dve.wait_ge(weights_in, 48)
            with dve.Fori(0, CHUNKS) as c:
                at = lambda b: c * BATCH + b + 1
                for b in G:
                    dve.wait_ge(gam_done, at(b))
                    nc.vector.scalar_tensor_tensor(nbg[b][:], gam[b][:, 0:H], -1.0, gbt[b][:, H:2 * H],
                                                   ALU.mult, ALU.mult).then_inc(nbg_done, 1)
                for b in G:
                    dve.wait_ge(kkqk_done, at(b))
                    dve.wait_ge(Eb_done, at(b))
                    for r, bk in enumerate((A[b], B[b])):
                        m = nc.vector.tensor_tensor(Am[b][:, 2 * r:2 * r + 2, :],
                                                    bk[:, 0:2 * P].rearrange("p (t j) -> p t j", t=2),
                                                    Eb[b][:, 2 * r:2 * r + 2, :], ALU.mult)
                    m.then_inc(am_done, 1)
                    dve.wait_ge(Em_done, at(b))
                    for r, bk in enumerate((A[b], B[b])):
                        m = nc.vector.tensor_tensor(Pm[b][:, 2 * r:2 * r + 2, :],
                                                    bk[:, 2 * P:4 * P].rearrange("p (t j) -> p t j", t=2),
                                                    Em[b][:, 2 * r:2 * r + 2, :], ALU.mult)
                    m.then_inc(pm_done, 1)
                for lev in MERGES:
                    lat = lambda b, lev=lev: (c * NL + (lev - 1)) * BATCH + b + 1
                    for b in G:
                        dve.wait_ge(lev_q, lat(b))
                        m = C_LEV + (lev - 1) * HP
                        nc.vector.tensor_tensor(Qs[b][:, :, 0:HP],
                                                A[b][:, 0:H * HP].rearrange("p (k j) -> p k j", k=H),
                                                con[:, m:m + HP].unsqueeze(1).broadcast_to([P, H, HP]), ALU.mult
                                                ).then_inc(lev_qs, 1)
                    for b in G:
                        dve.wait_ge(lev_y, lat(b))
                        y = right(Y[b], lev)
                        nc.vector.tensor_tensor(y, y, B[b][:, 0:H * HP].rearrange("p (k m j) -> p k m j", k=H,
                                                                                 j=2 ** lev),
                                                ALU.subtract).then_inc(lev_ys, 1)
                for b in G:
                    dve.wait_ge(ks_done, at(b))
                    dve.wait_ge(v_in[b], c * 16 + 16)
                    dve.wait_ge(ogT_done, c * BATCH)
                    dve.wait_ge(nbg_done, at(b))
                    for k in range(H):
                        bk, h = (A, B)[k // 2][b], head(k)
                        m = nc.vector.scalar_tensor_tensor(bb[b][:, k, :], bk[:, (k % 2) * P:(k % 2 + 1) * P],
                                                           nbg[b][:, h:h + 1], vb[b][:, h * HV:(h + 1) * HV],
                                                           ALU.mult, ALU.add)
                    m.then_inc(bb_done, 1)
                for b in G:
                    dve.wait_ge(o_done, at(b))
                    for t in range(2):
                        m = nc.vector.scalar_tensor_tensor(S[b][:, t, :], S[b][:, t, :], gC2[b][:, t:t + 1],
                                                           B[b][:, 2 * P + t * P:2 * P + (t + 1) * P],
                                                           ALU.mult, ALU.add)
                    m.then_inc(s_done, 1)
                for b in G:
                    dve.wait_ge(rs_sd, at(b))
                    nc.vector.reciprocal(ssum[b][:], ssum[b][:]).then_inc(rs_done, 1)
                for b in G:
                    dve.wait_ge(rs_done, at(b))
                    dve.wait_ge(gx_in[b], c * 32 + 32)
                    for k in range(H):
                        bk, h = (A, B)[k // 2][b], head(k)
                        m = nc.vector.scalar_tensor_tensor(og[b][:, k, :], bk[:, (k % 2) * P:(k % 2 + 1) * P],
                                                           ssum[b][:, k:k + 1], gt[b][:, h * HV:(h + 1) * HV],
                                                           ALU.mult, ALU.mult)
                    m.then_inc(og_done, 1)
                for b in G:
                    dve.wait_ge(wo_done, at(b))
                    dve.wait_ge(x1_out[b], c * 16)
                    nc.vector.scalar_tensor_tensor(x1t[b][:], xr[b][:], 2.0, B[b][:, 0:D], ALU.mult, ALU.add
                                                   ).then_inc(y_done, 1)
                for b in G:
                    dve.wait_ge(y_done, at(b))
                    nc.vector.bn_stats(stats[b][:], x1t[b][:]).then_inc(st_done, 1)
                for b in G:
                    dve.wait_ge(st_done, at(b))
                    nc.vector.sem_inc(st_seen, 1)
                    nc.vector.bn_aggr(mv[b][:], stats[b][:]).then_inc(mv_done, 1)
                for b in G:
                    dve.wait_ge(sd_done, at(b))
                    nc.vector.reciprocal(rstd[b][:], rstd[b][:]).then_inc(r_done, 1)
                for b in G:
                    dve.wait_ge(r_done, at(b))
                    nc.vector.tensor_scalar(x1t[b][:], x1t[b][:], mv[b][:, 0:1], rstd[b][:, 0:1],
                                            ALU.subtract, ALU.mult).then_inc(x1_done, 1)


def context_stage(nc, a, s):
    with ExitStack() as ctx:
        sb = lambda n, shape: ctx.enter_context(nc.sbuf_tensor(n, shape, F32))
        bank = lambda n: ctx.enter_context(nc.psum_tensor(n, [P, 512], F32))
        sem = ctx.enter_context(stage_semaphores(nc))
        XJ = XW // P
        con = sb("con3", [P, C_N])
        w_k = sb("xw_k", [P, KD, XW])
        w_v = sb("xw_v", [P, KD, XW])
        nw = sb("xnw", [P, 2])
        eps = sb("eps3", [P, 1])
        cx = sb("cx", [P, D])
        cxT = sb("cxT", [P, KD, CTX])
        k_sb = sb("k_sb", [P, XW])
        k_sq = sb("k_sq", [P, XW])
        v_sb = sb("v_sb", [P, XW])
        ss = sb("ss3", [P, XH])
        kT = sb("kT3", [P, XJ, CTX])
        ctx_len = ctx.enter_context(nc.sbuf_tensor("ctx_len", [P, 1], I32))
        len_f = sb("len_f", [P, 1])
        valid = sb("valid", [P, 1])
        madd = sb("madd3", [P, CTX])
        ps_c = bank("ps_c")
        ps_k = [bank(f"ps_k{h}") for h in range(2)]
        ps_v = [bank(f"ps_v{h}") for h in range(2)]
        ps_kT = [bank(f"ps_kT{h}") for h in range(2)]
        (weights_in, ctx_in, set_up, nw_done, cxT_done, cxT_sb, k_done, v_done, k_out, sq_done, ss_done, sd_done,
         r_done, rm_done, len_done, valid_done, m_half, madd_done, k_scaled, kT_done, kT_sb, v_sb_done, stored) = [
            sem(f"c_{n}") for n in
            ("weights_in ctx_in set_up nw_done cxT_done cxT_sb k_done v_done k_out sq_done ss_done sd_done r_done "
             "rm_done len_done valid_done m_half madd_done k_scaled kT_done kT_sb v_sb_done stored").split()]
        block = ctx.enter_context(nc.Block())
        ident = con[:, C_ID:C_ID + P]

        @block.sync
        def _(sp):
            sp.dma_start(con[:], a["consts"]).then_inc(weights_in, 16)
            sp.dma_start(w_k[:], a["L0_xattn_Wk"].rearrange("(k p) n -> p k n", p=P)).then_inc(weights_in, 16)
            sp.dma_start(w_v[:], a["L0_xattn_Wv"].rearrange("(k p) n -> p k n", p=P)).then_inc(weights_in, 16)
            for k, w in enumerate((a["L0_xattn_q_norm_w"], a["L0_xattn_k_norm_w"])):
                for r in range(2):
                    sp.dma_start(nw[r * XD:(r + 1) * XD, k:k + 1], w.rearrange("(p a) -> p a", a=1)
                                 ).then_inc(weights_in, 16)
            with sp.Fori(0, BATCH) as b:
                sp.wait_ge(cxT_done, b)
                sp.wait_ge(len_done, b)
                sp.dma_start(cx[0:CTX, :], a["ctx_1024"][b]).then_inc(ctx_in, 16)
                sp.dma_start(ctx_len[:], a["_lenS2"].rearrange("(b a) -> b a", a=1)[bass.ds(b, 1), :]
                             .broadcast_to([P, 1])).then_inc(ctx_in, 16)
                sp.wait_ge(kT_sb, 2 * b + 2)
                sp.dma_start(s["kT"][b], kT[:]).then_inc(stored, 16)
                sp.wait_ge(v_sb_done, 2 * b + 2)
                sp.dma_start(s["v"][b], v_sb[0:CTX, :]).then_inc(stored, 16)
                sp.wait_ge(madd_done, b + 1)
                sp.dma_start(s["madd"][b], madd[:]).then_inc(stored, 16)
            sp.wait_ge(stored, 48 * BATCH)

        @block.gpsimd
        def _(pool):
            nc.gpsimd.memset(eps[:], EPS).then_inc(set_up, 1)

        @block.tensor
        def _(pe):
            pe.wait_ge(weights_in, 16 * 7)
            with pe.Fori(0, BATCH) as b:
                pe.wait_ge(ctx_in, b * 32 + 32)
                pe.wait_ge(cxT_sb, b)
                for c in range(KD):
                    mm = pe.transpose(ps_c[:, c * P:c * P + CTX], cx[0:CTX, c * P:(c + 1) * P],
                                      con[0:CTX, C_ID:C_ID + CTX])
                mm.then_inc(cxT_done, 1)
                pe.wait_ge(cxT_sb, b + 1)
                pe.wait_ge(k_out, 2 * b)
                for h in range(2):
                    for c in range(KD):
                        mm = pe.matmul(ps_k[h][0:CTX, :], cxT[:, c, :], w_k[:, c, h * 512:(h + 1) * 512],
                                       start=c == 0, stop=c == KD - 1)
                mm.then_inc(k_done, 1)
                pe.wait_ge(v_sb_done, 2 * b)
                for h in range(2):
                    for c in range(KD):
                        mm = pe.matmul(ps_v[h][0:CTX, :], cxT[:, c, :], w_v[:, c, h * 512:(h + 1) * 512],
                                       start=c == 0, stop=c == KD - 1)
                mm.then_inc(v_done, 1)
                pe.wait_ge(k_scaled, b + 1)
                pe.wait_ge(kT_sb, 2 * b)
                for j in range(XJ):
                    mm = pe.transpose(ps_kT[j // 4][:, (j % 4) * P:(j % 4) * P + CTX],
                                      k_sb[0:CTX, j * P:(j + 1) * P], con[0:CTX, C_ID:C_ID + CTX])
                mm.then_inc(kT_done, 1)

        @block.scalar
        def _(act):
            act.wait_ge(set_up, 1)
            act.wait_ge(nw_done, 1)
            with act.Fori(0, BATCH) as b:
                act.wait_ge(cxT_done, b + 1)
                act.wait_ge(v_done, b)
                nc.scalar.activation(cxT[:], ps_c[:, 0:KD * P].rearrange("p (c j) -> p c j", c=KD)[:, :, 0:CTX],
                                     ACT.Copy).then_inc(cxT_sb, 1)
                act.wait_ge(k_done, b + 1)
                act.wait_ge(kT_done, b)
                act.wait_ge(ss_done, b)
                for h in range(2):
                    nc.scalar.activation(k_sb[0:CTX, h * 512:(h + 1) * 512], ps_k[h][0:CTX, :], ACT.Copy
                                         ).then_inc(k_out, 1)
                act.wait_ge(k_out, 2 * b + 2)
                nc.scalar.activation(k_sq[0:CTX, :], k_sb[0:CTX, :], ACT.Square).then_inc(sq_done, 1)
                act.wait_ge(v_done, b + 1)
                act.wait_ge(stored, b * 48)
                for h in range(2):
                    nc.scalar.activation(v_sb[0:CTX, h * 512:(h + 1) * 512], ps_v[h][0:CTX, :], ACT.Copy
                                         ).then_inc(v_sb_done, 1)
                act.wait_ge(ss_done, b + 1)
                nc.scalar.activation(ss[0:CTX, :], ss[0:CTX, :], ACT.Sqrt, bias=eps[0:CTX, 0:1], scale=1.0 / XD
                                     ).then_inc(sd_done, 1)
                act.wait_ge(kT_done, b + 1)
                for h in range(2):
                    nc.scalar.activation(kT[:, 4 * h:4 * h + 4, :],
                                         ps_kT[h][:].rearrange("p (c j) -> p c j", c=4)[:, :, 0:CTX],
                                         ACT.Copy, scale=nw[:, 0:1]).then_inc(kT_sb, 1)

        @block.vector
        def _(dve):
            dve.wait_ge(weights_in, 16 * 7)
            nc.vector.tensor_tensor(nw[:, 0:1], nw[:, 0:1], nw[:, 1:2], ALU.mult).then_inc(nw_done, 1)
            with dve.Fori(0, BATCH) as b:
                dve.wait_ge(ctx_in, b * 32 + 32)
                nc.vector.tensor_scalar(len_f[:], ctx_len[:], 1.0, None, ALU.mult).then_inc(len_done, 1)
                dve.wait_ge(len_done, b + 1)
                nc.vector.tensor_tensor(valid[:], con[:, C_COL:C_COL + 1], len_f[:], ALU.is_lt
                                        ).then_inc(valid_done, 1)
                dve.wait_ge(stored, b * 48)
                nc.vector.tensor_scalar(madd[:], con[:, C_IOTA:C_IOTA + CTX], len_f[:, 0:1], None, ALU.is_lt
                                        ).then_inc(m_half, 1)
                dve.wait_ge(m_half, b + 1)
                nc.vector.tensor_scalar(madd[:], madd[:], -1.0, 1e9, ALU.add, ALU.mult).then_inc(madd_done, 1)
                dve.wait_ge(sq_done, b + 1)
                dve.wait_ge(k_scaled, b)
                nc.vector.tensor_reduce(ss[0:CTX, :], k_sq[0:CTX, :].rearrange("p (h d) -> p h d", d=XD), AX_X,
                                        ALU.add).then_inc(ss_done, 1)
                dve.wait_ge(sd_done, b + 1)
                nc.vector.reciprocal(ss[0:CTX, :], ss[0:CTX, :]).then_inc(r_done, 1)
                dve.wait_ge(r_done, b + 1)
                dve.wait_ge(valid_done, b + 1)
                nc.vector.tensor_scalar(ss[0:CTX, :], ss[0:CTX, :], valid[0:CTX, 0:1], None, ALU.mult
                                        ).then_inc(rm_done, 1)
                dve.wait_ge(rm_done, b + 1)
                v = k_sb[0:CTX, :].rearrange("p (h d) -> p h d", d=XD)
                nc.vector.tensor_tensor(v, v, ss[0:CTX, :].unsqueeze(2).broadcast_to([CTX, XH, XD]), ALU.mult
                                        ).then_inc(k_scaled, 1)


def cross_stage(nc, a, s):
    with ExitStack() as ctx:
        sb = lambda n, shape: ctx.enter_context(nc.sbuf_tensor(n, shape, F32))
        bank = lambda n: ctx.enter_context(nc.psum_tensor(n, [P, 512], F32))
        sem = ctx.enter_context(stage_semaphores(nc))
        T = range(BLK)
        XJ = XW // P
        per = lambda n, shape: [sb(f"{n}{t}", shape) for t in T]
        x1_v = s["x1"].rearrange("(n t) p d -> n p t d", t=BLK)
        x2_v = s["x2"]
        con = sb("con4", [P, C_N])
        w_q = sb("xw_q", [P, KD, XW])
        w_o = sb("xw_o", [P, XJ, D])
        w_r = sb("w_r", [P, KD, NE])
        eps = sb("eps4", [P, 2])
        zeros = sb("zeros4", [P, D])
        x1b = sb("x1b", [P, BLK, D])
        kT = sb("kT4", [P, XJ, CTX])
        v = sb("v4", [P, XW])
        madd = sb("madd4", [P, CTX])
        x1T = sb("x1T", [P, KD, BT])
        qT = sb("qT", [P, XJ, BT])
        q2 = [sb(f"q2_{k}", [P, BT]) for k in range(2)]
        rq = sb("rq", [P, BLK, XH])
        sc = per("sc", [P, XH, CTX])
        mx = per("mx", [P, XH])
        aT = per("aT", [P, XH, P])
        on = per("on", [P, XW])
        onT = per("onT", [P, XJ, P])
        x2t = per("x2t", [P, D])
        x2T = per("x2T", [P, KD, P])
        lg = per("lg", [P, NE])
        stats = per("stats4_", [P, 6])
        mv = per("mv4_", [P, 2])
        rstd = per("rstd4_", [P, 1])
        A = [bank(f"xA{t}") for t in T]
        B = [bank(f"xB{t}") for t in T]
        J, SS = (A[2], A[3]), B[0]
        weights_in = sem("x_weights_in")
        x1_in = sem("x_x1_in")
        kv_in = sem("x_kv_in")
        zero_out = sem("x_zero_out")
        qp_done = [sem(f"x_qp_done{k}") for k in range(2)]
        q_sb = [sem(f"x_q_sb{k}") for k in range(2)]
        q2_done = [sem(f"x_q2_done{k}") for k in range(2)]
        ss_done = [sem(f"x_ss_done{k}") for k in range(2)]
        x2_out = [sem(f"x_x2_out{t}") for t in T]
        sc_sb = [sem(f"x_sc_sb{t}") for t in T]
        aT_a = [sem(f"x_aT_a{t}") for t in T]
        aT_b = [sem(f"x_aT_b{t}") for t in T]
        names = ("set_up x1T_done x1T_sb rq_sd rq_done sc_done masked mx_done shifted exp_done sum_done "
                 "rs_done aT_done pv_done on_done onT_done onT_a onT_b wo_done y_done st_done st_seen "
                 "mv_done sd_done r_done x2_done x2T_done x2T_sb lg_done lg_sb").split()
        (set_up, x1T_done, x1T_sb, rq_sd, rq_done, sc_done, masked, mx_done, shifted, exp_done, sum_done,
         rs_done, aT_done, pv_done, on_done, onT_done, onT_a, onT_b, wo_done, y_done, st_done, st_seen,
         mv_done, sd_done, r_done, x2_done, x2T_done, x2T_sb, lg_done, lg_sb) = [sem(f"x_{n}") for n in names]
        block = ctx.enter_context(nc.Block())
        ident = con[:, C_ID:C_ID + P]
        HX = XJ // 2

        @block.sync
        def _(sp):
            sp.dma_start(con[:], a["consts"]).then_inc(weights_in, 16)
            sp.dma_start(w_q[:], a["L0_xattn_Wq"].rearrange("(k p) n -> p k n", p=P)).then_inc(weights_in, 16)
            sp.dma_start(w_o[:], a["L0_xattn_Wo"].rearrange("(k p) n -> p k n", p=P)).then_inc(weights_in, 16)
            for c in range(KD):
                sp.dma_start(w_r[:, c, :], a["L0_ffn_router_w"].rearrange("e (k p) -> p k e", p=P)[:, c, :],
                             allow_slow_non_contiguous=True).then_inc(weights_in, 16)
            sp.wait_ge(set_up, 3)
            sp.dma_start(s["xs"].rearrange("t p d -> p t d"), zeros[:].unsqueeze(1).broadcast_to([P, FT + 1, D])
                         ).then_inc(zero_out, 16)
            with sp.Fori(0, BATCH) as i:
                for half in range(2):
                    n = i * 2 + half
                    sp.wait_ge(y_done, n * BLK)
                    sp.dma_start(x1b[:], x1_v[n]).then_inc(x1_in, 16)
                    if half == 0:
                        sp.wait_ge(pv_done, n * BLK)
                        sp.wait_ge(masked, n * BLK)
                        sp.dma_start(kT[:], s["kT"][i]).then_inc(kv_in, 16)
                        sp.dma_start(v[0:CTX, :], s["v"][i]).then_inc(kv_in, 16)
                        sp.dma_start(madd[:], s["madd"][i]).then_inc(kv_in, 16)
            sp.wait_ge(zero_out, 16)

        @block.gpsimd
        def _(pool):
            nc.gpsimd.memset(eps[:, 0:1], EPS).then_inc(set_up, 1)
            nc.gpsimd.memset(eps[:, 1:2], XD * EPS).then_inc(set_up, 1)
            nc.gpsimd.memset(zeros[:], 0.0).then_inc(set_up, 1)
            with pool.Fori(0, BATCH) as i:
                for half in range(2):
                    n = i * 2 + half
                    at = lambda t: n * BLK + t + 1
                    for j in range(XJ):
                        pool.wait_ge(q_sb[j % 2], n * HX + j // 2 + 1)
                        pool.wait_ge(ss_done[j % 2], n * HX + j // 2)
                        nc.gpsimd.tensor_tensor(q2[j % 2][:], qT[:, j, :], qT[:, j, :], ALU.mult
                                                ).then_inc(q2_done[j % 2], 1)
                    pool.wait_ge(kv_in, i * 48 + 48)
                    for t in T:
                        pool.wait_ge(sc_sb[t], n * 2 + 2)
                        nc.gpsimd.tensor_tensor(sc[t][:], sc[t][:], madd[:].unsqueeze(1).broadcast_to([P, XH, CTX]),
                                                ALU.add).then_inc(masked, 1)
                    for t in T:
                        pool.wait_ge(mx_done, at(t))
                        nc.gpsimd.tensor_tensor(sc[t][:], sc[t][:], mx[t][:].unsqueeze(2).broadcast_to([P, XH, CTX]),
                                                ALU.subtract).then_inc(shifted, 1)
                    for t in T:
                        pool.wait_ge(x2_done, at(t))
                        pool.dma_start(x2_v[n * BLK + t], x2t[t][:]).then_inc(x2_out[t], 16)
                    for t in T:
                        pool.wait_ge(lg_sb, at(t))
                        pool.dma_start(s["lg"][n * BLK + t], lg[t][:]).then_inc(x2_out[t], 16)
            for t in T:
                pool.wait_ge(x2_out[t], 32 * BLOCKS)

        @block.tensor
        def _(pe):
            pe.wait_ge(weights_in, 16 * 5)
            with pe.Fori(0, BATCH) as i:
                for half in range(2):
                    n = i * 2 + half
                    at = lambda t: n * BLK + t + 1
                    pe.wait_ge(x1_in, n * 16 + 16)
                    pe.wait_ge(lg_sb, n * BLK)
                    pe.wait_ge(x2T_sb, n * BLK)
                    for c in range(KD):
                        for t in T:
                            mm = pe.transpose(A[c][:, t * P:(t + 1) * P], x1b[:, t, c * P:(c + 1) * P], ident)
                    mm.then_inc(x1T_done, 1)
                    pe.wait_ge(x1T_sb, n * KD + KD)

                    def sums(j):
                        pe.wait_ge(q2_done[j % 2], n * HX + j // 2 + 1)
                        for t in T:
                            mm = pe.matmul(SS[:, t * XH + 2 * j:t * XH + 2 * j + 2], q2[j % 2][:, t * P:(t + 1) * P],
                                           con[:, C_BLK:C_BLK + 2], start=True, stop=True)
                        mm.then_inc(ss_done[j % 2], 1)

                    for j in range(XJ):
                        pe.wait_ge(q_sb[j % 2], n * HX + j // 2)
                        for c in range(KD):
                            mm = pe.matmul(J[j % 2][:], w_q[:, c, j * P:(j + 1) * P], x1T[:, c, :],
                                           start=c == 0, stop=c == KD - 1)
                        mm.then_inc(qp_done[j % 2], 1)
                        if j >= 2:
                            sums(j - 2)
                    for j in (XJ - 2, XJ - 1):
                        sums(j)
                    pe.wait_ge(kv_in, i * 48 + 48)
                    pe.wait_ge(q_sb[1], n * HX + HX)
                    pe.wait_ge(rq_sd, n + 1)
                    for g in range(2):
                        for t in T:
                            if g:
                                pe.wait_ge(sc_sb[t], n * 2 + 1)
                            for tt in range(4):
                                for r, bk in enumerate((A[t], B[t])):
                                    rows = slice(r * XD, (r + 1) * XD)
                                    mm = pe.matmul(bk[:, tt * CTX:(tt + 1) * CTX],
                                                   qT[rows, 4 * g + tt, t * P:(t + 1) * P],
                                                   kT[rows, 4 * g + tt, :], start=True, stop=True)
                            mm.then_inc(sc_done, 1)
                    for g in range(2):
                        for t in T:
                            if g:
                                pe.wait_ge(aT_a[t], n * 2 + 1)
                                pe.wait_ge(aT_b[t], n * 2 + 1)
                            else:
                                pe.wait_ge(exp_done, at(t))
                            for k in range(8):
                                bk = (A, B)[k // 4][t]
                                mm = pe.transpose(bk[0:CTX, (k % 4) * P:(k % 4 + 1) * P], sc[t][:, 8 * g + k, :],
                                                  ident)
                            mm.then_inc(aT_done, 1)
                    for t in T:
                        pe.wait_ge(aT_a[t], n * 2 + 2)
                        pe.wait_ge(aT_b[t], n * 2 + 2)
                        for g in range(2):
                            for tt in range(4):
                                for r in range(2):
                                    h = 8 * g + 2 * tt + r
                                    mm = pe.matmul((A, B)[g][t][:, (2 * tt + r) * XD:(2 * tt + r + 1) * XD],
                                                   aT[t][0:CTX, 8 * g + 4 * r + tt, :], v[0:CTX, h * XD:(h + 1) * XD],
                                                   start=True, stop=True)
                        mm.then_inc(pv_done, 1)
                    for t in T:
                        pe.wait_ge(on_done, at(t))
                        for k in range(XJ):
                            bk = (A, B)[k // 4][t]
                            mm = pe.transpose(bk[:, (k % 4) * P:(k % 4 + 1) * P], on[t][:, k * P:(k + 1) * P], ident)
                        mm.then_inc(onT_done, 1)
                    for t in T:
                        pe.wait_ge(onT_a, at(t))
                        pe.wait_ge(onT_b, at(t))
                        for k in range(XJ):
                            mm = pe.matmul(A[t][:, 0:D], onT[t][:, k, :], w_o[:, k, :], start=k == 0,
                                           stop=k == XJ - 1)
                        mm.then_inc(wo_done, 1)
                    for t in T:
                        pe.wait_ge(x2_done, at(t))
                        for c in range(KD):
                            mm = pe.transpose(B[t][:, c * P:(c + 1) * P], x2t[t][:, c * P:(c + 1) * P], ident)
                        mm.then_inc(x2T_done, 1)
                    for t in T:
                        pe.wait_ge(x2T_sb, at(t))
                        for c in range(KD):
                            mm = pe.matmul(A[t][:, 0:NE], x2T[t][:, c, :], w_r[:, c, :], start=c == 0,
                                           stop=c == KD - 1)
                        mm.then_inc(lg_done, 1)

        @block.scalar
        def _(act):
            act.wait_ge(set_up, 3)
            with act.Fori(0, BATCH) as i:
                for half in range(2):
                    n = i * 2 + half
                    at = lambda t: n * BLK + t + 1
                    act.wait_ge(x1T_done, n + 1)
                    for c in range(KD):
                        nc.scalar.activation(x1T[:, c, :], A[c][:], ACT.Copy).then_inc(x1T_sb, 1)
                    for j in range(XJ):
                        act.wait_ge(qp_done[j % 2], n * HX + j // 2 + 1)
                        nc.scalar.activation(qT[:, j, :], J[j % 2][:], ACT.Copy).then_inc(q_sb[j % 2], 1)
                    act.wait_ge(ss_done[0], n * HX + HX)
                    act.wait_ge(ss_done[1], n * HX + HX)
                    act.wait_ge(sc_sb[BLK - 1], n * 2)
                    nc.scalar.activation(rq[:], SS[:, 0:BLK * XH].rearrange("p (t h) -> p t h", t=BLK), ACT.Sqrt,
                                         bias=eps[:, 1:2]).then_inc(rq_sd, 1)
                    for t in T:
                        act.wait_ge(shifted, at(t))
                        nc.scalar.activation(sc[t][:], sc[t][:], ACT.Exp).then_inc(exp_done, 1)
                    for g in range(2):
                        for t in T:
                            act.wait_ge(aT_done, n * BLK * 2 + g * BLK + t + 1)
                            nc.scalar.activation(aT[t][0:CTX, 8 * g:8 * g + 4, :],
                                                 A[t][0:CTX, :].rearrange("p (k j) -> p k j", k=4), ACT.Copy
                                                 ).then_inc(aT_a[t], 1)
                    for t in T:
                        act.wait_ge(onT_done, at(t))
                        nc.scalar.activation(onT[t][:, 0:4, :], A[t][:].rearrange("p (k j) -> p k j", k=4), ACT.Copy
                                             ).then_inc(onT_a, 1)
                    for t in T:
                        act.wait_ge(mv_done, at(t))
                        nc.scalar.activation(rstd[t][:], mv[t][:, 1:2], ACT.Sqrt, bias=eps[:, 0:1]
                                             ).then_inc(sd_done, 1)
                    for t in T:
                        act.wait_ge(x2T_done, at(t))
                        nc.scalar.activation(x2T[t][:], B[t][:, 0:D].rearrange("p (c j) -> p c j", c=KD), ACT.Copy
                                             ).then_inc(x2T_sb, 1)

        @block.vector
        def _(dve):
            with dve.Fori(0, BATCH) as i:
                for half in range(2):
                    n = i * 2 + half
                    at = lambda t: n * BLK + t + 1
                    dve.wait_ge(rq_sd, n + 1)
                    nc.vector.reciprocal(rq[:], rq[:]).then_inc(rq_done, 1)
                    dve.wait_ge(rq_done, n + 1)
                    for g in range(2):
                        for t in T:
                            dve.wait_ge(sc_done, n * BLK * 2 + g * BLK + t + 1)
                            for r, bk in enumerate((A[t], B[t])):
                                q = rq[:, t, 8 * g:8 * g + 8].rearrange("p (a r) -> p r a", r=2)[:, r, :]
                                m = nc.vector.tensor_tensor(sc[t][:, 8 * g + 4 * r:8 * g + 4 * r + 4, :],
                                                            bk[:, 0:4 * CTX].rearrange("p (a c) -> p a c", c=CTX),
                                                            q.unsqueeze(2).broadcast_to([P, 4, CTX]), ALU.mult)
                            m.then_inc(sc_sb[t], 1)
                    for t in T:
                        dve.wait_ge(masked, at(t))
                        nc.vector.tensor_reduce(mx[t][:], sc[t][:], AX_X, ALU.max).then_inc(mx_done, 1)
                    for t in T:
                        dve.wait_ge(exp_done, at(t))
                        nc.vector.tensor_reduce(mx[t][:], sc[t][:], AX_X, ALU.add).then_inc(sum_done, 1)
                    for t in T:
                        dve.wait_ge(sum_done, at(t))
                        nc.vector.reciprocal(mx[t][:], mx[t][:]).then_inc(rs_done, 1)
                    for g in range(2):
                        for t in T:
                            dve.wait_ge(aT_done, n * BLK * 2 + g * BLK + t + 1)
                            nc.vector.tensor_copy(aT[t][0:CTX, 8 * g + 4:8 * g + 8, :],
                                                  B[t][0:CTX, :].rearrange("p (k j) -> p k j", k=4)
                                                  ).then_inc(aT_b[t], 1)
                    for t in T:
                        dve.wait_ge(pv_done, at(t))
                        dve.wait_ge(rs_done, at(t))
                        for g, bk in enumerate((A[t], B[t])):
                            w = mx[t][:, 8 * g:8 * g + 8].rearrange("p (r a) -> p a r", r=2)
                            m = nc.vector.tensor_tensor(
                                on[t][:, g * 512:(g + 1) * 512].rearrange("p (a r d) -> p a r d", r=2, d=XD),
                                bk[:].rearrange("p (a r d) -> p a r d", r=2, d=XD),
                                w.unsqueeze(3).broadcast_to([P, 4, 2, XD]), ALU.mult)
                        m.then_inc(on_done, 1)
                    for t in T:
                        dve.wait_ge(onT_done, at(t))
                        nc.vector.tensor_copy(onT[t][:, 4:8, :], B[t][:].rearrange("p (k j) -> p k j", k=4)
                                              ).then_inc(onT_b, 1)
                    for t in T:
                        dve.wait_ge(wo_done, at(t))
                        dve.wait_ge(x2_out[t], n * 32)
                        nc.vector.tensor_tensor(x2t[t][:], x1b[:, t, :], A[t][:, 0:D], ALU.add).then_inc(y_done, 1)
                    for t in T:
                        dve.wait_ge(y_done, at(t))
                        nc.vector.bn_stats(stats[t][:], x2t[t][:]).then_inc(st_done, 1)
                    for t in T:
                        dve.wait_ge(st_done, at(t))
                        nc.vector.sem_inc(st_seen, 1)
                        nc.vector.bn_aggr(mv[t][:], stats[t][:]).then_inc(mv_done, 1)
                    for t in T:
                        dve.wait_ge(sd_done, at(t))
                        nc.vector.reciprocal(rstd[t][:], rstd[t][:]).then_inc(r_done, 1)
                    for t in T:
                        dve.wait_ge(r_done, at(t))
                        nc.vector.tensor_scalar(x2t[t][:], x2t[t][:], mv[t][:, 0:1], rstd[t][:, 0:1],
                                                ALU.subtract, ALU.mult).then_inc(x2_done, 1)
                    for t in T:
                        dve.wait_ge(lg_done, at(t))
                        nc.vector.tensor_copy(lg[t][:], A[t][:, 0:NE]).then_inc(lg_sb, 1)


def route_stage(nc, a, s):
    with ExitStack() as ctx:
        sb = lambda n, shape, dt=F32: ctx.enter_context(nc.sbuf_tensor(n, shape, dt))
        sem = ctx.enter_context(stage_semaphores(nc))
        con = sb("con5", [P, C_N])
        lg = sb("lg5", [P, TILES, NE])
        pr = sb("pr", [P, TILES, NE])
        pick = sb("pick", [P, TILES, NE])
        w = sb("w5", [P, TILES, NE])
        pos = sb("pos", [P, TILES, NE])
        cmp1 = sb("cmp1", [P, TILES, NE, NE])
        cmp2 = sb("cmp2", [P, TILES, NE, NE])
        row = sb("row5", [P, TILES])
        tot = sb("tot", [P, TILES, NE])
        cum = sb("cum", [P, NE, TILES])
        k128 = sb("k128", [P, TILES])
        many = sb("many", [P, NE, TILES])
        nt = sb("nt", [P, NE])
        ct = sb("ct", [P, NE])
        base = sb("base", [P, NE])
        of = sb("of", [P, FT, NE])
        off = sb("off", [P, FT])
        posf = sb("posf", [P, 2, TILES])
        xt = [sb(f"xt5_{q}", [P, D]) for q in range(2)]
        idx = [sb(f"idx5_{q}", [P, 2], I32) for q in range(2)]
        ps_w = ctx.enter_context(nc.psum_tensor("ps_w", [P, 512], F32))
        ps_t = ctx.enter_context(nc.psum_tensor("ps_t", [P, 512], F32))
        loaded, steps, shifted, exped, picked, counted, tot_done, placed = [
            sem(f"r_{n}") for n in "loaded steps shifted exped picked counted tot_done placed".split()]
        x_in = [sem(f"r_x_in{q}") for q in range(2)]
        idx_done = [sem(f"r_idx_done{q}") for q in range(2)]
        seen = sem("r_seen")
        x_out = [sem(f"r_x_out{q}") for q in range(2)]
        pos_i, weight, tile_e = s["pos_i"], s["weight"], s["tile_e"]
        block = ctx.enter_context(nc.Block())
        ex = lambda t: t.unsqueeze(2).broadcast_to([P, TILES, NE])

        @block.sync
        def _(sp):
            sp.dma_start(con[:], a["consts"]).then_inc(loaded, 16)
            sp.dma_start(lg[:], s["lg"].rearrange("t p e -> p t e")).then_inc(loaded, 16)
            with sp.Fori(0, TILES // 2) as i:
                for q in range(2):
                    sp.wait_ge(x_out[q], i * 32)
                    sp.dma_start(xt[q][:], s["x2"][i * 2 + q]).then_inc(x_in[q], 16)

        @block.scalar
        def _(act):
            act.wait_ge(shifted, 1)
            nc.scalar.activation(pr[:], pr[:], ACT.Exp).then_inc(exped, 1)

        @block.tensor
        def _(pe):
            pe.wait_ge(loaded, 32)
            pe.wait_ge(picked, 1)
            m = pick[:].rearrange("p t e -> p (t e)")
            pe.matmul(ps_w[:, 0:TILES * NE], con[:, C_LT:C_LT + P], m, start=True, stop=True)
            pe.matmul(ps_t[:, 0:TILES * NE], con[:, C_ONE:C_ONE + P], m, start=True, stop=True).then_inc(counted, 1)

        @block.vector
        def _(dve):
            n = [0]

            def link(ins):
                n[0] += 1
                ins.then_inc(steps, 1)
                dve.wait_ge(steps, n[0])

            V = nc.vector
            dve.wait_ge(loaded, 32)
            link(V.tensor_reduce(row[:], lg[:], AX_X, ALU.max))
            V.tensor_tensor(pr[:], lg[:], ex(row[:]), ALU.subtract).then_inc(shifted, 1)
            link(V.tensor_scalar(k128[:], con[:, C_IOTA:C_IOTA + TILES], float(P), None, ALU.mult))
            dve.wait_ge(exped, 1)
            link(V.tensor_reduce(row[:], pr[:], AX_X, ALU.add))
            link(V.reciprocal(row[:], row[:]))
            link(V.tensor_tensor(pr[:], pr[:], ex(row[:]), ALU.mult))
            one = pr[:].unsqueeze(3).broadcast_to([P, TILES, NE, NE])
            other = pr[:].unsqueeze(2).broadcast_to([P, TILES, NE, NE])
            link(V.tensor_tensor(cmp1[:], other, one, ALU.is_gt))
            link(V.tensor_tensor(cmp2[:], other, one, ALU.is_equal))
            lower = con[:, C_LOW:C_LOW + NE * NE].rearrange("p (a b) -> p a b", b=NE)
            link(V.tensor_tensor(cmp2[:], cmp2[:], lower.unsqueeze(1).broadcast_to([P, TILES, NE, NE]), ALU.mult))
            link(V.tensor_tensor(cmp1[:], cmp1[:], cmp2[:], ALU.add))
            link(V.tensor_reduce(pick[:], cmp1[:], AX_X, ALU.add))
            V.tensor_scalar(pick[:], pick[:], 1.5, None, ALU.is_lt).then_inc(picked, 1)
            dve.wait_ge(picked, 1)
            link(V.tensor_tensor(w[:], pr[:], pick[:], ALU.mult))
            link(V.tensor_reduce(row[:], w[:], AX_X, ALU.add))
            link(V.tensor_scalar(row[:], row[:], 1e-9, None, ALU.add))
            link(V.reciprocal(row[:], row[:]))
            link(V.tensor_tensor(w[:], w[:], ex(row[:]), ALU.mult))
            dve.wait_ge(counted, 1)
            link(V.tensor_copy(tot[:], ps_t[:, 0:TILES * NE].rearrange("p (t e) -> p t e", e=NE)))
            for e in range(NE):
                sc = V.tensor_tensor_scan(cum[:, e, :], con[:, C_ONE:C_ONE + TILES], tot[:, :, e], 0.0,
                                          ALU.mult, ALU.add)
            link(sc)
            link(V.tensor_tensor(many[:], cum[:, :, TILES - 1:TILES].broadcast_to([P, NE, TILES]),
                                 k128[:].unsqueeze(1).broadcast_to([P, NE, TILES]), ALU.is_gt))
            link(V.tensor_reduce(nt[:], many[:], AX_X, ALU.add))
            link(V.tensor_tensor_scan(ct[:], con[:, C_ONE:C_ONE + NE], nt[:], 0.0, ALU.mult, ALU.add))
            link(V.tensor_tensor(base[:], ct[:], nt[:], ALU.subtract))
            link(V.tensor_scalar(base[:], base[:], float(P), None, ALU.mult))
            link(V.tensor_tensor(pos[:], cum[:].rearrange("p e t -> p t e"), tot[:], ALU.subtract))
            link(V.tensor_tensor(pos[:], pos[:], ps_w[:, 0:TILES * NE].rearrange("p (t e) -> p t e", e=NE), ALU.add))
            link(V.tensor_tensor(pos[:], pos[:], base[:].unsqueeze(1).broadcast_to([P, TILES, NE]), ALU.add))
            link(V.tensor_tensor(pos[:], pos[:], pick[:], ALU.mult))
            link(V.tensor_reduce(posf[:, 1, :], pos[:], AX_X, ALU.max))
            link(V.tensor_reduce(posf[:, 0, :], pos[:], AX_X, ALU.add))
            link(V.tensor_tensor(posf[:, 0, :], posf[:, 0, :], posf[:, 1, :], ALU.subtract))
            V.tensor_copy(pos_i[:], posf[:]).then_inc(placed, 1)
            link(V.tensor_tensor(pick[:], pos[:], ex(posf[:, 1, :]), ALU.is_equal))
            link(V.tensor_tensor(pick[:], pick[:], w[:], ALU.mult))
            link(V.tensor_reduce(weight[:, 1, :], pick[:], AX_X, ALU.add))
            link(V.tensor_tensor(w[:], w[:], pick[:], ALU.subtract))
            link(V.tensor_reduce(weight[:, 0, :], w[:], AX_X, ALU.add))
            link(V.tensor_tensor(of[:], con[:, C_IOTA:C_IOTA + FT].unsqueeze(2).broadcast_to([P, FT, NE]),
                                 ct[:].unsqueeze(1).broadcast_to([P, FT, NE]), ALU.is_ge))
            link(V.tensor_reduce(off[:], of[:], AX_X, ALU.add))
            link(V.tensor_scalar(off[:], off[:], float(NE - 1), None, ALU.min))
            link(V.tensor_copy(tile_e[:, 0:FT], off[:]))

        @block.gpsimd
        def _(pool):
            pool.wait_ge(placed, 1)
            with pool.Fori(0, TILES // 2) as i:
                for q in range(2):
                    pool.wait_ge(x_out[q], i * 32)
                    nc.gpsimd.sem_inc(seen, 1)
                    nc.gpsimd.tensor_copy(idx[q][:], pos_i[:, :, i * 2 + q]).then_inc(idx_done[q], 1)
                    pool.wait_ge(idx_done[q], i + 1)
                    pool.wait_ge(x_in[q], i * 16 + 16)
                    nc.gpsimd.sem_inc(seen, 1)
                    for k in range(2):
                        nc.gpsimd.indirect_dma_start(
                            out=s["xs"].rearrange("t p d -> (t p) d"),
                            out_offset=bass.IndirectOffsetOnAxis(ap=idx[q][:, k:k + 1], axis=0),
                            in_=xt[q][:], in_offset=None).then_inc(x_out[q], 16)
            for q in range(2):
                pool.wait_ge(x_out[q], 32 * TILES // 2)


def expert_stage(nc, a, s):
    with ExitStack() as ctx:
        sb = lambda n, shape, dt=F32: ctx.enter_context(nc.sbuf_tensor(n, shape, dt))
        bank = lambda n: ctx.enter_context(nc.psum_tensor(n, [P, 512], F32))
        sem = ctx.enter_context(stage_semaphores(nc))
        Q = range(2)
        two = lambda n, shape: [sb(f"{n}{q}", shape) for q in Q]
        sems = lambda n: [sem(f"e_{n}{q}") for q in Q]
        FK = FF // P
        ident = sb("ident6", [P, P])
        w_gu = sb("w_gu", [P, NE, KD, 2 * FF])
        w_d = sb("w_d", [P, NE, FK, D])
        b_gu = sb("b_gu", [P, NE, 2 * FF])
        b_d = sb("b_d", [P, NE, D])
        xs = two("xs6_", [P, D])
        xsT = two("xsT", [P, KD, P])
        g = two("g6_", [P, FF])
        u = two("u6_", [P, FF])
        hT = two("hT", [P, FK, P])
        o = two("o6_", [P, D])
        pG = [bank(f"pG{q}") for q in Q]
        pU = [bank(f"pU{q}") for q in Q]
        pX, pH = bank("pX6"), bank("pH6")
        pD = [bank(f"pD{q}") for q in Q]
        weights_in = sem("e_weights_in")
        xs_in, xT_done, xT_sb, gu_done, gb_done, ub_done, silu_done, h_done, hT_done, hT_sb, d_done, o_done, o_out = [
            sems(n) for n in ("xs_in xT_done xT_sb gu_done gb_done ub_done silu_done h_done hT_done hT_sb d_done "
                              "o_done o_out").split()]
        tile_e = s["tile_e"]
        LOOPS = (FT - 3) // 2
        NWT = 16 * (1 + 3 * NE + 3)
        block = ctx.enter_context(nc.Block())

        def turns(eng, turn):
            tile = lambda j: (j % 2, j // 2, j)
            turn(None, None, None, tile(0))
            turn(tile(0), None, None, tile(1))
            turn(tile(1), tile(0), None, tile(2))
            turn(tile(2), tile(1), tile(0), tile(3))
            with eng.Fori(0, LOOPS) as i:
                at = lambda k: (k % 2, i + k // 2, i * 2 + k)
                turn(at(3), at(2), at(1), at(4))
                turn(at(4), at(3), at(2), at(5))
            turn(None, tile(FT - 1), tile(FT - 2), None)
            turn(None, None, tile(FT - 1), None)

        @block.sync
        def _(sp):
            sp.dma_start(ident[:], a["consts"][:, C_ID:C_ID + P]).then_inc(weights_in, 16)
            for e in range(NE):
                sp.dma_start(w_gu[:, e, :, 0:FF], a["L0_ffn_gate_w"][e].rearrange("(k p) n -> p k n", p=P)
                             ).then_inc(weights_in, 16)
                sp.dma_start(w_gu[:, e, :, FF:2 * FF], a["L0_ffn_up_w"][e].rearrange("(k p) n -> p k n", p=P)
                             ).then_inc(weights_in, 16)
                sp.dma_start(w_d[:, e], a["L0_ffn_down_w"][e].rearrange("(k p) n -> p k n", p=P)
                             ).then_inc(weights_in, 16)
            for k, n in enumerate(("L0_ffn_gate_b", "L0_ffn_up_b", "L0_ffn_down_b")):
                dst = (b_gu[:, :, 0:FF], b_gu[:, :, FF:2 * FF], b_d[:])[k]
                sp.dma_start(dst, a[n].unsqueeze(0).broadcast_to([P, NE, a[n].shape[1]])).then_inc(weights_in, 16)

            def load(t):
                q, m, j = t
                sp.wait_ge(xT_done[q], m)
                sp.dma_start(xs[q][:], s["xs"][j]).then_inc(xs_in[q], 16)

            def store(t):
                q, m, j = t
                row = s["ys"][j]
                sp.wait_ge(o_done[q], m + 1)
                sp.dma_start(row, o[q][:]).then_inc(o_out[q], 16)

            def turn(t, before, earlier, after):
                if after:
                    load(after)
                if earlier:
                    store(earlier)

            turns(sp, turn)
            sp.wait_ge(o_out[0], 16 * ((FT + 1) // 2))
            sp.wait_ge(o_out[1], 16 * (FT // 2))

        @block.tensor
        def _(pe):
            pe.wait_ge(weights_in, NWT)

            def x_turned(t):
                q, m, _ = t
                pe.wait_ge(xs_in[q], m * 16 + 16)
                pe.wait_ge(xT_sb[1 - q], m if q == 0 else m + 1)
                for c in range(KD):
                    mm = pe.transpose(pX[:, c * P:(c + 1) * P], xs[q][:, c * P:(c + 1) * P], ident[:])
                mm.then_inc(xT_done[q], 1)

            def gate_up(t):
                q, m, j = t
                e = pe.value_load(tile_e[0:1, j:j + 1] if isinstance(j, int) else tile_e[0:1, bass.ds(j, 1)],
                                  min_val=0, max_val=NE - 1)
                pe.wait_ge(xT_sb[q], m + 1)
                pe.wait_ge(ub_done[q], m)
                pe.wait_ge(gb_done[q], m)
                for k, bk in enumerate((pG[q], pU[q])):
                    for c in range(KD):
                        mm = pe.matmul(bk[:], xsT[q][:, c, :], w_gu[:, bass.ds(e, 1), c, k * FF:(k + 1) * FF],
                                       start=c == 0, stop=c == KD - 1)
                mm.then_inc(gu_done[q], 1)

            def h_turned(t):
                q, m, j = t
                pe.wait_ge(h_done[q], m + 1)
                pe.wait_ge(hT_sb[1 - q], m if q == 0 else m + 1)
                for k in range(FK):
                    mm = pe.transpose(pH[:, k * P:(k + 1) * P], g[q][:, k * P:(k + 1) * P], ident[:])
                mm.then_inc(hT_done[q], 1)

            def down(t):
                q, m, j = t
                e = pe.value_load(tile_e[0:1, j:j + 1] if isinstance(j, int) else tile_e[0:1, bass.ds(j, 1)],
                                  min_val=0, max_val=NE - 1)
                pe.wait_ge(hT_sb[q], m + 1)
                pe.wait_ge(o_done[q], m)
                for k in range(FK):
                    mm = pe.matmul(pD[q][:, 0:D], hT[q][:, k, :], w_d[:, bass.ds(e, 1), k, :], start=k == 0,
                                   stop=k == FK - 1)
                mm.then_inc(d_done[q], 1)

            def turn(t, before, earlier, after):
                if t:
                    gate_up(t)
                if after:
                    x_turned(after)
                if before:
                    h_turned(before)
                if earlier:
                    down(earlier)

            turns(pe, turn)

        @block.scalar
        def _(act):
            def x_out(t):
                q, m, _ = t
                act.wait_ge(xT_done[q], m + 1)
                act.wait_ge(gu_done[q], m)
                nc.scalar.activation(xsT[q][:], pX[:, 0:D].rearrange("p (c j) -> p c j", c=KD), ACT.Copy
                                     ).then_inc(xT_sb[q], 1)

            def silu(t):
                q, m, _ = t
                act.wait_ge(gb_done[q], m + 1)
                nc.scalar.activation(g[q][:], g[q][:], ACT.Silu).then_inc(silu_done[q], 1)

            def h_out(t):
                q, m, _ = t
                act.wait_ge(hT_done[q], m + 1)
                act.wait_ge(d_done[q], m)
                nc.scalar.activation(hT[q][:], pH[:].rearrange("p (k j) -> p k j", k=FK), ACT.Copy
                                     ).then_inc(hT_sb[q], 1)

            def turn(t, before, earlier, after):
                if after:
                    x_out(after)
                if before:
                    h_out(before)
                if t:
                    silu(t)

            turns(act, turn)

        @block.vector
        def _(dve):
            dve.wait_ge(weights_in, NWT)

            def biased(t):
                q, m, j = t
                e = dve.value_load(tile_e[0:1, j:j + 1] if isinstance(j, int) else tile_e[0:1, bass.ds(j, 1)],
                                   min_val=0, max_val=NE - 1)
                dve.wait_ge(gu_done[q], m + 1)
                dve.wait_ge(hT_done[q], m)
                nc.vector.tensor_tensor(g[q][:], pG[q][:], b_gu[:, bass.ds(e, 1), 0:FF], ALU.add
                                        ).then_inc(gb_done[q], 1)
                nc.vector.tensor_tensor(u[q][:], pU[q][:], b_gu[:, bass.ds(e, 1), FF:2 * FF], ALU.add
                                        ).then_inc(ub_done[q], 1)

            def hidden(t):
                q, m, j = t
                dve.wait_ge(silu_done[q], m + 1)
                dve.wait_ge(ub_done[q], m + 1)
                nc.vector.tensor_tensor(g[q][:], g[q][:], u[q][:], ALU.mult).then_inc(h_done[q], 1)

            def out(t):
                q, m, j = t
                e = dve.value_load(tile_e[0:1, j:j + 1] if isinstance(j, int) else tile_e[0:1, bass.ds(j, 1)],
                                   min_val=0, max_val=NE - 1)
                dve.wait_ge(d_done[q], m + 1)
                dve.wait_ge(o_out[q], m * 16)
                nc.vector.tensor_tensor(o[q][:], pD[q][:, 0:D], b_d[:, bass.ds(e, 1), :], ALU.add
                                        ).then_inc(o_done[q], 1)

            def turn(t, before, earlier, after):
                if t:
                    biased(t)
                if earlier:
                    out(earlier)
                if t:
                    hidden(t)

            turns(dve, turn)


def combine_stage(nc, a, s, out):
    with ExitStack() as ctx:
        sb = lambda n, shape, dt=F32: ctx.enter_context(nc.sbuf_tensor(n, shape, dt))
        sem = ctx.enter_context(stage_semaphores(nc))
        R = 4
        r_ = range(R)
        sems = lambda n: [sem(f"f_{n}{q}") for q in r_]
        x2 = [sb(f"x2_7{q}", [P, D]) for q in r_]
        z = [sb(f"z7_{q}", [P, D]) for q in r_]
        ya = [[sb(f"y7_{q}{k}", [P, D]) for k in range(2)] for q in r_]
        idx = [sb(f"idx7_{q}", [P, 2], I32) for q in r_]
        wt = [sb(f"wt7_{q}", [P, 2]) for q in r_]
        stats = [sb(f"stats7_{q}", [P, 6]) for q in r_]
        mv = [sb(f"mv7_{q}", [P, 2]) for q in r_]
        rstd = [sb(f"rstd7_{q}", [P, 1]) for q in r_]
        eps = sb("eps7", [P, 1])
        set_up, seen, dseen = sem("f_set_up"), sem("f_seen"), sem("f_dseen")
        x_in, y_in, idx_done, wt_done, a_done, b_done, st_done, mv_done, sd_done, r_done, z_done, z_out = [
            sems(n) for n in ("x_in y_in idx_done wt_done a_done b_done st_done mv_done sd_done r_done z_done "
                              "z_out").split()]
        out_v = out.rearrange("b (c p) d -> (b c) p d", p=P)
        block = ctx.enter_context(nc.Block())

        @block.sync
        def _(sp):
            with sp.Fori(0, TILES // R) as i:
                for q in r_:
                    sp.wait_ge(z_done[q], i)
                    sp.dma_start(x2[q][:], s["x2"][i * R + q]).then_inc(x_in[q], 16)
                for q in r_:
                    sp.wait_ge(z_done[q], i + 1)
                    sp.dma_start(out_v[i * R + q], z[q][:]).then_inc(z_out[q], 16)
            for q in r_:
                sp.wait_ge(z_out[q], 16 * TILES // R)

        @block.gpsimd
        def _(pool):
            nc.gpsimd.memset(eps[:], EPS).then_inc(set_up, 1)
            with pool.Fori(0, TILES // R) as i:
                for q in r_:
                    pool.wait_ge(y_in[q], i * 32)
                    nc.gpsimd.sem_inc(seen, 1)
                    nc.gpsimd.tensor_copy(idx[q][:], s["pos_i"][:, :, i * R + q]).then_inc(idx_done[q], 1)
                    pool.wait_ge(idx_done[q], i + 1)
                    pool.wait_ge(b_done[q], i)
                    nc.gpsimd.sem_inc(seen, 1)
                    for k in range(2):
                        nc.gpsimd.indirect_dma_start(
                            out=ya[q][k][:], out_offset=None, in_=s["ys"].rearrange("t p d -> (t p) d"),
                            in_offset=bass.IndirectOffsetOnAxis(ap=idx[q][:, k:k + 1], axis=0)
                        ).then_inc(y_in[q], 16)

        @block.scalar
        def _(act):
            act.wait_ge(set_up, 1)
            with act.Fori(0, TILES // R) as i:
                for q in r_:
                    act.wait_ge(mv_done[q], i + 1)
                    nc.scalar.activation(rstd[q][:], mv[q][:, 1:2], ACT.Sqrt, bias=eps[:, 0:1]
                                         ).then_inc(sd_done[q], 1)

        @block.vector
        def _(dve):
            with dve.Fori(0, TILES // R) as i:
                for q in r_:
                    dve.wait_ge(b_done[q], i)
                    nc.vector.tensor_scalar(wt[q][:], s["weight"][:, :, i * R + q], 1.0, None, ALU.mult
                                            ).then_inc(wt_done[q], 1)
                for q in r_:
                    dve.wait_ge(x_in[q], i * 16 + 16)
                    dve.wait_ge(y_in[q], i * 32 + 32)
                    dve.wait_ge(wt_done[q], i + 1)
                    nc.vector.scalar_tensor_tensor(x2[q][:], ya[q][0][:], wt[q][:, 0:1], x2[q][:], ALU.mult,
                                                   ALU.add).then_inc(a_done[q], 1)
                for q in r_:
                    dve.wait_ge(a_done[q], i + 1)
                    nc.vector.scalar_tensor_tensor(x2[q][:], ya[q][1][:], wt[q][:, 1:2], x2[q][:], ALU.mult,
                                                   ALU.add).then_inc(b_done[q], 1)
                for q in r_:
                    dve.wait_ge(b_done[q], i + 1)
                    nc.vector.bn_stats(stats[q][:], x2[q][:]).then_inc(st_done[q], 1)
                for q in r_:
                    dve.wait_ge(st_done[q], i + 1)
                    nc.vector.sem_inc(dseen, 1)
                    nc.vector.bn_aggr(mv[q][:], stats[q][:]).then_inc(mv_done[q], 1)
                for q in r_:
                    dve.wait_ge(sd_done[q], i + 1)
                    nc.vector.reciprocal(rstd[q][:], rstd[q][:]).then_inc(r_done[q], 1)
                for q in r_:
                    dve.wait_ge(r_done[q], i + 1)
                    dve.wait_ge(z_out[q], i * 16)
                    nc.vector.tensor_scalar(z[q][:], x2[q][:], mv[q][:, 0:1], rstd[q][:, 0:1],
                                            ALU.subtract, ALU.mult).then_inc(z_done[q], 1)


def build(nc, a, out, stages=99):
    dram = lambda n, shape: nc.dram_tensor(n, shape, F32, kind="Internal").ap()
    s = {
        "qkvg": dram("qkvg", [TILES, P, QKV + DV]),
        "gb": dram("gb", [TILES, P, 2 * H]),
        "x1": dram("x1", [TILES, P, D]),
        "kT": dram("kT", [BATCH, P, XW // P, CTX]),
        "v": dram("v", [BATCH, CTX, XW]),
        "madd": dram("madd", [BATCH, P, CTX]),
        "x2": dram("x2", [TILES, P, D]),
        "lg": dram("lg", [TILES, P, NE]),
        "xs": dram("xs", [FT + 1, P, D]),
        "ys": dram("ys", [FT, P, D]),
    }
    if stages == 3:
        s["x1"] = a["x1dbg"]
    else:
        project_stage(nc, a, s)
        delta_stage(nc, a, s)
    context_stage(nc, a, s)
    cross_stage(nc, a, s)
    with ExitStack() as ctx:
        s["pos_i"] = ctx.enter_context(nc.sbuf_tensor("pos_i", [P, 2, TILES], I32))
        s["weight"] = ctx.enter_context(nc.sbuf_tensor("weight", [P, 2, TILES], F32))
        s["tile_e"] = ctx.enter_context(nc.sbuf_tensor("tile_e", [P, FT + 1], I32))
        route_stage(nc, a, s)
        expert_stage(nc, a, s)
        combine_stage(nc, a, s, out)


_INS = ['x', 'ctx_1024', '_lenS2', 'L0_attn_ln_w', 'L0_attn_ln_b', 'L0_attn_Wq', 'L0_attn_Wk', 'L0_attn_Wv',
        'L0_attn_conv_q', 'L0_attn_conv_k', 'L0_attn_conv_v', 'L0_attn_Wb', 'L0_attn_Wa', 'L0_attn_A_log',
        'L0_attn_dt_bias', 'L0_attn_Wg', 'L0_attn_norm_w', 'L0_attn_Wo', 'L0_xattn_Wq', 'L0_xattn_Wk',
        'L0_xattn_Wv', 'L0_xattn_Wo', 'L0_xattn_q_norm_w', 'L0_xattn_k_norm_w', 'L0_ffn_router_w',
        'L0_ffn_gate_w', 'L0_ffn_gate_b', 'L0_ffn_up_w', 'L0_ffn_up_b', 'L0_ffn_down_w', 'L0_ffn_down_b']


def kernel(**inputs):
    import concourse.bacc as _bacc
    from concourse.bass_utils import run_bass_kernel_spmd as _run

    nc = _bacc.Bacc("TRN2", target_bir_lowering=False, num_devices=1)
    arrays, aps = {}, {}
    for name in _INS:
        arrays[f"in_{name}"] = np.ascontiguousarray(inputs[name])
    arrays["in_consts"] = constants()
    for name, v in arrays.items():
        aps[name[3:]] = nc.dram_tensor(name, v.shape, mybir.dt.from_np(v.dtype), kind="ExternalInput").ap()
    out = nc.dram_tensor("out", [BATCH, SEQ, D], F32, kind="ExternalOutput").ap()
    build(nc, aps, out)
    r = _run(nc, [arrays], core_ids=[0])
    return r.results[0]["out"]
```

```python
from contextlib import ExitStack, contextmanager

import numpy as np

import concourse.bass as bass
from concourse import mybir

P = 128
F32 = mybir.dt.float32
I32 = mybir.dt.int32
ALU = mybir.AluOpType
ACT = mybir.ActivationFunctionType
AX_X = mybir.AxisListType.X

BATCH, SEQ, D = 4, 1024, 256
KD = D // P
TILES = BATCH * SEQ // P
BLK = 4
BT = BLK * P
BLOCKS = TILES // BLK
H, HK, HV, TAPS = 4, 64, 128, 4
DK, DV = H * HK, H * HV
QKV = 2 * DK + DV
CHUNKS = SEQ // P
EPS = 1e-5
NORM_EPS = 1e-6
DECAY_FLOOR = -200.0
XH, XD, CTX = 16, 64, 77
XW = XH * XD
KC = CTX + CTX % 2
NE, FF = 8, 512
FT = (TILES * P * 2) // P + NE - 1

C_ID, C_LE, C_GT, C_GE, C_ONE = 0, P, 2 * P, 3 * P, 4 * P
C_NM0 = 5 * P
C_LEV = 6 * P
LEVELS = 7
C_BLK = C_LEV + (LEVELS - 1) * P // 2
C_LT = C_BLK + 2
C_IOTA = C_LT + P
C_COL = C_IOTA + P
C_LOW = C_COL + 1
C_HEAD = C_LOW + NE * NE
C_N = C_HEAD + XW // P * XH


def constants():
    p, j = np.arange(P)[:, None], np.arange(P)[None, :]
    c = np.zeros((P, C_N), np.float32)
    c[:, C_ID:C_ID + P] = p == j
    c[:, C_LE:C_LE + P] = p <= j
    c[:, C_GT:C_GT + P] = p > j
    c[:, C_GE:C_GE + P] = p >= j
    c[:, C_ONE:C_ONE + P] = 1
    c[:, C_NM0:C_NM0 + P] = -1.0 * ((p // 2 == j // 2) & (p % 2 == 1) & (j % 2 == 0))
    for lev in range(1, LEVELS):
        s = 2 ** lev
        m = (p // (2 * s) == j // (2 * s)) & (p % (2 * s) < s) & (j % (2 * s) >= s)
        c[:, C_LEV + (lev - 1) * P // 2:C_LEV + lev * P // 2] = m[:, (np.arange(P) % (2 * s)) >= s]
    c[:, C_BLK:C_BLK + 2] = p // XD == np.arange(2)[None, :]
    c[:, C_LT:C_LT + P] = p < j
    c[:, C_IOTA:C_IOTA + P] = j
    c[:, C_COL:C_COL + 1] = p
    e = np.arange(NE)
    c[:, C_LOW:C_HEAD] = (e[None, :] < e[:, None]).reshape(1, -1)
    for j in range(XW // P):
        c[:, C_HEAD + j * XH:C_HEAD + (j + 1) * XH] = np.arange(XH)[None, :] == 2 * j + p // XD
    return c


@contextmanager
def stage_semaphores(nc):
    taken = []

    def sem(name):
        taken.append(nc.alloc_semaphore(name=name))
        return taken[-1]

    yield sem
    nc.clear_and_free_semaphores(taken)
    nc.all_engine_barrier()


def project_stage(nc, a, s):
    with ExitStack() as ctx:
        sb = lambda n, shape: ctx.enter_context(nc.sbuf_tensor(n, shape, F32))
        bank = lambda n: ctx.enter_context(nc.psum_tensor(n, [P, 512], F32))
        sem = ctx.enter_context(stage_semaphores(nc))

        NCT = QKV // P
        TURN_JOB = NCT - 3
        x_v = a["x"].rearrange("b (n t p) d -> (b n) p t d", t=BLK, p=P)
        tok_v = s["qkvg"].rearrange("(n t) p c -> n p t c", t=BLK)

        con = sb("con1", [P, C_N])
        w_qkv = sb("w_qkv", [P, KD, QKV])
        w_gate = sb("w_gate", [P, KD, DV])
        w_ba = sb("w_ba", [P, KD, 2 * H])
        taps = sb("taps", [P, NCT, TAPS])
        ln_wb = sb("ln_wb", [P, 2, KD])
        head_row = sb("head_row", [P, 2, H])
        neg_rate = sb("neg_rate", [P, H])
        eps = sb("eps1", [P, 2])
        xin = [sb(f"xin{b}", [P, BLK, D]) for b in range(2)]
        stats = sb("stats1", [P, BLK, 6])
        mv = sb("mv1", [P, BLK, 2])
        rstd = sb("rstd1", [P, BLK])
        xnT = [sb(f"xnT{b}", [P, KD, BT]) for b in range(2)]
        conv_in = [sb(f"conv_in{b}", [P, NCT, TAPS - 1 + BT]) for b in range(2)]
        conv_y = [sb(f"conv_y{b}", [P, BT]) for b in range(4)]
        act_y = [sb(f"act_y{b}", [P, BT]) for b in range(2)]
        tok = [sb(f"tok{b}", [P, BLK, QKV]) for b in range(2)]
        gate = [sb(f"gate{b}", [P, BLK, DV]) for b in range(2)]
        sq = sb("sq1", [P, BLK, 2 * DK])
        ss = sb("ss1", [P, BLK, 2 * H])
        rn = sb("rn1", [P, BLK, 2 * H])
        beta = [sb(f"beta{b}", [P, BLK, H]) for b in range(2)]
        ba = sb("ba1", [P, BLOCKS + 1, BLK, 2 * H])
        sm = sb("sm1", [P, 6, TILES, H])
        gb = sb("gb1", [P, TILES, 2 * H])

        ps_x = [bank(f"ps_x{c}") for c in range(KD)]
        ps_j = [bank(f"ps_j{c}") for c in range(2)]
        ps_t = [bank(f"ps_t{c}") for c in range(2)]
        ps_g = bank("ps_g")
        ps_ba = bank("ps_ba")

        weights_in = sem("weights_in")
        x_in = [sem(f"x_in{b}") for b in range(2)]
        consts_set = sem("consts_set")
        rate_exp = sem("rate_exp")
        rate_neg = sem("rate_neg")
        stats_done = sem("stats_done")
        stats_seen = sem("stats_seen")
        var_done = sem("var_done")
        sd_done = sem("sd_done")
        rstd_done = sem("rstd_done")
        xn_done = sem("xn_done")
        xT_done = sem("xT_done")
        xnT_done = sem("xnT_done")
        proj_done = [sem(f"proj_done{b}") for b in range(2)]
        proj_taken = [sem(f"proj_taken{b}") for b in range(2)]
        gate_done = sem("gate_done")
        gate_taken = sem("gate_taken")
        ba_done = sem("ba_done")
        hist_set = sem("hist_set")
        tap_done = [sem(f"tap_done{b}") for b in range(2)]
        conv_step = sem("conv_step")
        conv_done = sem("conv_done")
        silu_done = [sem(f"silu_done{b}") for b in range(2)]
        tokT_done = [sem(f"tokT_done{b}") for b in range(2)]
        tok_taken = [sem(f"tok_taken{b}") for b in range(2)]
        sq_done = sem("sq_done")
        ss_done = sem("ss_done")
        norm_sd = sem("norm_sd")
        norm_r = sem("norm_r")
        scaled = sem("scaled")
        beta_scaled = sem("beta_scaled")
        ba_sb = sem("ba_sb")
        beta_exp = sem("beta_exp")
        beta_done = sem("beta_done")
        z_abs = sem("z_abs")
        exps_done = sem("exps_done")
        soft = sem("soft")
        gb_done = sem("gb_done")
        tok_out = [sem(f"tok_out{b}") for b in range(2)]

        block = ctx.enter_context(nc.Block())

        def view_heads(t, lo, n, d):
            return t[:, :, lo:lo + n * d].rearrange("p t (h d) -> p t h d", d=d)

        @block.sync
        def _(sp):
            sp.dma_start(xin[0][:], x_v[0]).then_inc(x_in[0], 16)
            sp.dma_start(con[:], a["consts"]).then_inc(weights_in, 16)
            for k, w in enumerate((a["L0_attn_Wq"], a["L0_attn_Wk"], a["L0_attn_Wv"])):
                lo = (0, DK, 2 * DK)[k]
                sp.dma_start(w_qkv[:, :, lo:lo + w.shape[1]],
                             w.rearrange("(k p) n -> p k n", p=P)).then_inc(weights_in, 16)
            sp.dma_start(w_gate[:], a["L0_attn_Wg"].rearrange("(k p) n -> p k n", p=P)).then_inc(weights_in, 16)
            for k, w in enumerate((a["L0_attn_Wb"], a["L0_attn_Wa"])):
                sp.dma_start(w_ba[:, :, k * H:(k + 1) * H],
                             w.rearrange("(k p) n -> p k n", p=P)).then_inc(weights_in, 16)
            for k, w in enumerate((a["L0_attn_conv_q"], a["L0_attn_conv_k"], a["L0_attn_conv_v"])):
                lo, n = (0, DK // P, 2 * DK // P)[k], w.shape[0] // P
                sp.dma_start(taps[:, lo:lo + n, :],
                             w.rearrange("(m p) k -> p m k", p=P)).then_inc(weights_in, 16)
            for k, w in enumerate((a["L0_attn_ln_w"], a["L0_attn_ln_b"])):
                sp.dma_start(ln_wb[:, k, :], w.rearrange("(k p) -> p k", p=P), allow_slow_non_contiguous=True
                             ).then_inc(weights_in, 16)
            for k, w in enumerate((a["L0_attn_A_log"], a["L0_attn_dt_bias"])):
                sp.dma_start(head_row[:, k, :],
                             w.rearrange("(a h) -> a h", a=1).broadcast_to([P, H])).then_inc(weights_in, 16)
            sp.dma_start(xin[1][:], x_v[1]).then_inc(x_in[1], 16)
            sp.wait_ge(xT_done, 1)
            sp.dma_start(xin[0][:], x_v[2]).then_inc(x_in[0], 16)
            with sp.Fori(0, BLOCKS // 2) as i:
                for b in range(2):
                    n = i * 2 + b
                    sp.wait_ge(xT_done, n + 2)
                    sp.dma_start(xin[1 - b][:], x_v[(i * 2 + 2 + 2 * b) % BLOCKS + 1 - b]).then_inc(x_in[1 - b], 16)
                    sp.wait_ge(beta_scaled, n + 1)
                    sp.wait_ge(scaled, n + 1)
                    sp.wait_ge(tok_taken[0], n * (NCT // 2) + NCT // 2)
                    sp.wait_ge(tok_taken[1], n * (NCT // 2) + NCT // 2)
                    sp.dma_start(tok_v[n][:, :, 0:QKV], tok[b][:]).then_inc(tok_out[b], 16)
                    sp.wait_ge(gate_taken, n * BLK + BLK)
                    sp.dma_start(tok_v[n][:, :, QKV:QKV + DV], gate[b][:]).then_inc(tok_out[b], 16)
            sp.wait_ge(gb_done, 2)
            sp.dma_start(s["gb"].rearrange("t p c -> p t c"), gb[:]).then_inc(tok_out[0], 16)
            sp.wait_ge(tok_out[0], 32 * (BLOCKS // 2) + 16)
            sp.wait_ge(tok_out[1], 32 * (BLOCKS // 2))
            sp.wait_ge(x_in[0], 16 * (BLOCKS // 2 + 2))

        @block.gpsimd
        def _(pool):
            nc.gpsimd.memset(eps[:, 0:1], EPS).then_inc(consts_set, 1)
            nc.gpsimd.memset(eps[:, 1:2], NORM_EPS).then_inc(consts_set, 1)
            nc.gpsimd.memset(conv_in[0][:, :, 0:TAPS - 1], 0.0).then_inc(consts_set, 1)
            with pool.Fori(0, BLOCKS // 2) as i:
                for b in range(2):
                    n = i * 2 + b
                    for k in range(2):
                        pool.wait_ge(tok_taken[0], n * (NCT // 2) + k + 1)
                        pool.wait_ge(tok_taken[1], n * (NCT // 2) + k + 1)
                        pool.wait_ge(ss_done, n)
                        part = tok[b][:, :, k * DK:(k + 1) * DK]
                        nc.gpsimd.tensor_tensor(sq[:, :, k * DK:(k + 1) * DK], part, part, ALU.mult
                                                ).then_inc(sq_done, 1)
                    if b == 0:
                        pool.wait_ge(proj_taken[0], n * (NCT // 2) + NCT // 2)
                        pool.wait_ge(proj_taken[1], n * (NCT // 2) + NCT // 2)
                        pool.wait_ge(conv_done, n * NCT)
                        ones = con[:, C_ONE:C_ONE + TAPS - 1].unsqueeze(1).broadcast_to([P, NCT, TAPS - 1])
                        nc.gpsimd.tensor_tensor(conv_in[1][:, :, 0:TAPS - 1], conv_in[0][:, :, BT:BT + TAPS - 1],
                                                ones, ALU.mult).then_inc(hist_set, 1)
                    pool.wait_ge(norm_r, n * 2 + 2)
                    v = view_heads(tok[b], 0, 2 * H, HK)
                    nc.gpsimd.tensor_tensor(v, v, rn[:].unsqueeze(3).broadcast_to([P, BLK, 2 * H, HK]),
                                            ALU.mult).then_inc(scaled, 1)
                    pool.wait_ge(beta_done, n + 1)
                    pool.wait_ge(tok_taken[0], n * (NCT // 2) + NCT // 2)
                    pool.wait_ge(tok_taken[1], n * (NCT // 2) + NCT // 2)
                    v = view_heads(tok[b], 2 * DK, H, HV)
                    nc.gpsimd.tensor_tensor(v, v, beta[b][:].unsqueeze(3).broadcast_to([P, BLK, H, HV]),
                                            ALU.mult).then_inc(beta_scaled, 1)

        @block.tensor
        def _(pe):
            pe.wait_ge(weights_in, 16 * 14)

            def x_turned(n, b):
                pe.wait_ge(xn_done, n + 1)
                pe.wait_ge(xnT_done, n * KD)
                for c in range(KD):
                    for t in range(BLK):
                        mm = pe.transpose(ps_x[c][:, t * P:(t + 1) * P], xin[b][:, t, c * P:(c + 1) * P],
                                          con[:, C_ID:C_ID + P])
                mm.then_inc(xT_done, 1)

            def beta_decay(n, b):
                pe.wait_ge(xnT_done, n * KD + KD)
                pe.wait_ge(ba_sb, n)
                for t in range(BLK):
                    for c in range(KD):
                        mm = pe.matmul(ps_ba[:, t * 2 * H:(t + 1) * 2 * H], xnT[b][:, c, t * P:(t + 1) * P],
                                       w_ba[:, c, :], start=c == 0, stop=c == KD - 1)
                mm.then_inc(ba_done, 1)

            x_turned(0, 0)
            beta_decay(0, 0)
            with pe.Fori(0, BLOCKS // 2) as i:
                for b in range(2):
                    n = i * 2 + b
                    def to_tokens(m):
                        pe.wait_ge(silu_done[m % 2], n * (NCT // 2) + m // 2 + 1)
                        pe.wait_ge(tok_taken[m % 2], n * (NCT // 2) + m // 2)
                        for t in range(BLK):
                            mm = pe.transpose(ps_t[m % 2][:, t * P:(t + 1) * P],
                                              act_y[m % 2][:, t * P:(t + 1) * P], con[:, C_ID:C_ID + P])
                        mm.then_inc(tokT_done[m % 2], 1)

                    for j in range(NCT + 3):
                        if j < NCT:
                            pe.wait_ge(proj_taken[j % 2], n * (NCT // 2) + j // 2)
                            for c in range(KD):
                                mm = pe.matmul(ps_j[j % 2][:], w_qkv[:, c, j * P:(j + 1) * P], xnT[b][:, c, :],
                                               start=c == 0, stop=c == KD - 1)
                            mm.then_inc(proj_done[j % 2], 1)
                        if 3 <= j:
                            to_tokens(j - 3)
                        if j % 2 and j < NCT:
                            t = j // 2
                            pe.wait_ge(gate_taken, n * BLK + t)
                            for c in range(KD):
                                mm = pe.matmul(ps_g[:], xnT[b][:, c, t * P:(t + 1) * P], w_gate[:, c, :],
                                               start=c == 0, stop=c == KD - 1)
                            mm.then_inc(gate_done, 1)
                        if j == TURN_JOB:
                            x_turned(n + 1, 1 - b)
                        if j == TURN_JOB + 2:
                            beta_decay(n + 1, 1 - b)

        @block.scalar
        def _(act):
            act.wait_ge(weights_in, 16 * 14)
            act.wait_ge(consts_set, 3)
            nc.scalar.activation(neg_rate[:], head_row[:, 0, :], ACT.Exp).then_inc(rate_exp, 1)

            def block_sd(n):
                act.wait_ge(var_done, n + 1)
                act.wait_ge(xn_done, n)
                nc.scalar.activation(rstd[:], mv[:, :, 1], ACT.Sqrt, bias=eps[:, 0:1]).then_inc(sd_done, 1)

            def x_out(n, b):
                act.wait_ge(xT_done, n + 1)
                for c in range(KD):
                    nc.scalar.activation(xnT[b][:, c, :], ps_x[c][:], ACT.Identity,
                                         bias=ln_wb[:, 1, c:c + 1],
                                         scale=ln_wb[:, 0, c:c + 1]).then_inc(xnT_done, 1)

            def exps(n, b):
                act.wait_ge(ba_done, n + 1)
                act.wait_ge(beta_done, n)
                logit = ps_ba[:, 0:BLK * 2 * H].rearrange("p (t h) -> p t h", t=BLK)[:, :, 0:H]
                nc.scalar.activation(beta[b][:], logit, ACT.Exp, scale=-1.0).then_inc(beta_exp, 1)

            block_sd(0)
            block_sd(1)
            x_out(0, 0)
            exps(0, 0)
            with act.Fori(0, BLOCKS // 2) as i:
                for b in range(2):
                    n = i * 2 + b
                    if b == 0:
                        act.wait_ge(hist_set, i)

                    def silu(m):
                        act.wait_ge(conv_done, n * NCT + m + 1)
                        act.wait_ge(tokT_done[m % 2], n * (NCT // 2) + m // 2)
                        nc.scalar.activation(act_y[m % 2][:], conv_y[m % 4][:], ACT.Silu
                                             ).then_inc(silu_done[m % 2], 1)

                    def take_tokens(m):
                        act.wait_ge(tokT_done[m % 2], n * (NCT // 2) + m // 2 + 1)
                        if m == 0:
                            act.wait_ge(tok_out[b], i * 32)
                        nc.scalar.activation(tok[b][:, :, m * P:(m + 1) * P],
                                             ps_t[m % 2][:].rearrange("p (t c) -> p t c", t=BLK),
                                             ACT.Copy).then_inc(tok_taken[m % 2], 1)

                    for j in range(NCT + 4):
                        if j < NCT:
                            act.wait_ge(proj_done[j % 2], n * (NCT // 2) + j // 2 + 1)
                            nc.scalar.activation(conv_in[b][:, j, TAPS - 1:TAPS - 1 + BT], ps_j[j % 2][:], ACT.Copy)
                            act.wait_ge(silu_done[j % 2], n * (NCT // 2) + max(j // 2 - 1, 0))
                            nc.scalar.activation(conv_y[j % 4][:], ps_j[j % 2][:], ACT.Copy,
                                                 scale=taps[:, j, TAPS - 1:TAPS]).then_inc(proj_taken[j % 2], 1)
                        if 2 <= j < NCT + 2:
                            silu(j - 2)
                        if 4 <= j:
                            take_tokens(j - 4)
                        if j % 2 and j < NCT:
                            act.wait_ge(gate_done, n * BLK + j // 2 + 1)
                            if j == 1:
                                act.wait_ge(tok_out[b], i * 32)
                            nc.scalar.activation(gate[b][:, j // 2, :], ps_g[:], ACT.Silu).then_inc(gate_taken, 1)
                        if j == TURN_JOB + 1:
                            x_out(n + 1, 1 - b)
                        if j == NCT + 1:
                            block_sd(n + 2)
                            act.wait_ge(ss_done, n + 1)
                            nc.scalar.activation(rn[:], ss[:], ACT.Sqrt, bias=eps[:, 1:2]).then_inc(norm_sd, 1)
                            act.wait_ge(beta_scaled, n)
                            exps(n + 1, 1 - b)
            act.wait_ge(z_abs, 1)
            nc.scalar.activation(sm[:, 0], ba[:, 0:BLOCKS, :, 0:H].rearrange("p n t h -> p (n t) h"), ACT.Exp, scale=-1.0
                                 ).then_inc(exps_done, 1)
            nc.scalar.activation(sm[:, 2], sm[:, 1], ACT.Exp, scale=-1.0).then_inc(exps_done, 1)

        @block.vector
        def _(dve):
            dve.wait_ge(rate_exp, 1)
            nc.vector.tensor_scalar(neg_rate[:], neg_rate[:], -1.0, None, ALU.mult).then_inc(rate_neg, 1)
            dve.wait_ge(rate_neg, 1)

            def moments(n, b, k):
                dve.wait_ge(x_in[b], k * 16 + 16)
                for t in range(BLK):
                    nc.vector.bn_stats(stats[:, t, :], xin[b][:, t, :]).then_inc(stats_done, 1)
                dve.wait_ge(stats_done, n * BLK + BLK)
                dve.wait_ge(sd_done, n)
                nc.vector.sem_inc(stats_seen, 1)
                for t in range(BLK):
                    ag = nc.vector.bn_aggr(mv[:, t, :], stats[:, t, :])
                ag.then_inc(var_done, 1)

            def normalise(n, b):
                dve.wait_ge(sd_done, n + 1)
                nc.vector.reciprocal(rstd[:], rstd[:]).then_inc(rstd_done, 1)
                dve.wait_ge(rstd_done, n + 1)
                for t in range(BLK):
                    xn = nc.vector.tensor_scalar(xin[b][:, t, :], xin[b][:, t, :], mv[:, t, 0:1],
                                                 rstd[:, t:t + 1], ALU.subtract, ALU.mult)
                xn.then_inc(xn_done, 1)

            def beta_out(n, b):
                dve.wait_ge(beta_exp, n + 1)
                kept = ba[:, n] if isinstance(n, int) else ba[:, bass.ds(n, 1)]
                logit = ps_ba[:, 0:BLK * 2 * H].rearrange("p (t h) -> p t h", t=BLK)
                nc.vector.tensor_copy(kept, logit if isinstance(n, int) else logit.unsqueeze(1)).then_inc(ba_sb, 1)
                nc.vector.tensor_scalar(beta[b][:], beta[b][:], 1.0, None, ALU.add).then_inc(soft, 1)
                dve.wait_ge(soft, n + 1)
                nc.vector.reciprocal(beta[b][:], beta[b][:]).then_inc(beta_done, 1)

            def gates_out():
                step = [BLOCKS + 1]

                def link(ins):
                    step[0] += 1
                    ins.then_inc(soft, 1)
                    dve.wait_ge(soft, step[0])

                every = ba[:, 0:BLOCKS].rearrange("p n t h -> p (n t) h")
                dve.wait_ge(ba_sb, BLOCKS + 1)
                link(nc.vector.tensor_tensor(sm[:, 3], every[:, :, H:2 * H],
                                             head_row[:, 1:2, :].broadcast_to([P, TILES, H]), ALU.add))
                nc.vector.scalar_tensor_tensor(sm[:, 1], sm[:, 3], -1.0, sm[:, 3], ALU.mult, ALU.max
                                               ).then_inc(z_abs, 1)
                dve.wait_ge(exps_done, 2)
                link(nc.vector.tensor_scalar(sm[:, 0], sm[:, 0], 1.0, None, ALU.add))
                nc.vector.reciprocal(gb[:, :, H:2 * H], sm[:, 0]).then_inc(gb_done, 1)
                link(nc.vector.tensor_scalar(sm[:, 4], sm[:, 2], 2.0, None, ALU.add))
                link(nc.vector.reciprocal(sm[:, 4], sm[:, 4]))
                link(nc.vector.tensor_tensor(sm[:, 4], sm[:, 4], sm[:, 2], ALU.mult))
                link(nc.vector.tensor_tensor(sm[:, 5], sm[:, 4], sm[:, 4], ALU.mult))
                link(nc.vector.tensor_scalar(sm[:, 2], sm[:, 5], 2.0 / 15, None, ALU.mult))
                for c in (13, 11, 9, 7, 5, 3):
                    link(nc.vector.scalar_tensor_tensor(sm[:, 2], sm[:, 2], 2.0 / c, sm[:, 5], ALU.add, ALU.mult))
                link(nc.vector.scalar_tensor_tensor(sm[:, 2], sm[:, 2], 2.0, sm[:, 4], ALU.add, ALU.mult))
                link(nc.vector.scalar_tensor_tensor(sm[:, 2], sm[:, 3], 0.0, sm[:, 2], ALU.max, ALU.add))
                link(nc.vector.tensor_tensor(sm[:, 2], sm[:, 2],
                                             neg_rate[:].unsqueeze(1).broadcast_to([P, TILES, H]), ALU.mult))
                nc.vector.tensor_scalar(gb[:, :, 0:H], sm[:, 2], DECAY_FLOOR, None, ALU.max
                                        ).then_inc(gb_done, 1)

            for b in range(2):
                moments(b, b, 0)
                normalise(b, b)
            beta_out(0, 0)
            with dve.Fori(0, BLOCKS // 2) as i:
                for b in range(2):
                    n = i * 2 + b
                    if b:
                        dve.wait_ge(hist_set, i + 1)
                    for m in range(NCT):
                        dve.wait_ge(proj_taken[m % 2], n * (NCT // 2) + m // 2 + 1)
                        for k in range(TAPS - 1):
                            if k:
                                dve.wait_ge(conv_step, (n * NCT + m) * (TAPS - 2) + k)
                            y = nc.vector.scalar_tensor_tensor(conv_y[m % 4][:], conv_in[b][:, m, k:k + BT],
                                                               taps[:, m, k:k + 1], conv_y[m % 4][:],
                                                               ALU.mult, ALU.add)
                            y.then_inc(conv_step if k < TAPS - 2 else conv_done, 1)
                        if m == 3:
                            moments(n + 2, b, i + 1)
                    dve.wait_ge(sq_done, n * 2 + 2)
                    dve.wait_ge(scaled, n)
                    nc.vector.tensor_reduce(ss[:], sq[:].rearrange("p t (h d) -> p t h d", d=HK), AX_X,
                                            ALU.add).then_inc(ss_done, 1)
                    dve.wait_ge(norm_sd, n + 1)
                    nc.vector.reciprocal(rn[:], rn[:]).then_inc(norm_r, 1)
                    dve.wait_ge(norm_r, n * 2 + 1)
                    nc.vector.tensor_scalar(rn[:, :, 0:H], rn[:, :, 0:H], HK ** -0.5, None, ALU.mult
                                            ).then_inc(norm_r, 1)
                    normalise(n + 2, b)
                    beta_out(n + 1, 1 - b)
            gates_out()




def delta_stage(nc, a, s):
    with ExitStack() as ctx:
        sb = lambda n, shape: ctx.enter_context(nc.sbuf_tensor(n, shape, F32))
        bank = lambda n: ctx.enter_context(nc.psum_tensor(n, [P, 512], F32))
        sem = ctx.enter_context(stage_semaphores(nc))
        G = range(BATCH)
        per = lambda n, shape: [sb(f"{n}{b}", shape) for b in G]

        con = sb("con2", [P, C_N])
        w_o = sb("w_o", [P, H, D])
        norm_w = sb("norm_w", [P, 1])
        eps = sb("eps2", [P, 1])
        qk = per("qk", [P, 2 * DK])
        vb = per("vb", [P, DV])
        gt = per("gt", [P, DV])
        gbt = per("gbt", [P, 2 * H])
        xr = per("xr", [P, D])
        gam = per("gam", [P, 3 * H])
        gC2 = per("gC2", [P, 2])
        nbg = per("nbg", [P, H])
        g_gt = per("g_gt", [P, H, P])
        E = per("E", [P, H, P])
        Em = per("Em", [P, H, P])
        Eb = per("Eb", [P, H, P])
        qg = per("qg", [P, DK])
        ke = per("ke", [P, DK])
        qkT = per("qkT", [P, 4, P])
        qgT = per("qgT", [P, 2, P])
        PT = per("PT", [P, H, P])
        Y = per("Y", [P, H, P])
        bb = per("bb", [P, H, P])
        u = per("u", [P, H, P])
        S = per("S", [P, 2, HV])
        ssum = per("ssum", [P, H])
        stats = per("stats2_", [P, 6])
        mv = per("mv2_", [P, 2])
        rstd = per("rstd2_", [P, 1])
        x1t = per("x1t", [P, D])
        X, Qs, Pm, Am, og, ogT = g_gt, E, Em, Eb, bb, u

        A = [bank(f"psA{b}") for b in G]
        B = [bank(f"psB{b}") for b in G]

        weights_in = sem("weights_in2")
        qk_in = [sem(f"qk_in{b}") for b in G]
        v_in = [sem(f"v_in{b}") for b in G]
        gx_in = [sem(f"gx_in{b}") for b in G]
        x1_out = [sem(f"x1_out{b}") for b in G]
        names = ("set_up g_gt_done cum_done gam_done D_done E_done Em_done Eb_done nbg_done qg_done ke_done "
                 "qkT_done qkT_sb qgT_done qgT_sb kkqk_done am_done pm_done x0_half x0_done pT_done pT_sb y0_done "
                 "y0_sb lev_q lev_qs lev_y lev_ys lev_x lev_xs ks_done bb_done u_done u_sb o_done s_done "
                 "sq_done rs_sd rs_done og_done ogT_done ogT_sb wo_done y_done st_done st_seen mv_done sd_done "
                 "r_done x1_done").split()
        (set_up, g_gt_done, cum_done, gam_done, D_done, E_done, Em_done, Eb_done, nbg_done, qg_done, ke_done,
         qkT_done, qkT_sb, qgT_done, qgT_sb, kkqk_done, am_done, pm_done, x0_half, x0_done, pT_done, pT_sb, y0_done,
         y0_sb, lev_q, lev_qs, lev_y, lev_ys, lev_x, lev_xs, ks_done, bb_done, u_done, u_sb, o_done, s_done,
         sq_done, rs_sd, rs_done, og_done, ogT_done, ogT_sb, wo_done, y_done, st_done, st_seen, mv_done, sd_done,
         r_done, x1_done) = [sem(f"d_{n}") for n in names]

        block = ctx.enter_context(nc.Block())
        MERGES = range(1, LEVELS)
        NL = LEVELS - 1
        head = lambda slot: 2 * (slot % 2) + slot // 2
        ident = con[:, C_ID:C_ID + P]
        rows = lambda slot: slice(HK * (slot // 2), HK * (slot // 2) + HK)
        by_slot = lambda t: t.rearrange("p (t r) -> p r t", r=2)
        mask4 = lambda lo: con[:, lo:lo + P].unsqueeze(1).broadcast_to([P, H, P])
        HP = P // 2
        right = lambda t, lev: t[:].rearrange("p k (m w j) -> p k m w j", w=2, j=2 ** lev)[:, :, :, 1, :]
        split = lambda t: t[:].rearrange("p (r t) j -> p r t j", r=2)

        @block.sync
        def _(sp):
            sp.dma_start(con[:], a["consts"]).then_inc(weights_in, 16)
            sp.dma_start(w_o[:], a["L0_attn_Wo"].rearrange("(h p) n -> p h n", p=P)).then_inc(weights_in, 16)
            sp.dma_start(norm_w[:], a["L0_attn_norm_w"].rearrange("(p a) -> p a", a=1)).then_inc(weights_in, 16)
            for b in G:
                sp.dma_start(gbt[b][:], s["gb"][b * CHUNKS]).then_inc(qk_in[b], 16)
                sp.dma_start(qk[b][:], s["qkvg"][b * CHUNKS, :, 0:2 * DK]).then_inc(qk_in[b], 16)
            with sp.Fori(0, CHUNKS) as c:
                sp.wait_ge(bb_done, c * BATCH)
                for b in G:
                    sp.dma_start(vb[b][:], s["qkvg"][c + b * CHUNKS, :, 2 * DK:QKV]).then_inc(v_in[b], 16)
                sp.wait_ge(og_done, c * BATCH)
                sp.wait_ge(y_done, c * BATCH)
                for b in G:
                    sp.dma_start(gt[b][:], s["qkvg"][c + b * CHUNKS, :, QKV:QKV + DV]).then_inc(gx_in[b], 16)
                    sp.dma_start(xr[b][:], a["x"].rearrange("b (c p) d -> b c p d", p=P)[b, c]).then_inc(gx_in[b], 16)
                sp.wait_ge(Eb_done, (c + 1) * BATCH)
                sp.wait_ge(ke_done, (c + 1) * BATCH)
                sp.wait_ge(nbg_done, (c + 1) * BATCH)
                sp.wait_ge(qkT_done, (c + 1) * BATCH)
                for b in G:
                    sp.dma_start(gbt[b][:], s["gb"][(c + 1) % CHUNKS + b * CHUNKS]).then_inc(qk_in[b], 16)
                    sp.dma_start(qk[b][:], s["qkvg"][(c + 1) % CHUNKS + b * CHUNKS, :, 0:2 * DK]
                                 ).then_inc(qk_in[b], 16)

        @block.gpsimd
        def _(pool):
            nc.gpsimd.memset(eps[:], EPS).then_inc(set_up, 1)
            for b in G:
                nc.gpsimd.memset(S[b][:], 0.0).then_inc(set_up, 1)
            pool.wait_ge(weights_in, 48)

            def masked_decays(b, c):
                pool.wait_ge(qk_in[b], c * 32 + 32)
                pool.wait_ge(lev_y, c * NL * BATCH)
                nc.gpsimd.tensor_tensor(split(g_gt[b]),
                                        by_slot(gbt[b][:, 0:H]).unsqueeze(3).broadcast_to([P, 2, 2, P]),
                                        con[:, C_GT:C_GT + P].unsqueeze(1).unsqueeze(1).broadcast_to([P, 2, 2, P]),
                                        ALU.mult).then_inc(g_gt_done, 1)

            for b in G:
                masked_decays(b, 0)
            with pool.Fori(0, CHUNKS) as c:
                for b in G:
                    pool.wait_ge(gam_done, c * BATCH + b + 1)
                    pool.wait_ge(qgT_done, c * BATCH)
                    nc.gpsimd.tensor_tensor(qg[b][:].rearrange("p (h d) -> p h d", d=HK),
                                            qk[b][:, 0:DK].rearrange("p (h d) -> p h d", d=HK),
                                            gam[b][:, 0:H].unsqueeze(2).broadcast_to([P, H, HK]),
                                            ALU.mult).then_inc(qg_done, 1)
                for b in G:
                    pool.wait_ge(E_done, c * BATCH + b + 1)
                    pool.wait_ge(lev_q, c * NL * BATCH)
                    nc.gpsimd.tensor_tensor(split(Eb[b]), split(E[b]),
                                            by_slot(gbt[b][:, H:2 * H]).unsqueeze(3).broadcast_to([P, 2, 2, P]),
                                            ALU.mult).then_inc(Eb_done, 1)
                for b in G:
                    pool.wait_ge(am_done, c * BATCH + b + 1)
                    nc.gpsimd.tensor_tensor(X[b][:], Am[b][:], mask4(C_NM0), ALU.mult).then_inc(x0_half, 1)
                for b in G:
                    pool.wait_ge(o_done, c * BATCH)
                    nc.gpsimd.tensor_tensor(ke[b][:].rearrange("p (h d) -> p h d", d=HK),
                                            qk[b][:, DK:2 * DK].rearrange("p (h d) -> p h d", d=HK),
                                            gam[b][:, H:2 * H].unsqueeze(2).broadcast_to([P, H, HK]),
                                            ALU.mult).then_inc(ke_done, 1)
                for b in G:
                    masked_decays(b, c + 1)
                for b in G:
                    pool.wait_ge(x1_done, c * BATCH + b + 1)
                    pool.dma_start(s["x1"][c + b * CHUNKS], x1t[b][:]).then_inc(x1_out[b], 16)
            for b in G:
                pool.wait_ge(x1_out[b], 16 * CHUNKS)

        @block.tensor
        def _(pe):
            pe.wait_ge(weights_in, 48)
            pe.wait_ge(set_up, 1 + BATCH)

            def decay_sums(b, c):
                pe.wait_ge(g_gt_done, c * BATCH + b + 1)
                pe.wait_ge(ogT_sb, (c - 1) * BATCH + b + 1) if not isinstance(c, int) else None
                pe.matmul(A[b][:], con[:, C_LE:C_LE + P], g_gt[b][:], start=True, stop=True).then_inc(D_done, 1)

            for b in G:
                decay_sums(b, 0)
            with pe.Fori(0, CHUNKS) as c:
                at = lambda b: c * BATCH + b + 1
                for b in G:
                    pe.wait_ge(qk_in[b], c * 32 + 32)
                    pe.wait_ge(y_done, c * BATCH)
                    for k, lo in enumerate((C_LE, C_GT, C_ONE)):
                        mm = pe.matmul(B[b][:, k * H:(k + 1) * H], con[:, lo:lo + P], gbt[b][:, 0:H],
                                       start=True, stop=True)
                    mm.then_inc(cum_done, 1)
                for b in G:
                    pe.wait_ge(gam_done, at(b))
                    for k in range(4):
                        mm = pe.transpose(B[b][:, k * P:(k + 1) * P], qk[b][:, k * P:(k + 1) * P], ident)
                    mm.then_inc(qkT_done, 1)
                for b in G:
                    pe.wait_ge(E_done, at(b))
                    pe.wait_ge(qg_done, at(b))
                    for k in range(2):
                        mm = pe.transpose(A[b][:, k * P:(k + 1) * P], qg[b][:, k * P:(k + 1) * P], ident)
                    mm.then_inc(qgT_done, 1)
                for b in G:
                    pe.wait_ge(qkT_sb, at(b))
                    pe.wait_ge(qgT_sb, at(b))
                    for w in (2, 0):
                        for t in range(2):
                            for r, bk in enumerate((A[b], B[b])):
                                lo = (t if w else 2 + t) * P
                                mm = pe.matmul(bk[:, lo:lo + P], qkT[b][rows(2 * r), w + t, :],
                                               qkT[b][rows(2 * r), 2 + t, :], start=True, stop=True)
                    mm.then_inc(kkqk_done, 1)
                for b in G:
                    pe.wait_ge(pm_done, at(b))
                    for k in range(H):
                        mm = pe.transpose(B[b][:, k * P:(k + 1) * P], Pm[b][:, k, :], ident)
                    mm.then_inc(pT_done, 1)
                for b in G:
                    pe.wait_ge(x0_done, at(b))
                    for k in range(H):
                        mm = pe.transpose(A[b][:, k * P:(k + 1) * P], X[b][:, k, :], ident)
                    mm.then_inc(y0_done, 1)
                for lev in MERGES:
                    lat = lambda b, lev=lev: (c * NL + (lev - 1)) * BATCH + b + 1
                    for b in G:
                        if lev == 1:
                            pe.wait_ge(y0_sb, at(b))
                        else:
                            pe.wait_ge(lev_ys, lat(b) - BATCH)
                            pe.wait_ge(lev_xs, (c * (NL - 1) + (lev - 2)) * BATCH + b + 1)
                        for k in range(H):
                            mm = pe.matmul(A[b][:, k * HP:(k + 1) * HP], Am[b][:, k, :], right(Y[b], lev)[:, k],
                                           start=True, stop=True)
                        mm.then_inc(lev_q, 1)
                    for b in G:
                        pe.wait_ge(lev_qs, lat(b))
                        if lev == 1:
                            pe.wait_ge(pT_sb, at(b))
                        for k in range(H):
                            mm = pe.matmul(B[b][:, k * HP:(k + 1) * HP], X[b][:, k, :], Qs[b][:, k, 0:HP],
                                           start=True, stop=True)
                        mm.then_inc(lev_y, 1)
                    if lev < NL:
                        for b in G:
                            pe.wait_ge(lev_ys, lat(b))
                            for k in range(H):
                                mm = pe.transpose(A[b][:, k * P:(k + 1) * P], Y[b][:, k, :], ident)
                            mm.then_inc(lev_x, 1)
                for b in G:
                    pe.wait_ge(lev_ys, (c + 1) * NL * BATCH - BATCH + b + 1)
                    pe.wait_ge(s_done, c * BATCH)
                    for t in range(2):
                        for r, bk in enumerate((A[b], B[b])):
                            mm = pe.matmul(bk[:, t * P:(t + 1) * P], qkT[b][rows(2 * r), 2 + t, :],
                                           S[b][rows(2 * r), t, :], start=True, stop=True)
                    mm.then_inc(ks_done, 1)
                for b in G:
                    pe.wait_ge(bb_done, at(b))
                    for k in range(H):
                        mm = pe.matmul(A[b][:, k * P:(k + 1) * P], Y[b][:, k, :], bb[b][:, k, :],
                                       start=True, stop=True)
                    mm.then_inc(u_done, 1)
                for b in G:
                    pe.wait_ge(u_sb, at(b))
                    pe.wait_ge(ke_done, at(b))
                    for t in range(2):
                        for r, bk in enumerate((A[b], B[b])):
                            pe.matmul(bk[:, t * P:(t + 1) * P], qgT[b][rows(2 * r), t, :],
                                      S[b][rows(2 * r), t, :], start=True, stop=False)
                            pe.matmul(bk[:, t * P:(t + 1) * P], PT[b][:, 2 * r + t, :], u[b][:, 2 * r + t, :],
                                      start=False, stop=True)
                    for t in range(2):
                        for r in range(2):
                            h = 2 * t + r
                            mm = pe.matmul(B[b][rows(2 * r), 2 * P + t * P:2 * P + (t + 1) * P],
                                           ke[b][:, h * HK:(h + 1) * HK], u[b][:, 2 * r + t, :],
                                           start=True, stop=True)
                    mm.then_inc(o_done, 1)
                for b in G:
                    pe.wait_ge(og_done, at(b))
                    for k in range(H):
                        mm = pe.transpose(A[b][:, k * P:(k + 1) * P], og[b][:, k, :], ident)
                    mm.then_inc(ogT_done, 1)
                for b in G:
                    pe.wait_ge(ogT_sb, at(b))
                    for k in range(H):
                        mm = pe.matmul(B[b][:, 0:D], ogT[b][:, k, :], w_o[:, head(k), :],
                                       start=k == 0, stop=k == H - 1)
                    mm.then_inc(wo_done, 1)
                    decay_sums(b, c + 1)

        @block.scalar
        def _(act):
            act.wait_ge(weights_in, 48)
            act.wait_ge(set_up, 1 + BATCH)
            with act.Fori(0, CHUNKS) as c:
                at = lambda b: c * BATCH + b + 1
                flat = lambda t: t[:].rearrange("p k j -> p (k j)")
                for b in G:
                    act.wait_ge(cum_done, at(b))
                    act.wait_ge(ke_done, c * BATCH)
                    act.wait_ge(s_done, c * BATCH)
                    nc.scalar.activation(gam[b][:], B[b][:, 0:3 * H], ACT.Exp)
                    tot = B[b][:, 2 * H:3 * H].rearrange("p (t r) -> p r t", r=2)
                    for r in range(2):
                        e = nc.scalar.activation(gC2[b][rows(2 * r), :], tot[rows(2 * r), r, :], ACT.Exp)
                    e.then_inc(gam_done, 1)
                for b in G:
                    act.wait_ge(D_done, at(b))
                    nc.scalar.activation(flat(E[b]), A[b][:], ACT.Exp).then_inc(E_done, 1)
                for b in G:
                    act.wait_ge(qkT_done, at(b))
                    nc.scalar.activation(flat(qkT[b]), B[b][:], ACT.Copy).then_inc(qkT_sb, 1)
                for b in G:
                    act.wait_ge(qgT_done, at(b))
                    nc.scalar.activation(flat(qgT[b]), A[b][:, 0:2 * P], ACT.Copy).then_inc(qgT_sb, 1)
                for b in G:
                    act.wait_ge(pT_done, at(b))
                    nc.scalar.activation(flat(PT[b]), B[b][:], ACT.Copy).then_inc(pT_sb, 1)
                for b in G:
                    act.wait_ge(y0_done, at(b))
                    nc.scalar.activation(flat(Y[b]), A[b][:], ACT.Copy).then_inc(y0_sb, 1)
                for lev in range(1, NL):
                    for b in G:
                        act.wait_ge(lev_x, (c * (NL - 1) + (lev - 1)) * BATCH + b + 1)
                        nc.scalar.activation(flat(X[b]), A[b][:], ACT.Copy).then_inc(lev_xs, 1)
                for b in G:
                    act.wait_ge(u_done, at(b))
                    nc.scalar.activation(flat(u[b]), A[b][:], ACT.Copy).then_inc(u_sb, 1)
                for b in G:
                    act.wait_ge(o_done, at(b))
                    act.wait_ge(s_done, at(b))
                    for k in range(H):
                        bk = (A, B)[k // 2][b]
                        q = nc.scalar.activation(og[b][:, k, :], bk[:, (k % 2) * P:(k % 2 + 1) * P], ACT.Square,
                                                 accum_out=ssum[b][:, k:k + 1])
                    q.then_inc(sq_done, 1)
                for b in G:
                    act.wait_ge(sq_done, at(b))
                    nc.scalar.activation(ssum[b][:], ssum[b][:], ACT.Sqrt, bias=eps[:, 0:1], scale=1.0 / HV
                                         ).then_inc(rs_sd, 1)
                for b in G:
                    act.wait_ge(ogT_done, at(b))
                    nc.scalar.activation(flat(ogT[b]), A[b][:], ACT.Copy, scale=norm_w[:, 0:1]).then_inc(ogT_sb, 1)
                for b in G:
                    act.wait_ge(mv_done, at(b))
                    nc.scalar.activation(rstd[b][:], mv[b][:, 1:2], ACT.Sqrt, bias=eps[:, 0:1]).then_inc(sd_done, 1)

        @block.vector
        def _(dve):
            dve.wait_ge(weights_in, 48)
            with dve.Fori(0, CHUNKS) as c:
                at = lambda b: c * BATCH + b + 1
                for b in G:
                    dve.wait_ge(gam_done, at(b))
                    nc.vector.scalar_tensor_tensor(nbg[b][:], gam[b][:, 0:H], -1.0, gbt[b][:, H:2 * H],
                                                   ALU.mult, ALU.mult).then_inc(nbg_done, 1)
                for b in G:
                    dve.wait_ge(E_done, at(b))
                    dve.wait_ge(pT_done, c * BATCH)
                    nc.vector.tensor_tensor(Em[b][:], E[b][:], mask4(C_GE), ALU.mult).then_inc(Em_done, 1)
                for b in G:
                    dve.wait_ge(kkqk_done, at(b))
                    dve.wait_ge(Eb_done, at(b))
                    for r, bk in enumerate((A[b], B[b])):
                        m = nc.vector.tensor_tensor(Am[b][:, 2 * r:2 * r + 2, :],
                                                    bk[:, 0:2 * P].rearrange("p (t j) -> p t j", t=2),
                                                    Eb[b][:, 2 * r:2 * r + 2, :], ALU.mult)
                    m.then_inc(am_done, 1)
                    dve.wait_ge(Em_done, at(b))
                    for r, bk in enumerate((A[b], B[b])):
                        m = nc.vector.tensor_tensor(Pm[b][:, 2 * r:2 * r + 2, :],
                                                    bk[:, 2 * P:4 * P].rearrange("p (t j) -> p t j", t=2),
                                                    Em[b][:, 2 * r:2 * r + 2, :], ALU.mult)
                    m.then_inc(pm_done, 1)
                for b in G:
                    dve.wait_ge(x0_half, at(b))
                    nc.vector.tensor_tensor(X[b][:], X[b][:], mask4(C_ID), ALU.add).then_inc(x0_done, 1)
                for lev in MERGES:
                    lat = lambda b, lev=lev: (c * NL + (lev - 1)) * BATCH + b + 1
                    for b in G:
                        dve.wait_ge(lev_q, lat(b))
                        m = C_LEV + (lev - 1) * HP
                        nc.vector.tensor_tensor(Qs[b][:, :, 0:HP],
                                                A[b][:, 0:H * HP].rearrange("p (k j) -> p k j", k=H),
                                                con[:, m:m + HP].unsqueeze(1).broadcast_to([P, H, HP]), ALU.mult
                                                ).then_inc(lev_qs, 1)
                    for b in G:
                        dve.wait_ge(lev_y, lat(b))
                        y = right(Y[b], lev)
                        nc.vector.tensor_tensor(y, y, B[b][:, 0:H * HP].rearrange("p (k m j) -> p k m j", k=H,
                                                                                 j=2 ** lev),
                                                ALU.subtract).then_inc(lev_ys, 1)
                for b in G:
                    dve.wait_ge(ks_done, at(b))
                    dve.wait_ge(v_in[b], c * 16 + 16)
                    dve.wait_ge(ogT_done, c * BATCH)
                    dve.wait_ge(nbg_done, at(b))
                    for k in range(H):
                        bk, h = (A, B)[k // 2][b], head(k)
                        m = nc.vector.scalar_tensor_tensor(bb[b][:, k, :], bk[:, (k % 2) * P:(k % 2 + 1) * P],
                                                           nbg[b][:, h:h + 1], vb[b][:, h * HV:(h + 1) * HV],
                                                           ALU.mult, ALU.add)
                    m.then_inc(bb_done, 1)
                for b in G:
                    dve.wait_ge(o_done, at(b))
                    for t in range(2):
                        m = nc.vector.scalar_tensor_tensor(S[b][:, t, :], S[b][:, t, :], gC2[b][:, t:t + 1],
                                                           B[b][:, 2 * P + t * P:2 * P + (t + 1) * P],
                                                           ALU.mult, ALU.add)
                    m.then_inc(s_done, 1)
                for b in G:
                    dve.wait_ge(rs_sd, at(b))
                    nc.vector.reciprocal(ssum[b][:], ssum[b][:]).then_inc(rs_done, 1)
                for b in G:
                    dve.wait_ge(rs_done, at(b))
                    dve.wait_ge(gx_in[b], c * 32 + 32)
                    for k in range(H):
                        bk, h = (A, B)[k // 2][b], head(k)
                        m = nc.vector.scalar_tensor_tensor(og[b][:, k, :], bk[:, (k % 2) * P:(k % 2 + 1) * P],
                                                           ssum[b][:, k:k + 1], gt[b][:, h * HV:(h + 1) * HV],
                                                           ALU.mult, ALU.mult)
                    m.then_inc(og_done, 1)
                for b in G:
                    dve.wait_ge(wo_done, at(b))
                    dve.wait_ge(x1_out[b], c * 16)
                    nc.vector.scalar_tensor_tensor(x1t[b][:], xr[b][:], 2.0, B[b][:, 0:D], ALU.mult, ALU.add
                                                   ).then_inc(y_done, 1)
                for b in G:
                    dve.wait_ge(y_done, at(b))
                    nc.vector.bn_stats(stats[b][:], x1t[b][:]).then_inc(st_done, 1)
                for b in G:
                    dve.wait_ge(st_done, at(b))
                    nc.vector.sem_inc(st_seen, 1)
                    nc.vector.bn_aggr(mv[b][:], stats[b][:]).then_inc(mv_done, 1)
                for b in G:
                    dve.wait_ge(sd_done, at(b))
                    nc.vector.reciprocal(rstd[b][:], rstd[b][:]).then_inc(r_done, 1)
                for b in G:
                    dve.wait_ge(r_done, at(b))
                    nc.vector.tensor_scalar(x1t[b][:], x1t[b][:], mv[b][:, 0:1], rstd[b][:, 0:1],
                                            ALU.subtract, ALU.mult).then_inc(x1_done, 1)


def context_stage(nc, a, s):
    with ExitStack() as ctx:
        sb = lambda n, shape: ctx.enter_context(nc.sbuf_tensor(n, shape, F32))
        bank = lambda n: ctx.enter_context(nc.psum_tensor(n, [P, 512], F32))
        sem = ctx.enter_context(stage_semaphores(nc))
        XJ = XW // P
        con = sb("con3", [P, C_N])
        w_k = sb("xw_k", [P, KD, XW])
        w_v = sb("xw_v", [P, KD, XW])
        nw = sb("xnw", [P, 2])
        eps = sb("eps3", [P, 1])
        cx = sb("cx", [P, D])
        cxT = sb("cxT", [P, KD, CTX])
        k_sb = sb("k_sb", [P, XW])
        k_sq = sb("k_sq", [P, XW])
        v_sb = sb("v_sb", [P, XW])
        ss = sb("ss3", [P, XH])
        kT = sb("kT3", [P, XJ, KC])
        ctx_len = ctx.enter_context(nc.sbuf_tensor("ctx_len", [P, 1], I32))
        len_f = sb("len_f", [P, 1])
        valid = sb("valid", [P, 1])
        madd = sb("madd3", [P, CTX])
        ps_c = bank("ps_c")
        ps_k = [bank(f"ps_k{h}") for h in range(2)]
        ps_v = [bank(f"ps_v{h}") for h in range(2)]
        ps_kT = [bank(f"ps_kT{h}") for h in range(2)]
        (weights_in, ctx_in, set_up, nw_done, cxT_done, cxT_sb, k_done, v_done, k_out, sq_done, ss_done, sd_done,
         r_done, rm_done, len_done, valid_done, m_half, madd_done, k_scaled, kT_done, kT_sb, v_sb_done, stored) = [
            sem(f"c_{n}") for n in
            ("weights_in ctx_in set_up nw_done cxT_done cxT_sb k_done v_done k_out sq_done ss_done sd_done r_done "
             "rm_done len_done valid_done m_half madd_done k_scaled kT_done kT_sb v_sb_done stored").split()]
        block = ctx.enter_context(nc.Block())
        ident = con[:, C_ID:C_ID + P]

        @block.sync
        def _(sp):
            sp.dma_start(con[:], a["consts"]).then_inc(weights_in, 16)
            sp.dma_start(w_k[:], a["L0_xattn_Wk"].rearrange("(k p) n -> p k n", p=P)).then_inc(weights_in, 16)
            sp.dma_start(w_v[:], a["L0_xattn_Wv"].rearrange("(k p) n -> p k n", p=P)).then_inc(weights_in, 16)
            for k, w in enumerate((a["L0_xattn_q_norm_w"], a["L0_xattn_k_norm_w"])):
                for r in range(2):
                    sp.dma_start(nw[r * XD:(r + 1) * XD, k:k + 1], w.rearrange("(p a) -> p a", a=1)
                                 ).then_inc(weights_in, 16)
            with sp.Fori(0, BATCH) as b:
                sp.wait_ge(cxT_done, b)
                sp.wait_ge(len_done, b)
                sp.dma_start(cx[0:CTX, :], a["ctx_1024"][b]).then_inc(ctx_in, 16)
                sp.dma_start(ctx_len[:], a["_lenS2"].rearrange("(b a) -> b a", a=1)[bass.ds(b, 1), :]
                             .broadcast_to([P, 1])).then_inc(ctx_in, 16)
                sp.wait_ge(kT_sb, 2 * b + 2)
                sp.dma_start(s["kT"][b], kT[:]).then_inc(stored, 16)
                sp.wait_ge(v_sb_done, 2 * b + 2)
                sp.dma_start(s["v"][b], v_sb[0:CTX, :]).then_inc(stored, 16)
                sp.wait_ge(madd_done, b + 1)
                sp.dma_start(s["madd"][b], madd[:]).then_inc(stored, 16)
            sp.wait_ge(stored, 48 * BATCH)

        @block.gpsimd
        def _(pool):
            nc.gpsimd.memset(eps[:], EPS).then_inc(set_up, 1)
            nc.gpsimd.memset(kT[:, :, CTX:KC], 0.0).then_inc(set_up, 1)

        @block.tensor
        def _(pe):
            pe.wait_ge(weights_in, 16 * 7)
            with pe.Fori(0, BATCH) as b:
                pe.wait_ge(ctx_in, b * 32 + 32)
                pe.wait_ge(cxT_sb, b)
                for c in range(KD):
                    mm = pe.transpose(ps_c[:, c * P:c * P + CTX], cx[0:CTX, c * P:(c + 1) * P],
                                      con[0:CTX, C_ID:C_ID + CTX])
                mm.then_inc(cxT_done, 1)
                pe.wait_ge(cxT_sb, b + 1)
                pe.wait_ge(k_out, 2 * b)
                for h in range(2):
                    for c in range(KD):
                        mm = pe.matmul(ps_k[h][0:CTX, :], cxT[:, c, :], w_k[:, c, h * 512:(h + 1) * 512],
                                       start=c == 0, stop=c == KD - 1)
                mm.then_inc(k_done, 1)
                pe.wait_ge(v_sb_done, 2 * b)
                for h in range(2):
                    for c in range(KD):
                        mm = pe.matmul(ps_v[h][0:CTX, :], cxT[:, c, :], w_v[:, c, h * 512:(h + 1) * 512],
                                       start=c == 0, stop=c == KD - 1)
                mm.then_inc(v_done, 1)
                pe.wait_ge(k_scaled, b + 1)
                pe.wait_ge(kT_sb, 2 * b)
                for j in range(XJ):
                    mm = pe.transpose(ps_kT[j // 4][:, (j % 4) * P:(j % 4) * P + CTX],
                                      k_sb[0:CTX, j * P:(j + 1) * P], con[0:CTX, C_ID:C_ID + CTX])
                mm.then_inc(kT_done, 1)

        @block.scalar
        def _(act):
            act.wait_ge(set_up, 2)
            act.wait_ge(nw_done, 1)
            with act.Fori(0, BATCH) as b:
                act.wait_ge(cxT_done, b + 1)
                act.wait_ge(v_done, b)
                nc.scalar.activation(cxT[:], ps_c[:, 0:KD * P].rearrange("p (c j) -> p c j", c=KD)[:, :, 0:CTX],
                                     ACT.Copy).then_inc(cxT_sb, 1)
                act.wait_ge(k_done, b + 1)
                act.wait_ge(kT_done, b)
                act.wait_ge(ss_done, b)
                for h in range(2):
                    nc.scalar.activation(k_sb[0:CTX, h * 512:(h + 1) * 512], ps_k[h][0:CTX, :], ACT.Copy
                                         ).then_inc(k_out, 1)
                act.wait_ge(k_out, 2 * b + 2)
                nc.scalar.activation(k_sq[0:CTX, :], k_sb[0:CTX, :], ACT.Square).then_inc(sq_done, 1)
                act.wait_ge(v_done, b + 1)
                act.wait_ge(stored, b * 48)
                for h in range(2):
                    nc.scalar.activation(v_sb[0:CTX, h * 512:(h + 1) * 512], ps_v[h][0:CTX, :], ACT.Copy
                                         ).then_inc(v_sb_done, 1)
                act.wait_ge(ss_done, b + 1)
                nc.scalar.activation(ss[0:CTX, :], ss[0:CTX, :], ACT.Sqrt, bias=eps[0:CTX, 0:1], scale=1.0 / XD
                                     ).then_inc(sd_done, 1)
                act.wait_ge(kT_done, b + 1)
                for h in range(2):
                    nc.scalar.activation(kT[:, 4 * h:4 * h + 4, 0:CTX],
                                         ps_kT[h][:].rearrange("p (c j) -> p c j", c=4)[:, :, 0:CTX],
                                         ACT.Copy, scale=nw[:, 0:1]).then_inc(kT_sb, 1)

        @block.vector
        def _(dve):
            dve.wait_ge(weights_in, 16 * 7)
            nc.vector.tensor_tensor(nw[:, 0:1], nw[:, 0:1], nw[:, 1:2], ALU.mult).then_inc(nw_done, 1)
            with dve.Fori(0, BATCH) as b:
                dve.wait_ge(ctx_in, b * 32 + 32)
                nc.vector.tensor_scalar(len_f[:], ctx_len[:], 1.0, None, ALU.mult).then_inc(len_done, 1)
                dve.wait_ge(len_done, b + 1)
                nc.vector.tensor_tensor(valid[:], con[:, C_COL:C_COL + 1], len_f[:], ALU.is_lt
                                        ).then_inc(valid_done, 1)
                dve.wait_ge(stored, b * 48)
                nc.vector.tensor_scalar(madd[:], con[:, C_IOTA:C_IOTA + CTX], len_f[:, 0:1], None, ALU.is_lt
                                        ).then_inc(m_half, 1)
                dve.wait_ge(m_half, b + 1)
                nc.vector.tensor_scalar(madd[:], madd[:], -1.0, 1e30, ALU.add, ALU.mult).then_inc(madd_done, 1)
                dve.wait_ge(sq_done, b + 1)
                dve.wait_ge(k_scaled, b)
                nc.vector.tensor_reduce(ss[0:CTX, :], k_sq[0:CTX, :].rearrange("p (h d) -> p h d", d=XD), AX_X,
                                        ALU.add).then_inc(ss_done, 1)
                dve.wait_ge(sd_done, b + 1)
                nc.vector.reciprocal(ss[0:CTX, :], ss[0:CTX, :]).then_inc(r_done, 1)
                dve.wait_ge(r_done, b + 1)
                dve.wait_ge(valid_done, b + 1)
                nc.vector.tensor_scalar(ss[0:CTX, :], ss[0:CTX, :], valid[0:CTX, 0:1], None, ALU.mult
                                        ).then_inc(rm_done, 1)
                dve.wait_ge(rm_done, b + 1)
                v = k_sb[0:CTX, :].rearrange("p (h d) -> p h d", d=XD)
                nc.vector.tensor_tensor(v, v, ss[0:CTX, :].unsqueeze(2).broadcast_to([CTX, XH, XD]), ALU.mult
                                        ).then_inc(k_scaled, 1)


def cross_stage(nc, a, s):
    with ExitStack() as ctx:
        sb = lambda n, shape: ctx.enter_context(nc.sbuf_tensor(n, shape, F32))
        bank = lambda n: ctx.enter_context(nc.psum_tensor(n, [P, 512], F32))
        sem = ctx.enter_context(stage_semaphores(nc))
        T, R, W = range(BLK), range(2), range(BLK // 2)
        XJ = XW // P
        two = lambda n, shape: [sb(f"{n}{k}", shape) for k in R]
        x1_v = s["x1"].rearrange("(n t) p d -> n p t d", t=BLK)
        x2_v = s["x2"].rearrange("(n t) p d -> n p t d", t=BLK)
        lg_v = s["lg"].rearrange("(n t) p e -> n p t e", t=BLK)
        con = sb("con4", [P, C_N])
        w_q = sb("xw_q", [P, KD, XW])
        w_o = sb("xw_o", [P, XJ, D])
        w_r = sb("w_r", [P, KD, NE])
        zeros = sb("zeros4", [P, D])
        eps = sb("eps4", [P, 2])
        xq = sb("xq", [P, BLK, D])
        xr = sb("xr4", [P, BLK, D])
        kT = sb("kT4", [P, XJ, KC])
        v = sb("v4", [P, XW])
        madd = sb("madd4", [P, CTX])
        x1T = sb("x1T", [P, KD, BT])
        qT = two("qT", [P, XJ, BT])
        q2 = two("q2_", [P, BT])
        ss = sb("ss4", [XH, BT])
        rq = sb("rq", [P, XH, BLK])
        sc = two("sc", [P, 2, BLK, CTX])
        mx = two("mx", [P, 2, BLK])
        nb = two("nb", [P, 2, BLK])
        den = two("den", [P, 2, BLK])
        aT = two("aT", [P, 2, BT])
        oT = sb("oT", [P, XJ, BT])
        x2t = sb("x2t", [P, BLK, D])
        x2T = sb("x2T", [P, BLK, KD, P])
        lg = sb("lg4", [P, BLK, NE])
        stats = sb("stats4", [P, BLK, 6])
        mv = sb("mv4", [P, BLK, 2])
        rstd = sb("rstd4", [P, BLK])
        S = [bank(f"xS{r}") for r in R]
        TB = [bank(f"xT{r}") for r in R]
        V, Q, SS, X = bank("xV"), bank("xQ"), bank("xSS"), bank("xX")
        weights_in = sem("x_weights_in")
        q2_done = [sem(f"x_q2_done{k}") for k in R]
        ss_done = [sem(f"x_ss_done{k}") for k in R]
        names = ("set_up xq_in xr_in kv_in zero_out x2_out lg_out x1T_done x1T_sb q_done q_sb ss_sb ss_seen ssT_done "
                 "rq_done sc_done added mx_done nb_done exp_done den_done scaled tr_done tr_a tr_b pv_done o_sb "
                 "wo_done y_done st_done st_seen mv_done sd_done r_done x2_done x2T_done x2T_sb lg_done lg_sb").split()
        (set_up, xq_in, xr_in, kv_in, zero_out, x2_out, lg_out, x1T_done, x1T_sb, q_done, q_sb, ss_sb, ss_seen, ssT_done,
         rq_done, sc_done, added, mx_done, nb_done, exp_done, den_done, scaled, tr_done, tr_a, tr_b, pv_done, o_sb,
         wo_done, y_done, st_done, st_seen, mv_done, sd_done, r_done, x2_done, x2T_done, x2T_sb, lg_done, lg_sb) = [
            sem(f"x_{n}") for n in names]
        block = ctx.enter_context(nc.Block())
        ident = con[:, C_ID:C_ID + P]
        HX = XJ // 2
        X2T_STEP, LG_STEP = 2, 5

        def blocks(eng, turn):
            turn(0, 0, 0, True, False)
            with eng.Fori(0, BATCH - 1) as i:
                turn(i * 2 + 1, i, 1, False, False)
                turn(i * 2 + 2, i + 1, 0, False, False)
            turn(BLOCKS - 1, BATCH - 1, 1, False, True)

        @block.sync
        def _(sp):
            sp.dma_start(xq[:], x1_v[0]).then_inc(xq_in, 16)
            sp.dma_start(con[:], a["consts"]).then_inc(weights_in, 16)
            sp.dma_start(w_q[:], a["L0_xattn_Wq"].rearrange("(k p) n -> p k n", p=P)).then_inc(weights_in, 16)
            sp.dma_start(w_o[:], a["L0_xattn_Wo"].rearrange("(k p) n -> p k n", p=P)).then_inc(weights_in, 16)
            for c in range(KD):
                sp.dma_start(w_r[:, c, :], a["L0_ffn_router_w"].rearrange("e (k p) -> p k e", p=P)[:, c, :],
                             allow_slow_non_contiguous=True).then_inc(weights_in, 16)

            def load_kv(i):
                sp.dma_start(kT[:], s["kT"][i]).then_inc(kv_in, 16)
                sp.dma_start(v[0:CTX, :], s["v"][i]).then_inc(kv_in, 16)
                sp.dma_start(madd[:], s["madd"][i]).then_inc(kv_in, 16)

            load_kv(0)
            sp.wait_ge(set_up, 3)
            sp.dma_start(s["xs"].rearrange("t p d -> p t d"), zeros[:].unsqueeze(1).broadcast_to([P, FT + 1, D])
                         ).then_inc(zero_out, 16)
            sp.wait_ge(x1T_done, 1)
            sp.dma_start(xq[:], x1_v[1]).then_inc(xq_in, 16)

            def store(n):
                sp.wait_ge(x2_done, n + 1)
                sp.dma_start(x2_v[n], x2t[:]).then_inc(x2_out, 16)
                sp.wait_ge(lg_sb, n + 1)
                sp.dma_start(lg_v[n], lg[:]).then_inc(lg_out, 16)

            def turn(n, i, half, first, last):
                sp.wait_ge(y_done, n * 2)
                sp.dma_start(xr[:], x1_v[n]).then_inc(xr_in, 16)
                if not last:
                    sp.wait_ge(x1T_done, n + 2)
                    sp.dma_start(xq[:], x1_v[(n + 2) % BLOCKS]).then_inc(xq_in, 16)
                if not first:
                    store(n - 1)
                if half == 1 and not last:
                    sp.wait_ge(pv_done, (n + 1) * XJ)
                    load_kv(i + 1)

            blocks(sp, turn)
            store(BLOCKS - 1)
            sp.wait_ge(zero_out, 16)
            sp.wait_ge(xq_in, 16 * (BLOCKS + 1))
            sp.wait_ge(x2_out, 16 * BLOCKS)
            sp.wait_ge(lg_out, 16 * BLOCKS)

        @block.gpsimd
        def _(pool):
            nc.gpsimd.memset(eps[:, 0:1], EPS).then_inc(set_up, 1)
            nc.gpsimd.memset(eps[:, 1:2], XD * EPS).then_inc(set_up, 1)
            nc.gpsimd.memset(zeros[:], 0.0).then_inc(set_up, 1)

            def squares(m, b):
                for j in range(XJ):
                    pool.wait_ge(q_sb, m * XJ + j + 1)
                    pool.wait_ge(ss_done[j % 2], m * HX + j // 2)
                    nc.gpsimd.tensor_tensor(q2[j % 2][:], qT[b][:, j, :], qT[b][:, j, :], ALU.mult
                                            ).then_inc(q2_done[j % 2], 1)

            def turn(n, i, half, first, last):
                if not last:
                    squares(n + 1, 1 - half)

            squares(0, 0)
            blocks(pool, turn)

        @block.tensor
        def _(pe):
            pe.wait_ge(weights_in, 16 * 5)

            def x1_turned(m, first):
                pe.wait_ge(xq_in, m * 16 + 16)
                if not first:
                    pe.wait_ge(q_sb, m * XJ)
                    pe.wait_ge(rq_done, m)
                for c in range(KD):
                    for t in T:
                        mm = pe.transpose((Q, X)[c][:, t * P:(t + 1) * P], xq[:, t, c * P:(c + 1) * P], ident)
                mm.then_inc(x1T_done, 1)

            def queries(m, j):
                if j == 0:
                    pe.wait_ge(x1T_sb, m * KD + KD)
                pe.wait_ge(q_sb, m * XJ + j)
                for c in range(KD):
                    mm = pe.matmul(Q[:], w_q[:, c, j * P:(j + 1) * P], x1T[:, c, :], start=c == 0, stop=c == KD - 1)
                mm.then_inc(q_done, 1)

            def square_sums(m, j):
                pe.wait_ge(q2_done[j % 2], m * HX + j // 2 + 1)
                if j == 0:
                    pe.wait_ge(ss_sb, m)
                pe.matmul(SS[0:XH, :], con[:, C_HEAD + j * XH:C_HEAD + (j + 1) * XH], q2[j % 2][:], start=j == 0,
                          stop=j == XJ - 1).then_inc(ss_done[j % 2], 1)

            def sums_turned(m):
                pe.wait_ge(ss_sb, m + 1)
                nc.tensor.sem_inc(ss_seen, 1)
                for t in T:
                    mm = pe.transpose(X[:, t * XH:(t + 1) * XH], ss[:, t * P:(t + 1) * P],
                                      con[0:XH, C_ID:C_ID + XH])
                mm.then_inc(ssT_done, 1)

            def x2_turned(n, k):
                if k == 0:
                    pe.wait_ge(x2_done, n + 1)
                pe.wait_ge(x2T_sb, n * 2 + k)
                for t in R:
                    for c in range(KD):
                        mm = pe.transpose(X[:, (t * KD + c) * P:(t * KD + c + 1) * P],
                                          x2t[:, 2 * k + t, c * P:(c + 1) * P], ident)
                mm.then_inc(x2T_done, 1)

            def logits(n):
                pe.wait_ge(x2T_sb, n * 2 + 2)
                for t in T:
                    for c in range(KD):
                        mm = pe.matmul(X[:, t * NE:(t + 1) * NE], x2T[:, t, c, :], w_r[:, c, :], start=c == 0,
                                       stop=c == KD - 1)
                mm.then_inc(lg_done, 1)

            def turn(n, i, half, first, last):
                at = lambda j: n * XJ + j + 1

                def scores(j):
                    if j == 0:
                        pe.wait_ge(q_sb, at(XJ - 1))
                        pe.wait_ge(kv_in, i * 48 + 48)
                    pe.wait_ge(added, at(j) - 1)
                    for t in T:
                        for r in R:
                            rows = slice(r * XD, (r + 1) * XD)
                            mm = pe.matmul(S[r][:, t * KC:(t + 1) * KC], qT[half][rows, j, t * P:(t + 1) * P],
                                           kT[rows, j, :], start=True, stop=True)
                    mm.then_inc(sc_done, 1)

                def weights_turned(j):
                    pe.wait_ge(scaled, at(j))
                    if j == 0 and not first:
                        pe.wait_ge(y_done, n * 2)
                    pe.wait_ge(tr_a, at(j) - 1)
                    pe.wait_ge(tr_b, at(j) - 1)
                    for r in R:
                        for t in T:
                            mm = pe.transpose(TB[r][0:CTX, t * P:(t + 1) * P], sc[j % 2][:, r, t, :], ident)
                    mm.then_inc(tr_done, 1)

                def values(j):
                    pe.wait_ge(o_sb, at(j) - 1)
                    pe.wait_ge(tr_a, at(j))
                    pe.wait_ge(tr_b, at(j))
                    for r in R:
                        h = 2 * j + r
                        mm = pe.matmul(V[r * XD:(r + 1) * XD, :], v[0:CTX, h * XD:(h + 1) * XD],
                                       aT[j % 2][0:CTX, r, :], start=True, stop=True)
                    mm.then_inc(pv_done, 1)

                scores(0)
                if not last:
                    x1_turned(n + 1, False)
                for j in range(XJ):
                    if j < XJ - 1:
                        scores(j + 1)
                    if not last:
                        queries(n + 1, j)
                        if j:
                            square_sums(n + 1, j - 1)
                    weights_turned(j)
                    if j:
                        values(j - 1)
                    if not first and j in (X2T_STEP, X2T_STEP + 1):
                        x2_turned(n - 1, j - X2T_STEP)
                    if not first and j == LG_STEP:
                        logits(n - 1)
                values(XJ - 1)
                if not last:
                    square_sums(n + 1, XJ - 1)
                pe.wait_ge(o_sb, at(XJ - 1))
                pe.wait_ge(tr_a, at(XJ - 1))
                pe.wait_ge(tr_b, at(XJ - 1))
                for t in T:
                    for j in range(XJ):
                        mm = pe.matmul(TB[t // 2][:, (t % 2) * D:(t % 2 + 1) * D], oT[:, j, t * P:(t + 1) * P],
                                       w_o[:, j, :], start=j == 0, stop=j == XJ - 1)
                    if t % 2:
                        mm.then_inc(wo_done, 1)
                if not last:
                    pe.wait_ge(lg_sb, n)
                    sums_turned(n + 1)

            x1_turned(0, True)
            for j in range(XJ):
                queries(0, j)
                if j:
                    square_sums(0, j - 1)
            square_sums(0, XJ - 1)
            sums_turned(0)
            blocks(pe, turn)
            for k in R:
                x2_turned(BLOCKS - 1, k)
            logits(BLOCKS - 1)

        @block.scalar
        def _(act):
            def x1_out(m):
                act.wait_ge(x1T_done, m + 1)
                for c in range(KD):
                    nc.scalar.activation(x1T[:, c, :], (Q, X)[c][:], ACT.Copy).then_inc(x1T_sb, 1)

            def query_out(m, b, j):
                act.wait_ge(q_done, m * XJ + j + 1)
                nc.scalar.activation(qT[b][:, j, :], Q[:], ACT.Copy).then_inc(q_sb, 1)

            def sums_out(m):
                act.wait_ge(ss_done[0], m * HX + HX)
                act.wait_ge(ss_done[1], m * HX + HX)
                if not (isinstance(m, int) and m == 0):
                    act.wait_ge(ssT_done, m)
                nc.scalar.activation(ss[:], SS[0:XH, :], ACT.Sqrt, bias=eps[0:XH, 1:2]).then_inc(ss_sb, 1)

            def x2_sd(n):
                act.wait_ge(mv_done, n + 1)
                nc.scalar.activation(rstd[:], mv[:, :, 1], ACT.Sqrt, bias=eps[:, 0:1]).then_inc(sd_done, 1)

            def x2_out_of_psum(n, k):
                act.wait_ge(x2T_done, n * 2 + k + 1)
                nc.scalar.activation(x2T[:, 2 * k:2 * k + 2], X[:].rearrange("p (t c j) -> p t c j", c=KD, j=P),
                                     ACT.Copy).then_inc(x2T_sb, 1)

            def turn(n, i, half, first, last):
                at = lambda j: n * XJ + j + 1

                def exponentials(j):
                    act.wait_ge(nb_done, at(j))
                    for r in R:
                        for t in T:
                            e = nc.scalar.activation(sc[j % 2][:, r, t, :], sc[j % 2][:, r, t, :], ACT.Exp,
                                                     bias=nb[j % 2][:, r, t:t + 1],
                                                     scale=rq[:, 2 * j + r, t:t + 1],
                                                     accum_out=den[j % 2][:, r, t:t + 1])
                    e.then_inc(exp_done, 1)

                def out_out(j):
                    act.wait_ge(pv_done, at(j))
                    nc.scalar.activation(oT[:, j, :], V[:], ACT.Copy).then_inc(o_sb, 1)

                if not last:
                    x1_out(n + 1)
                if not first:
                    x2_sd(n - 1)
                exponentials(0)
                for j in range(XJ):
                    if not last:
                        query_out(n + 1, 1 - half, j)
                    if j < XJ - 1:
                        exponentials(j + 1)
                    act.wait_ge(tr_done, at(j))
                    nc.scalar.activation(aT[j % 2][0:CTX, 0, :], TB[0][0:CTX, :], ACT.Copy).then_inc(tr_a, 1)
                    if j:
                        out_out(j - 1)
                    if not first and j in (X2T_STEP, X2T_STEP + 1):
                        x2_out_of_psum(n - 1, j - X2T_STEP)
                out_out(XJ - 1)
                if not last:
                    sums_out(n + 1)

            act.wait_ge(set_up, 3)
            x1_out(0)
            for j in range(XJ):
                query_out(0, 0, j)
            sums_out(0)
            blocks(act, turn)
            x2_sd(BLOCKS - 1)
            for k in R:
                x2_out_of_psum(BLOCKS - 1, k)

        @block.vector
        def _(dve):
            def sums_out(m):
                dve.wait_ge(ssT_done, m + 1)
                nc.vector.reciprocal(rq[:], X[:, 0:BLK * XH].rearrange("p (t h) -> p h t", t=BLK)
                                     ).then_inc(rq_done, 1)

            def norm(n):
                dve.wait_ge(sd_done, n + 1)
                nc.vector.reciprocal(rstd[:], rstd[:]).then_inc(r_done, 1)
                dve.wait_ge(r_done, n + 1)
                for t in T:
                    z = nc.vector.tensor_scalar(x2t[:, t, :], x2t[:, t, :], mv[:, t, 0:1], rstd[:, t:t + 1],
                                                ALU.subtract, ALU.mult)
                z.then_inc(x2_done, 1)

            def logits_out(n):
                dve.wait_ge(lg_out, n * 16)
                dve.wait_ge(lg_done, n + 1)
                nc.vector.tensor_copy(lg[:], X[:, 0:BLK * NE].rearrange("p (t e) -> p t e", e=NE)
                                      ).then_inc(lg_sb, 1)

            def turn(n, i, half, first, last):
                at = lambda j: n * XJ + j + 1

                def masked(j):
                    dve.wait_ge(sc_done, at(j))
                    if j == 0:
                        dve.wait_ge(kv_in, i * 48 + 48)
                    for r in R:
                        m = nc.vector.tensor_tensor(sc[j % 2][:, r],
                                                    S[r][:, 0:BLK * KC].rearrange("p (t c) -> p t c", c=KC)[:, :, 0:CTX],
                                                    madd[:].unsqueeze(1).broadcast_to([P, BLK, CTX]), ALU.add)
                    m.then_inc(added, 1)
                    dve.wait_ge(added, at(j))
                    nc.vector.tensor_reduce(mx[j % 2][:], sc[j % 2][:], AX_X, ALU.max).then_inc(mx_done, 1)
                    if j == 0:
                        dve.wait_ge(rq_done, n + 1)
                    dve.wait_ge(mx_done, at(j))
                    nc.vector.scalar_tensor_tensor(nb[j % 2][:], mx[j % 2][:], -1.0, rq[:, 2 * j:2 * j + 2, :],
                                                   ALU.mult, ALU.mult).then_inc(nb_done, 1)

                def normed(j):
                    dve.wait_ge(exp_done, at(j))
                    nc.vector.reciprocal(den[j % 2][:], den[j % 2][:]).then_inc(den_done, 1)
                    dve.wait_ge(den_done, at(j))
                    nc.vector.tensor_tensor(sc[j % 2][:], sc[j % 2][:],
                                            den[j % 2][:].unsqueeze(3).broadcast_to([P, 2, BLK, CTX]), ALU.mult
                                            ).then_inc(scaled, 1)

                masked(0)
                for j in range(XJ):
                    if j < XJ - 1:
                        masked(j + 1)
                    normed(j)
                    if j == 0 and not first:
                        norm(n - 1)
                    dve.wait_ge(tr_done, at(j))
                    nc.vector.tensor_copy(aT[j % 2][0:CTX, 1, :], TB[1][0:CTX, :]).then_inc(tr_b, 1)
                    if not first and j == LG_STEP:
                        logits_out(n - 1)
                dve.wait_ge(xr_in, n * 16 + 16)
                dve.wait_ge(x2_out, n * 16)
                for k in W:
                    dve.wait_ge(wo_done, n * 2 + k + 1)
                    nc.vector.tensor_tensor(x2t[:, 2 * k:2 * k + 2, :], xr[:, 2 * k:2 * k + 2, :],
                                            TB[k][:].rearrange("p (t d) -> p t d", d=D), ALU.add
                                            ).then_inc(y_done, 1)
                    dve.wait_ge(y_done, n * 2 + k + 1)
                    for t in (2 * k, 2 * k + 1):
                        nc.vector.bn_stats(stats[:, t, :], x2t[:, t, :]).then_inc(st_done, 1)
                dve.wait_ge(st_done, n * BLK + BLK)
                nc.vector.sem_inc(st_seen, 1)
                for t in T:
                    ag = nc.vector.bn_aggr(mv[:, t, :], stats[:, t, :])
                ag.then_inc(mv_done, 1)
                if not last:
                    sums_out(n + 1)

            sums_out(0)
            blocks(dve, turn)
            norm(BLOCKS - 1)
            logits_out(BLOCKS - 1)



EXPERT_LOADS = 3 * NE + 3


def load_experts(eng, a, s):
    w_gu, w_d, b_gu, b_d, weights_in = s["w_gu"], s["w_d"], s["b_gu"], s["b_d"], s["weights_in"]
    for e in range(NE):
        eng.dma_start(w_gu[:, e, :, 0:FF], a["L0_ffn_gate_w"][e].rearrange("(k p) n -> p k n", p=P)
                      ).then_inc(weights_in, 16)
        eng.dma_start(w_gu[:, e, :, FF:2 * FF], a["L0_ffn_up_w"][e].rearrange("(k p) n -> p k n", p=P)
                      ).then_inc(weights_in, 16)
        eng.dma_start(w_d[:, e], a["L0_ffn_down_w"][e].rearrange("(k p) n -> p k n", p=P)
                      ).then_inc(weights_in, 16)
    for k, n in enumerate(("L0_ffn_gate_b", "L0_ffn_up_b", "L0_ffn_down_b")):
        dst = (b_gu[:, :, 0:FF], b_gu[:, :, FF:2 * FF], b_d[:])[k]
        eng.dma_start(dst, a[n].unsqueeze(0).broadcast_to([P, NE, a[n].shape[1]])).then_inc(weights_in, 16)



def route_stage(nc, a, s):
    with ExitStack() as ctx:
        sb = lambda n, shape, dt=F32: ctx.enter_context(nc.sbuf_tensor(n, shape, dt))
        sem = ctx.enter_context(stage_semaphores(nc))
        con = sb("con5", [P, C_N])
        lg = sb("lg5", [P, TILES, NE])
        pr = sb("pr", [P, TILES, NE])
        pick = sb("pick", [P, TILES, NE])
        w = sb("w5", [P, TILES, NE])
        pos = sb("pos", [P, TILES, NE])
        cmp1 = sb("cmp1", [P, TILES, NE, NE])
        cmp2 = sb("cmp2", [P, TILES, NE, NE])
        row = sb("row5", [P, TILES])
        tot = sb("tot", [P, TILES, NE])
        cum = sb("cum", [P, NE, TILES])
        k128 = sb("k128", [P, TILES])
        many = sb("many", [P, NE, TILES])
        nt = sb("nt", [P, NE])
        ct = sb("ct", [P, NE])
        base = sb("base", [P, NE])
        of = sb("of", [P, FT, NE])
        off = sb("off", [P, FT])
        posf = sb("posf", [P, 2, TILES])
        xt = [sb(f"xt5_{q}", [P, D]) for q in range(2)]
        idx = [sb(f"idx5_{q}", [P, 2], I32) for q in range(2)]
        ps_w = ctx.enter_context(nc.psum_tensor("ps_w", [P, 512], F32))
        ps_t = ctx.enter_context(nc.psum_tensor("ps_t", [P, 512], F32))
        loaded, steps, shifted, exped, picked, counted, tot_done, placed = [
            sem(f"r_{n}") for n in "loaded steps shifted exped picked counted tot_done placed".split()]
        x_in = [sem(f"r_x_in{q}") for q in range(2)]
        idx_done = [sem(f"r_idx_done{q}") for q in range(2)]
        seen = sem("r_seen")
        x_out = [sem(f"r_x_out{q}") for q in range(2)]
        pos_i, weight, tile_e = s["pos_i"], s["weight"], s["tile_e"]
        block = ctx.enter_context(nc.Block())
        ex = lambda t: t.unsqueeze(2).broadcast_to([P, TILES, NE])

        @block.sync
        def _(sp):
            sp.dma_start(con[:], a["consts"]).then_inc(loaded, 16)
            sp.dma_start(lg[:], s["lg"].rearrange("t p e -> p t e")).then_inc(loaded, 16)
            with sp.Fori(0, TILES // 2) as i:
                for q in range(2):
                    sp.wait_ge(x_out[q], i * 32)
                    sp.dma_start(xt[q][:], s["x2"][i * 2 + q]).then_inc(x_in[q], 16)

        @block.scalar
        def _(act):
            act.wait_ge(shifted, 1)
            nc.scalar.activation(pr[:], pr[:], ACT.Exp).then_inc(exped, 1)
            load_experts(act, a, s)

        @block.tensor
        def _(pe):
            pe.wait_ge(loaded, 32)
            pe.wait_ge(picked, 1)
            m = pick[:].rearrange("p t e -> p (t e)")
            pe.matmul(ps_w[:, 0:TILES * NE], con[:, C_LT:C_LT + P], m, start=True, stop=True)
            pe.matmul(ps_t[:, 0:TILES * NE], con[:, C_ONE:C_ONE + P], m, start=True, stop=True).then_inc(counted, 1)

        @block.vector
        def _(dve):
            n = [0]

            def link(ins):
                n[0] += 1
                ins.then_inc(steps, 1)
                dve.wait_ge(steps, n[0])

            V = nc.vector
            dve.wait_ge(loaded, 32)
            link(V.tensor_reduce(row[:], lg[:], AX_X, ALU.max))
            V.tensor_tensor(pr[:], lg[:], ex(row[:]), ALU.subtract).then_inc(shifted, 1)
            link(V.tensor_scalar(k128[:], con[:, C_IOTA:C_IOTA + TILES], float(P), None, ALU.mult))
            dve.wait_ge(exped, 1)
            link(V.tensor_reduce(row[:], pr[:], AX_X, ALU.add))
            link(V.reciprocal(row[:], row[:]))
            link(V.tensor_tensor(pr[:], pr[:], ex(row[:]), ALU.mult))
            one = pr[:].unsqueeze(3).broadcast_to([P, TILES, NE, NE])
            other = pr[:].unsqueeze(2).broadcast_to([P, TILES, NE, NE])
            link(V.tensor_tensor(cmp1[:], other, one, ALU.is_gt))
            link(V.tensor_tensor(cmp2[:], other, one, ALU.is_equal))
            lower = con[:, C_LOW:C_LOW + NE * NE].rearrange("p (a b) -> p a b", b=NE)
            link(V.tensor_tensor(cmp2[:], cmp2[:], lower.unsqueeze(1).broadcast_to([P, TILES, NE, NE]), ALU.mult))
            link(V.tensor_tensor(cmp1[:], cmp1[:], cmp2[:], ALU.add))
            link(V.tensor_reduce(pick[:], cmp1[:], AX_X, ALU.add))
            V.tensor_scalar(pick[:], pick[:], 1.5, None, ALU.is_lt).then_inc(picked, 1)
            dve.wait_ge(picked, 1)
            link(V.tensor_tensor(w[:], pr[:], pick[:], ALU.mult))
            link(V.tensor_reduce(row[:], w[:], AX_X, ALU.add))
            link(V.tensor_scalar(row[:], row[:], 1e-9, None, ALU.add))
            link(V.reciprocal(row[:], row[:]))
            link(V.tensor_tensor(w[:], w[:], ex(row[:]), ALU.mult))
            dve.wait_ge(counted, 1)
            link(V.tensor_copy(tot[:], ps_t[:, 0:TILES * NE].rearrange("p (t e) -> p t e", e=NE)))
            for e in range(NE):
                sc = V.tensor_tensor_scan(cum[:, e, :], con[:, C_ONE:C_ONE + TILES], tot[:, :, e], 0.0,
                                          ALU.mult, ALU.add)
            link(sc)
            link(V.tensor_tensor(many[:], cum[:, :, TILES - 1:TILES].broadcast_to([P, NE, TILES]),
                                 k128[:].unsqueeze(1).broadcast_to([P, NE, TILES]), ALU.is_gt))
            link(V.tensor_reduce(nt[:], many[:], AX_X, ALU.add))
            link(V.tensor_tensor_scan(ct[:], con[:, C_ONE:C_ONE + NE], nt[:], 0.0, ALU.mult, ALU.add))
            link(V.tensor_tensor(base[:], ct[:], nt[:], ALU.subtract))
            link(V.tensor_scalar(base[:], base[:], float(P), None, ALU.mult))
            link(V.tensor_tensor(pos[:], cum[:].rearrange("p e t -> p t e"), tot[:], ALU.subtract))
            link(V.tensor_tensor(pos[:], pos[:], ps_w[:, 0:TILES * NE].rearrange("p (t e) -> p t e", e=NE), ALU.add))
            link(V.tensor_tensor(pos[:], pos[:], base[:].unsqueeze(1).broadcast_to([P, TILES, NE]), ALU.add))
            link(V.tensor_tensor(pos[:], pos[:], pick[:], ALU.mult))
            link(V.tensor_reduce(posf[:, 1, :], pos[:], AX_X, ALU.max))
            link(V.tensor_reduce(posf[:, 0, :], pos[:], AX_X, ALU.add))
            link(V.tensor_tensor(posf[:, 0, :], posf[:, 0, :], posf[:, 1, :], ALU.subtract))
            V.tensor_copy(pos_i[:], posf[:]).then_inc(placed, 1)
            link(V.tensor_tensor(pick[:], pos[:], ex(posf[:, 1, :]), ALU.is_equal))
            link(V.tensor_tensor(pick[:], pick[:], w[:], ALU.mult))
            link(V.tensor_reduce(weight[:, 1, :], pick[:], AX_X, ALU.add))
            link(V.tensor_tensor(w[:], w[:], pick[:], ALU.subtract))
            link(V.tensor_reduce(weight[:, 0, :], w[:], AX_X, ALU.add))
            link(V.tensor_tensor(of[:], con[:, C_IOTA:C_IOTA + FT].unsqueeze(2).broadcast_to([P, FT, NE]),
                                 ct[:].unsqueeze(1).broadcast_to([P, FT, NE]), ALU.is_ge))
            link(V.tensor_reduce(off[:], of[:], AX_X, ALU.add))
            link(V.tensor_scalar(off[:], off[:], float(NE - 1), None, ALU.min))
            link(V.tensor_copy(tile_e[:, 0:FT], off[:]))

        @block.gpsimd
        def _(pool):
            pool.wait_ge(placed, 1)
            with pool.Fori(0, TILES // 2) as i:
                for q in range(2):
                    pool.wait_ge(x_out[q], i * 32)
                    nc.gpsimd.sem_inc(seen, 1)
                    nc.gpsimd.tensor_copy(idx[q][:], pos_i[:, :, i * 2 + q]).then_inc(idx_done[q], 1)
                    pool.wait_ge(idx_done[q], i + 1)
                    pool.wait_ge(x_in[q], i * 16 + 16)
                    nc.gpsimd.sem_inc(seen, 1)
                    for k in range(2):
                        nc.gpsimd.indirect_dma_start(
                            out=s["xs"].rearrange("t p d -> (t p) d"),
                            out_offset=bass.IndirectOffsetOnAxis(ap=idx[q][:, k:k + 1], axis=0),
                            in_=xt[q][:], in_offset=None).then_inc(x_out[q], 16)
            for q in range(2):
                pool.wait_ge(x_out[q], 32 * TILES // 2)


def expert_stage(nc, a, s):
    with ExitStack() as ctx:
        sb = lambda n, shape, dt=F32: ctx.enter_context(nc.sbuf_tensor(n, shape, dt))
        bank = lambda n: ctx.enter_context(nc.psum_tensor(n, [P, 512], F32))
        sem = ctx.enter_context(stage_semaphores(nc))
        Q = range(2)
        two = lambda n, shape: [sb(f"{n}{q}", shape) for q in Q]
        sems = lambda n: [sem(f"e_{n}{q}") for q in Q]
        FK = FF // P
        ident = sb("ident6", [P, P])
        w_gu, w_d, b_gu, b_d, weights_in = s["w_gu"], s["w_d"], s["b_gu"], s["b_d"], s["weights_in"]
        xs = two("xs6_", [P, D])
        xsT = two("xsT", [P, KD, P])
        g = two("g6_", [P, FF])
        u = two("u6_", [P, FF])
        hT = two("hT", [P, FK, P])
        o = two("o6_", [P, D])
        pG = [bank(f"pG{q}") for q in Q]
        pU = [bank(f"pU{q}") for q in Q]
        pX, pH = bank("pX6"), bank("pH6")
        pD = [bank(f"pD{q}") for q in Q]
        ident_in = sem("e_ident_in")
        xs_in, xT_done, xT_sb, gu_done, gb_done, ub_done, silu_done, h_done, hT_done, hT_sb, d_done, o_done, o_out = [
            sems(n) for n in ("xs_in xT_done xT_sb gu_done gb_done ub_done silu_done h_done hT_done hT_sb d_done "
                              "o_done o_out").split()]
        tile_e = s["tile_e"]
        LOOPS = (FT - 3) // 2
        block = ctx.enter_context(nc.Block())

        def turns(eng, turn):
            tile = lambda j: (j % 2, j // 2, j)
            turn(None, None, None, tile(0))
            turn(tile(0), None, None, tile(1))
            turn(tile(1), tile(0), None, tile(2))
            turn(tile(2), tile(1), tile(0), tile(3))
            with eng.Fori(0, LOOPS) as i:
                at = lambda k: (k % 2, i + k // 2, i * 2 + k)
                turn(at(3), at(2), at(1), at(4))
                turn(at(4), at(3), at(2), at(5))
            turn(None, tile(FT - 1), tile(FT - 2), None)
            turn(None, None, tile(FT - 1), None)

        @block.sync
        def _(sp):
            sp.dma_start(ident[:], a["consts"][:, C_ID:C_ID + P]).then_inc(ident_in, 16)

            def load(t):
                q, m, j = t
                sp.wait_ge(xT_done[q], m)
                sp.dma_start(xs[q][:], s["xs"][j]).then_inc(xs_in[q], 16)

            def turn(t, before, earlier, after):
                if after:
                    load(after)

            turns(sp, turn)

        @block.gpsimd
        def _(pool):
            def turn(t, before, earlier, after):
                if earlier:
                    q, m, j = earlier
                    pool.wait_ge(o_done[q], m + 1)
                    pool.dma_start(s["ys"][j], o[q][:]).then_inc(o_out[q], 16)

            turns(pool, turn)
            pool.wait_ge(o_out[0], 16 * ((FT + 1) // 2))
            pool.wait_ge(o_out[1], 16 * (FT // 2))

        @block.tensor
        def _(pe):
            pe.wait_ge(ident_in, 16)
            pe.wait_ge(weights_in, EXPERT_LOADS * 16)

            def x_turned(t):
                q, m, _ = t
                pe.wait_ge(xs_in[q], m * 16 + 16)
                pe.wait_ge(xT_sb[1 - q], m if q == 0 else m + 1)
                for c in range(KD):
                    mm = pe.transpose(pX[:, c * P:(c + 1) * P], xs[q][:, c * P:(c + 1) * P], ident[:])
                mm.then_inc(xT_done[q], 1)

            def expert(t):
                _, _, j = t
                return pe.value_load(tile_e[0:1, j:j + 1] if isinstance(j, int) else tile_e[0:1, bass.ds(j, 1)],
                                     min_val=0, max_val=NE - 1)

            def gate_up(t, e):
                q, m, j = t
                pe.wait_ge(xT_sb[q], m + 1)
                pe.wait_ge(ub_done[q], m)
                pe.wait_ge(gb_done[q], m)
                for k, bk in enumerate((pG[q], pU[q])):
                    for c in range(KD):
                        mm = pe.matmul(bk[:], xsT[q][:, c, :], w_gu[:, bass.ds(e, 1), c, k * FF:(k + 1) * FF],
                                       start=c == 0, stop=c == KD - 1)
                mm.then_inc(gu_done[q], 1)

            def h_turned(t):
                q, m, j = t
                pe.wait_ge(h_done[q], m + 1)
                pe.wait_ge(hT_sb[1 - q], m if q == 0 else m + 1)
                for k in range(FK):
                    mm = pe.transpose(pH[:, k * P:(k + 1) * P], g[q][:, k * P:(k + 1) * P], ident[:])
                mm.then_inc(hT_done[q], 1)

            def down(t, e):
                q, m, j = t
                pe.wait_ge(hT_sb[q], m + 1)
                pe.wait_ge(o_done[q], m)
                for k in range(FK):
                    mm = pe.matmul(pD[q][:, 0:D], hT[q][:, k, :], w_d[:, bass.ds(e, 1), k, :], start=k == 0,
                                   stop=k == FK - 1)
                mm.then_inc(d_done[q], 1)

            def turn(t, before, earlier, after):
                e, e_earlier = t and expert(t), earlier and expert(earlier)
                if t:
                    gate_up(t, e)
                if after:
                    x_turned(after)
                if before:
                    h_turned(before)
                if earlier:
                    down(earlier, e_earlier)

            turns(pe, turn)

        @block.scalar
        def _(act):
            def x_out(t):
                q, m, _ = t
                act.wait_ge(xT_done[q], m + 1)
                act.wait_ge(gu_done[q], m)
                nc.scalar.activation(xsT[q][:], pX[:, 0:D].rearrange("p (c j) -> p c j", c=KD), ACT.Copy
                                     ).then_inc(xT_sb[q], 1)

            def silu(t):
                q, m, _ = t
                act.wait_ge(gb_done[q], m + 1)
                nc.scalar.activation(g[q][:], g[q][:], ACT.Silu).then_inc(silu_done[q], 1)

            def h_out(t):
                q, m, _ = t
                act.wait_ge(hT_done[q], m + 1)
                act.wait_ge(d_done[q], m)
                nc.scalar.activation(hT[q][:], pH[:].rearrange("p (k j) -> p k j", k=FK), ACT.Copy
                                     ).then_inc(hT_sb[q], 1)

            def turn(t, before, earlier, after):
                if after:
                    x_out(after)
                if before:
                    h_out(before)
                if t:
                    silu(t)

            turns(act, turn)

        @block.vector
        def _(dve):
            dve.wait_ge(weights_in, EXPERT_LOADS * 16)

            def biased(t):
                q, m, j = t
                e = dve.value_load(tile_e[0:1, j:j + 1] if isinstance(j, int) else tile_e[0:1, bass.ds(j, 1)],
                                   min_val=0, max_val=NE - 1)
                dve.wait_ge(gu_done[q], m + 1)
                dve.wait_ge(hT_done[q], m)
                nc.vector.tensor_tensor(g[q][:], pG[q][:], b_gu[:, bass.ds(e, 1), 0:FF], ALU.add
                                        ).then_inc(gb_done[q], 1)
                nc.vector.tensor_tensor(u[q][:], pU[q][:], b_gu[:, bass.ds(e, 1), FF:2 * FF], ALU.add
                                        ).then_inc(ub_done[q], 1)

            def hidden(t):
                q, m, j = t
                dve.wait_ge(silu_done[q], m + 1)
                dve.wait_ge(ub_done[q], m + 1)
                nc.vector.tensor_tensor(g[q][:], g[q][:], u[q][:], ALU.mult).then_inc(h_done[q], 1)

            def out(t):
                q, m, j = t
                e = dve.value_load(tile_e[0:1, j:j + 1] if isinstance(j, int) else tile_e[0:1, bass.ds(j, 1)],
                                   min_val=0, max_val=NE - 1)
                dve.wait_ge(d_done[q], m + 1)
                dve.wait_ge(o_out[q], m * 16)
                nc.vector.tensor_tensor(o[q][:], pD[q][:, 0:D], b_d[:, bass.ds(e, 1), :], ALU.add
                                        ).then_inc(o_done[q], 1)

            def turn(t, before, earlier, after):
                if t:
                    biased(t)
                if earlier:
                    out(earlier)
                if t:
                    hidden(t)

            turns(dve, turn)


def combine_stage(nc, a, s, out):
    with ExitStack() as ctx:
        sb = lambda n, shape, dt=F32: ctx.enter_context(nc.sbuf_tensor(n, shape, dt))
        sem = ctx.enter_context(stage_semaphores(nc))
        R = 4
        r_ = range(R)
        sems = lambda n: [sem(f"f_{n}{q}") for q in r_]
        x2 = [sb(f"x2_7{q}", [P, D]) for q in r_]
        z = [sb(f"z7_{q}", [P, D]) for q in r_]
        ya = [[sb(f"y7_{q}{k}", [P, D]) for k in range(2)] for q in r_]
        idx = [sb(f"idx7_{q}", [P, 2], I32) for q in r_]
        wt = [sb(f"wt7_{q}", [P, 2]) for q in r_]
        stats = [sb(f"stats7_{q}", [P, 6]) for q in r_]
        mv = [sb(f"mv7_{q}", [P, 2]) for q in r_]
        rstd = [sb(f"rstd7_{q}", [P, 1]) for q in r_]
        eps = sb("eps7", [P, 1])
        set_up, seen, dseen = sem("f_set_up"), sem("f_seen"), sem("f_dseen")
        x_in, y_in, idx_done, wt_done, a_done, b_done, st_done, mv_done, sd_done, r_done, z_done, z_out = [
            sems(n) for n in ("x_in y_in idx_done wt_done a_done b_done st_done mv_done sd_done r_done z_done "
                              "z_out").split()]
        out_v = out.rearrange("b (c p) d -> (b c) p d", p=P)
        block = ctx.enter_context(nc.Block())

        @block.sync
        def _(sp):
            with sp.Fori(0, TILES // R) as i:
                for q in r_:
                    sp.wait_ge(z_done[q], i)
                    sp.dma_start(x2[q][:], s["x2"][i * R + q]).then_inc(x_in[q], 16)
                for q in r_:
                    sp.wait_ge(z_done[q], i + 1)
                    sp.dma_start(out_v[i * R + q], z[q][:]).then_inc(z_out[q], 16)
            for q in r_:
                sp.wait_ge(z_out[q], 16 * TILES // R)

        @block.gpsimd
        def _(pool):
            nc.gpsimd.memset(eps[:], EPS).then_inc(set_up, 1)
            with pool.Fori(0, TILES // R) as i:
                for q in r_:
                    pool.wait_ge(y_in[q], i * 32)
                    nc.gpsimd.sem_inc(seen, 1)
                    nc.gpsimd.tensor_copy(idx[q][:], s["pos_i"][:, :, i * R + q]).then_inc(idx_done[q], 1)
                    pool.wait_ge(idx_done[q], i + 1)
                    pool.wait_ge(b_done[q], i)
                    nc.gpsimd.sem_inc(seen, 1)
                    for k in range(2):
                        nc.gpsimd.indirect_dma_start(
                            out=ya[q][k][:], out_offset=None, in_=s["ys"].rearrange("t p d -> (t p) d"),
                            in_offset=bass.IndirectOffsetOnAxis(ap=idx[q][:, k:k + 1], axis=0)
                        ).then_inc(y_in[q], 16)

        @block.scalar
        def _(act):
            act.wait_ge(set_up, 1)
            with act.Fori(0, TILES // R) as i:
                for q in r_:
                    act.wait_ge(mv_done[q], i + 1)
                    nc.scalar.activation(rstd[q][:], mv[q][:, 1:2], ACT.Sqrt, bias=eps[:, 0:1]
                                         ).then_inc(sd_done[q], 1)

        @block.vector
        def _(dve):
            with dve.Fori(0, TILES // R) as i:
                for q in r_:
                    dve.wait_ge(b_done[q], i)
                    nc.vector.tensor_scalar(wt[q][:], s["weight"][:, :, i * R + q], 1.0, None, ALU.mult
                                            ).then_inc(wt_done[q], 1)
                for q in r_:
                    dve.wait_ge(x_in[q], i * 16 + 16)
                    dve.wait_ge(y_in[q], i * 32 + 32)
                    dve.wait_ge(wt_done[q], i + 1)
                    nc.vector.scalar_tensor_tensor(x2[q][:], ya[q][0][:], wt[q][:, 0:1], x2[q][:], ALU.mult,
                                                   ALU.add).then_inc(a_done[q], 1)
                for q in r_:
                    dve.wait_ge(a_done[q], i + 1)
                    nc.vector.scalar_tensor_tensor(x2[q][:], ya[q][1][:], wt[q][:, 1:2], x2[q][:], ALU.mult,
                                                   ALU.add).then_inc(b_done[q], 1)
                for q in r_:
                    dve.wait_ge(b_done[q], i + 1)
                    nc.vector.bn_stats(stats[q][:], x2[q][:]).then_inc(st_done[q], 1)
                for q in r_:
                    dve.wait_ge(st_done[q], i + 1)
                    nc.vector.sem_inc(dseen, 1)
                    nc.vector.bn_aggr(mv[q][:], stats[q][:]).then_inc(mv_done[q], 1)
                for q in r_:
                    dve.wait_ge(sd_done[q], i + 1)
                    nc.vector.reciprocal(rstd[q][:], rstd[q][:]).then_inc(r_done[q], 1)
                for q in r_:
                    dve.wait_ge(r_done[q], i + 1)
                    dve.wait_ge(z_out[q], i * 16)
                    nc.vector.tensor_scalar(z[q][:], x2[q][:], mv[q][:, 0:1], rstd[q][:, 0:1],
                                            ALU.subtract, ALU.mult).then_inc(z_done[q], 1)


def build(nc, a, out, stages=99):
    dram = lambda n, shape: nc.dram_tensor(n, shape, F32, kind="Internal").ap()
    s = {
        "qkvg": dram("qkvg", [TILES, P, QKV + DV]),
        "gb": dram("gb", [TILES, P, 2 * H]),
        "x1": dram("x1", [TILES, P, D]),
        "kT": dram("kT", [BATCH, P, XW // P, KC]),
        "v": dram("v", [BATCH, CTX, XW]),
        "madd": dram("madd", [BATCH, P, CTX]),
        "x2": dram("x2", [TILES, P, D]),
        "lg": dram("lg", [TILES, P, NE]),
        "xs": dram("xs", [FT + 1, P, D]),
        "ys": dram("ys", [FT, P, D]),
    }
    if stages == 3:
        s["x1"] = a["x1dbg"]
    else:
        project_stage(nc, a, s)
        delta_stage(nc, a, s)
    context_stage(nc, a, s)
    cross_stage(nc, a, s)
    with ExitStack() as ctx:
        s["pos_i"] = ctx.enter_context(nc.sbuf_tensor("pos_i", [P, 2, TILES], I32))
        s["weight"] = ctx.enter_context(nc.sbuf_tensor("weight", [P, 2, TILES], F32))
        s["tile_e"] = ctx.enter_context(nc.sbuf_tensor("tile_e", [P, FT + 1], I32))
        with ExitStack() as experts, stage_semaphores(nc) as sem:
            sb = lambda n, shape: experts.enter_context(nc.sbuf_tensor(n, shape, F32))
            s["w_gu"] = sb("w_gu", [P, NE, KD, 2 * FF])
            s["w_d"] = sb("w_d", [P, NE, FF // P, D])
            s["b_gu"] = sb("b_gu", [P, NE, 2 * FF])
            s["b_d"] = sb("b_d", [P, NE, D])
            s["weights_in"] = sem("weights_in6")
            route_stage(nc, a, s)
            expert_stage(nc, a, s)
        combine_stage(nc, a, s, out)


_INS = ['x', 'ctx_1024', '_lenS2', 'L0_attn_ln_w', 'L0_attn_ln_b', 'L0_attn_Wq', 'L0_attn_Wk', 'L0_attn_Wv',
        'L0_attn_conv_q', 'L0_attn_conv_k', 'L0_attn_conv_v', 'L0_attn_Wb', 'L0_attn_Wa', 'L0_attn_A_log',
        'L0_attn_dt_bias', 'L0_attn_Wg', 'L0_attn_norm_w', 'L0_attn_Wo', 'L0_xattn_Wq', 'L0_xattn_Wk',
        'L0_xattn_Wv', 'L0_xattn_Wo', 'L0_xattn_q_norm_w', 'L0_xattn_k_norm_w', 'L0_ffn_router_w',
        'L0_ffn_gate_w', 'L0_ffn_gate_b', 'L0_ffn_up_w', 'L0_ffn_up_b', 'L0_ffn_down_w', 'L0_ffn_down_b']


def kernel(**inputs):
    import concourse.bacc as _bacc
    from concourse.bass_utils import run_bass_kernel_spmd as _run

    nc = _bacc.Bacc("TRN2", target_bir_lowering=False, num_devices=1)
    arrays, aps = {}, {}
    for name in _INS:
        arrays[f"in_{name}"] = np.ascontiguousarray(inputs[name])
    arrays["in_consts"] = constants()
    for name, v in arrays.items():
        aps[name[3:]] = nc.dram_tensor(name, v.shape, mybir.dt.from_np(v.dtype), kind="ExternalInput").ap()
    out = nc.dram_tensor("out", [BATCH, SEQ, D], F32, kind="ExternalOutput").ap()
    build(nc, aps, out)
    r = _run(nc, [arrays], core_ids=[0])
    return r.results[0]["out"]
```

```python
from contextlib import ExitStack, contextmanager

import numpy as np

import concourse.bass as bass
from concourse import mybir

P = 128
F32 = mybir.dt.float32
I32 = mybir.dt.int32
ALU = mybir.AluOpType
ACT = mybir.ActivationFunctionType
AX_X = mybir.AxisListType.X

BATCH, SEQ, D = 4, 1024, 256
KD = D // P
TILES = BATCH * SEQ // P
BLK = 4
BT = BLK * P
BLOCKS = TILES // BLK
H, HK, HV, TAPS = 4, 64, 128, 4
DK, DV = H * HK, H * HV
QKV = 2 * DK + DV
CHUNKS = SEQ // P
EPS = 1e-5
NORM_EPS = 1e-6
DECAY_FLOOR = -200.0
XH, XD, CTX = 16, 64, 77
XW = XH * XD
KC = CTX + CTX % 2
NE, FF = 8, 512
ROW = D + 2
FT = (TILES * P * 2) // P + NE - 1

C_ID, C_LE, C_GT, C_GE, C_ONE = 0, P, 2 * P, 3 * P, 4 * P
C_NM0 = 5 * P
C_LEV = 6 * P
LEVELS = 7
C_BLK = C_LEV + (LEVELS - 1) * P // 2
C_LT = C_BLK + 2
C_IOTA = C_LT + P
C_COL = C_IOTA + P
C_LOW = C_COL + 1
C_HEAD = C_LOW + NE * NE
C_N = C_HEAD + XW // P * XH


def constants():
    p, j = np.arange(P)[:, None], np.arange(P)[None, :]
    c = np.zeros((P, C_N), np.float32)
    c[:, C_ID:C_ID + P] = p == j
    c[:, C_LE:C_LE + P] = p <= j
    c[:, C_GT:C_GT + P] = p > j
    c[:, C_GE:C_GE + P] = p >= j
    c[:, C_ONE:C_ONE + P] = 1
    c[:, C_NM0:C_NM0 + P] = -1.0 * ((p // 2 == j // 2) & (p % 2 == 1) & (j % 2 == 0))
    for lev in range(1, LEVELS):
        s = 2 ** lev
        m = (p // (2 * s) == j // (2 * s)) & (p % (2 * s) < s) & (j % (2 * s) >= s)
        c[:, C_LEV + (lev - 1) * P // 2:C_LEV + lev * P // 2] = m[:, (np.arange(P) % (2 * s)) >= s]
    c[:, C_BLK:C_BLK + 2] = p // XD == np.arange(2)[None, :]
    c[:, C_LT:C_LT + P] = p < j
    c[:, C_IOTA:C_IOTA + P] = j
    c[:, C_COL:C_COL + 1] = p
    e = np.arange(NE)
    c[:, C_LOW:C_HEAD] = (e[None, :] < e[:, None]).reshape(1, -1)
    for j in range(XW // P):
        c[:, C_HEAD + j * XH:C_HEAD + (j + 1) * XH] = np.arange(XH)[None, :] == 2 * j + p // XD
    return c


@contextmanager
def stage_semaphores(nc):
    taken = []

    def sem(name):
        taken.append(nc.alloc_semaphore(name=name))
        return taken[-1]

    yield sem
    nc.clear_and_free_semaphores(taken)
    nc.all_engine_barrier()


def project_stage(nc, a, s):
    with ExitStack() as ctx:
        sb = lambda n, shape: ctx.enter_context(nc.sbuf_tensor(n, shape, F32))
        bank = lambda n: ctx.enter_context(nc.psum_tensor(n, [P, 512], F32))
        sem = ctx.enter_context(stage_semaphores(nc))

        NCT = QKV // P
        TURN_JOB = NCT - 3
        x_v = a["x"].rearrange("b (n t p) d -> (b n) p t d", t=BLK, p=P)
        tok_v = s["qkvg"].rearrange("(n t) p c -> n p t c", t=BLK)

        con = s["con"]
        w_qkv = sb("w_qkv", [P, KD, QKV])
        w_gate = sb("w_gate", [P, KD, DV])
        w_ba = sb("w_ba", [P, KD, 2 * H])
        taps = sb("taps", [P, NCT, TAPS])
        ln_wb = sb("ln_wb", [P, 2, KD])
        head_row = sb("head_row", [P, 2, H])
        neg_rate = sb("neg_rate", [P, H])
        eps = sb("eps1", [P, 2])
        xin = [sb(f"xin{b}", [P, BLK, D]) for b in range(2)]
        stats = sb("stats1", [P, BLK, 6])
        mv = sb("mv1", [P, BLK, 2])
        rstd = sb("rstd1", [P, BLK])
        xnT = [sb(f"xnT{b}", [P, KD, BT]) for b in range(2)]
        conv_in = [sb(f"conv_in{b}", [P, NCT, TAPS - 1 + BT]) for b in range(2)]
        conv_y = [sb(f"conv_y{b}", [P, BT]) for b in range(4)]
        act_y = [sb(f"act_y{b}", [P, BT]) for b in range(2)]
        tok = [sb(f"tok{b}", [P, BLK, QKV]) for b in range(2)]
        gate = [sb(f"gate{b}", [P, BLK, DV]) for b in range(2)]
        sq = sb("sq1", [P, BLK, 2 * DK])
        ss = sb("ss1", [P, BLK, 2 * H])
        rn = sb("rn1", [P, BLK, 2 * H])
        beta = [sb(f"beta{b}", [P, BLK, H]) for b in range(2)]
        ba = sb("ba1", [P, BLOCKS + 1, BLK, 2 * H])
        sm = sb("sm1", [P, 6, TILES, H])
        gb = sb("gb1", [P, TILES, 2 * H])

        ps_x = [bank(f"ps_x{c}") for c in range(KD)]
        ps_j = [bank(f"ps_j{c}") for c in range(2)]
        ps_t = [bank(f"ps_t{c}") for c in range(2)]
        ps_g = bank("ps_g")
        ps_ba = bank("ps_ba")

        weights_in = sem("weights_in")
        x_in = [sem(f"x_in{b}") for b in range(2)]
        consts_set = sem("consts_set")
        rate_exp = sem("rate_exp")
        rate_neg = sem("rate_neg")
        stats_done = sem("stats_done")
        stats_seen = sem("stats_seen")
        var_done = sem("var_done")
        sd_done = sem("sd_done")
        rstd_done = sem("rstd_done")
        xn_done = sem("xn_done")
        xT_done = sem("xT_done")
        xnT_done = sem("xnT_done")
        proj_done = [sem(f"proj_done{b}") for b in range(2)]
        proj_taken = [sem(f"proj_taken{b}") for b in range(2)]
        gate_done = sem("gate_done")
        gate_taken = sem("gate_taken")
        ba_done = sem("ba_done")
        hist_set = sem("hist_set")
        tap_done = [sem(f"tap_done{b}") for b in range(2)]
        conv_step = sem("conv_step")
        conv_done = sem("conv_done")
        silu_done = [sem(f"silu_done{b}") for b in range(2)]
        tokT_done = [sem(f"tokT_done{b}") for b in range(2)]
        tok_taken = [sem(f"tok_taken{b}") for b in range(2)]
        sq_done = sem("sq_done")
        ss_done = sem("ss_done")
        norm_sd = sem("norm_sd")
        norm_r = sem("norm_r")
        scaled = sem("scaled")
        beta_scaled = sem("beta_scaled")
        ba_sb = sem("ba_sb")
        beta_exp = sem("beta_exp")
        beta_done = sem("beta_done")
        z_abs = sem("z_abs")
        exps_done = sem("exps_done")
        soft = sem("soft")
        gb_done = sem("gb_done")
        tok_out = [sem(f"tok_out{b}") for b in range(2)]

        block = ctx.enter_context(nc.Block())

        def view_heads(t, lo, n, d):
            return t[:, :, lo:lo + n * d].rearrange("p t (h d) -> p t h d", d=d)

        @block.sync
        def _(sp):
            sp.dma_start(xin[0][:], x_v[0]).then_inc(x_in[0], 16)
            sp.dma_start(con[:], a["consts"]).then_inc(weights_in, 16)
            for k, w in enumerate((a["L0_attn_Wq"], a["L0_attn_Wk"], a["L0_attn_Wv"])):
                lo = (0, DK, 2 * DK)[k]
                sp.dma_start(w_qkv[:, :, lo:lo + w.shape[1]],
                             w.rearrange("(k p) n -> p k n", p=P)).then_inc(weights_in, 16)
            sp.dma_start(w_gate[:], a["L0_attn_Wg"].rearrange("(k p) n -> p k n", p=P)).then_inc(weights_in, 16)
            for k, w in enumerate((a["L0_attn_Wb"], a["L0_attn_Wa"])):
                sp.dma_start(w_ba[:, :, k * H:(k + 1) * H],
                             w.rearrange("(k p) n -> p k n", p=P)).then_inc(weights_in, 16)
            for k, w in enumerate((a["L0_attn_conv_q"], a["L0_attn_conv_k"], a["L0_attn_conv_v"])):
                lo, n = (0, DK // P, 2 * DK // P)[k], w.shape[0] // P
                sp.dma_start(taps[:, lo:lo + n, :],
                             w.rearrange("(m p) k -> p m k", p=P)).then_inc(weights_in, 16)
            for k, w in enumerate((a["L0_attn_ln_w"], a["L0_attn_ln_b"])):
                sp.dma_start(ln_wb[:, k, :], w.rearrange("(k p) -> p k", p=P), allow_slow_non_contiguous=True
                             ).then_inc(weights_in, 16)
            for k, w in enumerate((a["L0_attn_A_log"], a["L0_attn_dt_bias"])):
                sp.dma_start(head_row[:, k, :],
                             w.rearrange("(a h) -> a h", a=1).broadcast_to([P, H])).then_inc(weights_in, 16)
            sp.dma_start(xin[1][:], x_v[1]).then_inc(x_in[1], 16)
            sp.wait_ge(xT_done, 1)
            sp.dma_start(xin[0][:], x_v[2]).then_inc(x_in[0], 16)
            with sp.Fori(0, BLOCKS // 2) as i:
                for b in range(2):
                    n = i * 2 + b
                    sp.wait_ge(xT_done, n + 2)
                    sp.dma_start(xin[1 - b][:], x_v[(i * 2 + 2 + 2 * b) % BLOCKS + 1 - b]).then_inc(x_in[1 - b], 16)
                    sp.wait_ge(beta_scaled, n + 1)
                    sp.wait_ge(scaled, n + 1)
                    sp.wait_ge(tok_taken[0], n * (NCT // 2) + NCT // 2)
                    sp.wait_ge(tok_taken[1], n * (NCT // 2) + NCT // 2)
                    sp.dma_start(tok_v[n][:, :, 0:QKV], tok[b][:]).then_inc(tok_out[b], 16)
                    sp.wait_ge(gate_taken, n * BLK + BLK)
                    sp.dma_start(tok_v[n][:, :, QKV:QKV + DV], gate[b][:]).then_inc(tok_out[b], 16)
            sp.wait_ge(gb_done, 2)
            sp.dma_start(s["gb"].rearrange("t p c -> p t c"), gb[:]).then_inc(tok_out[0], 16)
            sp.wait_ge(tok_out[0], 32 * (BLOCKS // 2) + 16)
            sp.wait_ge(tok_out[1], 32 * (BLOCKS // 2))
            sp.wait_ge(x_in[0], 16 * (BLOCKS // 2 + 2))

        @block.gpsimd
        def _(pool):
            nc.gpsimd.memset(eps[:, 0:1], EPS).then_inc(consts_set, 1)
            nc.gpsimd.memset(eps[:, 1:2], NORM_EPS).then_inc(consts_set, 1)
            nc.gpsimd.memset(conv_in[0][:, :, 0:TAPS - 1], 0.0).then_inc(consts_set, 1)
            with pool.Fori(0, BLOCKS // 2) as i:
                for b in range(2):
                    n = i * 2 + b
                    for k in range(2):
                        pool.wait_ge(tok_taken[0], n * (NCT // 2) + k + 1)
                        pool.wait_ge(tok_taken[1], n * (NCT // 2) + k + 1)
                        pool.wait_ge(ss_done, n)
                        part = tok[b][:, :, k * DK:(k + 1) * DK]
                        nc.gpsimd.tensor_tensor(sq[:, :, k * DK:(k + 1) * DK], part, part, ALU.mult
                                                ).then_inc(sq_done, 1)
                    if b == 0:
                        pool.wait_ge(proj_taken[0], n * (NCT // 2) + NCT // 2)
                        pool.wait_ge(proj_taken[1], n * (NCT // 2) + NCT // 2)
                        pool.wait_ge(conv_done, n * NCT)
                        ones = con[:, C_ONE:C_ONE + TAPS - 1].unsqueeze(1).broadcast_to([P, NCT, TAPS - 1])
                        nc.gpsimd.tensor_tensor(conv_in[1][:, :, 0:TAPS - 1], conv_in[0][:, :, BT:BT + TAPS - 1],
                                                ones, ALU.mult).then_inc(hist_set, 1)
                    pool.wait_ge(norm_r, n * 2 + 2)
                    v = view_heads(tok[b], 0, 2 * H, HK)
                    nc.gpsimd.tensor_tensor(v, v, rn[:].unsqueeze(3).broadcast_to([P, BLK, 2 * H, HK]),
                                            ALU.mult).then_inc(scaled, 1)
                    pool.wait_ge(beta_done, n + 1)
                    pool.wait_ge(tok_taken[0], n * (NCT // 2) + NCT // 2)
                    pool.wait_ge(tok_taken[1], n * (NCT // 2) + NCT // 2)
                    v = view_heads(tok[b], 2 * DK, H, HV)
                    nc.gpsimd.tensor_tensor(v, v, beta[b][:].unsqueeze(3).broadcast_to([P, BLK, H, HV]),
                                            ALU.mult).then_inc(beta_scaled, 1)

        @block.tensor
        def _(pe):
            pe.wait_ge(weights_in, 16 * 14)

            def x_turned(n, b):
                pe.wait_ge(xn_done, n + 1)
                pe.wait_ge(xnT_done, n * KD)
                for c in range(KD):
                    for t in range(BLK):
                        mm = pe.transpose(ps_x[c][:, t * P:(t + 1) * P], xin[b][:, t, c * P:(c + 1) * P],
                                          con[:, C_ID:C_ID + P])
                mm.then_inc(xT_done, 1)

            def beta_decay(n, b):
                pe.wait_ge(xnT_done, n * KD + KD)
                pe.wait_ge(ba_sb, n)
                for t in range(BLK):
                    for c in range(KD):
                        mm = pe.matmul(ps_ba[:, t * 2 * H:(t + 1) * 2 * H], xnT[b][:, c, t * P:(t + 1) * P],
                                       w_ba[:, c, :], start=c == 0, stop=c == KD - 1)
                mm.then_inc(ba_done, 1)

            x_turned(0, 0)
            beta_decay(0, 0)
            with pe.Fori(0, BLOCKS // 2) as i:
                for b in range(2):
                    n = i * 2 + b
                    def to_tokens(m):
                        pe.wait_ge(silu_done[m % 2], n * (NCT // 2) + m // 2 + 1)
                        pe.wait_ge(tok_taken[m % 2], n * (NCT // 2) + m // 2)
                        for t in range(BLK):
                            mm = pe.transpose(ps_t[m % 2][:, t * P:(t + 1) * P],
                                              act_y[m % 2][:, t * P:(t + 1) * P], con[:, C_ID:C_ID + P])
                        mm.then_inc(tokT_done[m % 2], 1)

                    for j in range(NCT + 3):
                        if j < NCT:
                            pe.wait_ge(proj_taken[j % 2], n * (NCT // 2) + j // 2)
                            for c in range(KD):
                                mm = pe.matmul(ps_j[j % 2][:], w_qkv[:, c, j * P:(j + 1) * P], xnT[b][:, c, :],
                                               start=c == 0, stop=c == KD - 1)
                            mm.then_inc(proj_done[j % 2], 1)
                        if 3 <= j:
                            to_tokens(j - 3)
                        if j % 2 and j < NCT:
                            t = j // 2
                            pe.wait_ge(gate_taken, n * BLK + t)
                            for c in range(KD):
                                mm = pe.matmul(ps_g[:], xnT[b][:, c, t * P:(t + 1) * P], w_gate[:, c, :],
                                               start=c == 0, stop=c == KD - 1)
                            mm.then_inc(gate_done, 1)
                        if j == TURN_JOB:
                            x_turned(n + 1, 1 - b)
                        if j == TURN_JOB + 2:
                            beta_decay(n + 1, 1 - b)

        @block.scalar
        def _(act):
            act.wait_ge(weights_in, 16 * 14)
            act.wait_ge(consts_set, 3)
            nc.scalar.activation(neg_rate[:], head_row[:, 0, :], ACT.Exp).then_inc(rate_exp, 1)

            def block_sd(n):
                act.wait_ge(var_done, n + 1)
                act.wait_ge(xn_done, n)
                nc.scalar.activation(rstd[:], mv[:, :, 1], ACT.Sqrt, bias=eps[:, 0:1]).then_inc(sd_done, 1)

            def x_out(n, b):
                act.wait_ge(xT_done, n + 1)
                for c in range(KD):
                    nc.scalar.activation(xnT[b][:, c, :], ps_x[c][:], ACT.Identity,
                                         bias=ln_wb[:, 1, c:c + 1],
                                         scale=ln_wb[:, 0, c:c + 1]).then_inc(xnT_done, 1)

            def exps(n, b):
                act.wait_ge(ba_done, n + 1)
                act.wait_ge(beta_done, n)
                logit = ps_ba[:, 0:BLK * 2 * H].rearrange("p (t h) -> p t h", t=BLK)[:, :, 0:H]
                nc.scalar.activation(beta[b][:], logit, ACT.Exp, scale=-1.0).then_inc(beta_exp, 1)

            block_sd(0)
            block_sd(1)
            x_out(0, 0)
            exps(0, 0)
            with act.Fori(0, BLOCKS // 2) as i:
                for b in range(2):
                    n = i * 2 + b
                    if b == 0:
                        act.wait_ge(hist_set, i)

                    def silu(m):
                        act.wait_ge(conv_done, n * NCT + m + 1)
                        act.wait_ge(tokT_done[m % 2], n * (NCT // 2) + m // 2)
                        nc.scalar.activation(act_y[m % 2][:], conv_y[m % 4][:], ACT.Silu
                                             ).then_inc(silu_done[m % 2], 1)

                    def take_tokens(m):
                        act.wait_ge(tokT_done[m % 2], n * (NCT // 2) + m // 2 + 1)
                        if m == 0:
                            act.wait_ge(tok_out[b], i * 32)
                        nc.scalar.activation(tok[b][:, :, m * P:(m + 1) * P],
                                             ps_t[m % 2][:].rearrange("p (t c) -> p t c", t=BLK),
                                             ACT.Copy).then_inc(tok_taken[m % 2], 1)

                    for j in range(NCT + 4):
                        if j < NCT:
                            act.wait_ge(proj_done[j % 2], n * (NCT // 2) + j // 2 + 1)
                            nc.scalar.activation(conv_in[b][:, j, TAPS - 1:TAPS - 1 + BT], ps_j[j % 2][:], ACT.Copy)
                            act.wait_ge(silu_done[j % 2], n * (NCT // 2) + max(j // 2 - 1, 0))
                            nc.scalar.activation(conv_y[j % 4][:], ps_j[j % 2][:], ACT.Copy,
                                                 scale=taps[:, j, TAPS - 1:TAPS]).then_inc(proj_taken[j % 2], 1)
                        if 2 <= j < NCT + 2:
                            silu(j - 2)
                        if 4 <= j:
                            take_tokens(j - 4)
                        if j % 2 and j < NCT:
                            act.wait_ge(gate_done, n * BLK + j // 2 + 1)
                            if j == 1:
                                act.wait_ge(tok_out[b], i * 32)
                            nc.scalar.activation(gate[b][:, j // 2, :], ps_g[:], ACT.Silu).then_inc(gate_taken, 1)
                        if j == TURN_JOB + 1:
                            x_out(n + 1, 1 - b)
                        if j == NCT + 1:
                            block_sd(n + 2)
                            act.wait_ge(ss_done, n + 1)
                            nc.scalar.activation(rn[:], ss[:], ACT.Sqrt, bias=eps[:, 1:2]).then_inc(norm_sd, 1)
                            act.wait_ge(beta_scaled, n)
                            exps(n + 1, 1 - b)
            act.wait_ge(z_abs, 1)
            nc.scalar.activation(sm[:, 0], ba[:, 0:BLOCKS, :, 0:H].rearrange("p n t h -> p (n t) h"), ACT.Exp, scale=-1.0
                                 ).then_inc(exps_done, 1)
            nc.scalar.activation(sm[:, 2], sm[:, 1], ACT.Exp, scale=-1.0).then_inc(exps_done, 1)

        @block.vector
        def _(dve):
            dve.wait_ge(rate_exp, 1)
            nc.vector.tensor_scalar(neg_rate[:], neg_rate[:], -1.0, None, ALU.mult).then_inc(rate_neg, 1)
            dve.wait_ge(rate_neg, 1)

            def moments(n, b, k):
                dve.wait_ge(x_in[b], k * 16 + 16)
                for t in range(BLK):
                    nc.vector.bn_stats(stats[:, t, :], xin[b][:, t, :]).then_inc(stats_done, 1)
                dve.wait_ge(stats_done, n * BLK + BLK)
                dve.wait_ge(sd_done, n)
                nc.vector.sem_inc(stats_seen, 1)
                for t in range(BLK):
                    ag = nc.vector.bn_aggr(mv[:, t, :], stats[:, t, :])
                ag.then_inc(var_done, 1)

            def normalise(n, b):
                dve.wait_ge(sd_done, n + 1)
                nc.vector.reciprocal(rstd[:], rstd[:]).then_inc(rstd_done, 1)
                dve.wait_ge(rstd_done, n + 1)
                for t in range(BLK):
                    xn = nc.vector.tensor_scalar(xin[b][:, t, :], xin[b][:, t, :], mv[:, t, 0:1],
                                                 rstd[:, t:t + 1], ALU.subtract, ALU.mult)
                xn.then_inc(xn_done, 1)

            def beta_out(n, b):
                dve.wait_ge(beta_exp, n + 1)
                kept = ba[:, n] if isinstance(n, int) else ba[:, bass.ds(n, 1)]
                logit = ps_ba[:, 0:BLK * 2 * H].rearrange("p (t h) -> p t h", t=BLK)
                nc.vector.tensor_copy(kept, logit if isinstance(n, int) else logit.unsqueeze(1)).then_inc(ba_sb, 1)
                nc.vector.tensor_scalar(beta[b][:], beta[b][:], 1.0, None, ALU.add).then_inc(soft, 1)
                dve.wait_ge(soft, n + 1)
                nc.vector.reciprocal(beta[b][:], beta[b][:]).then_inc(beta_done, 1)

            def gates_out():
                step = [BLOCKS + 1]

                def link(ins):
                    step[0] += 1
                    ins.then_inc(soft, 1)
                    dve.wait_ge(soft, step[0])

                every = ba[:, 0:BLOCKS].rearrange("p n t h -> p (n t) h")
                dve.wait_ge(ba_sb, BLOCKS + 1)
                link(nc.vector.tensor_tensor(sm[:, 3], every[:, :, H:2 * H],
                                             head_row[:, 1:2, :].broadcast_to([P, TILES, H]), ALU.add))
                nc.vector.scalar_tensor_tensor(sm[:, 1], sm[:, 3], -1.0, sm[:, 3], ALU.mult, ALU.max
                                               ).then_inc(z_abs, 1)
                dve.wait_ge(exps_done, 2)
                link(nc.vector.tensor_scalar(sm[:, 0], sm[:, 0], 1.0, None, ALU.add))
                nc.vector.reciprocal(gb[:, :, H:2 * H], sm[:, 0]).then_inc(gb_done, 1)
                link(nc.vector.tensor_scalar(sm[:, 4], sm[:, 2], 2.0, None, ALU.add))
                link(nc.vector.reciprocal(sm[:, 4], sm[:, 4]))
                link(nc.vector.tensor_tensor(sm[:, 4], sm[:, 4], sm[:, 2], ALU.mult))
                link(nc.vector.tensor_tensor(sm[:, 5], sm[:, 4], sm[:, 4], ALU.mult))
                link(nc.vector.tensor_scalar(sm[:, 2], sm[:, 5], 2.0 / 15, None, ALU.mult))
                for c in (13, 11, 9, 7, 5, 3):
                    link(nc.vector.scalar_tensor_tensor(sm[:, 2], sm[:, 2], 2.0 / c, sm[:, 5], ALU.add, ALU.mult))
                link(nc.vector.scalar_tensor_tensor(sm[:, 2], sm[:, 2], 2.0, sm[:, 4], ALU.add, ALU.mult))
                link(nc.vector.scalar_tensor_tensor(sm[:, 2], sm[:, 3], 0.0, sm[:, 2], ALU.max, ALU.add))
                link(nc.vector.tensor_tensor(sm[:, 2], sm[:, 2],
                                             neg_rate[:].unsqueeze(1).broadcast_to([P, TILES, H]), ALU.mult))
                nc.vector.tensor_scalar(gb[:, :, 0:H], sm[:, 2], DECAY_FLOOR, None, ALU.max
                                        ).then_inc(gb_done, 1)

            for b in range(2):
                moments(b, b, 0)
                normalise(b, b)
            beta_out(0, 0)
            with dve.Fori(0, BLOCKS // 2) as i:
                for b in range(2):
                    n = i * 2 + b
                    if b:
                        dve.wait_ge(hist_set, i + 1)
                    for m in range(NCT):
                        dve.wait_ge(proj_taken[m % 2], n * (NCT // 2) + m // 2 + 1)
                        for k in range(TAPS - 1):
                            if k:
                                dve.wait_ge(conv_step, (n * NCT + m) * (TAPS - 2) + k)
                            y = nc.vector.scalar_tensor_tensor(conv_y[m % 4][:], conv_in[b][:, m, k:k + BT],
                                                               taps[:, m, k:k + 1], conv_y[m % 4][:],
                                                               ALU.mult, ALU.add)
                            y.then_inc(conv_step if k < TAPS - 2 else conv_done, 1)
                        if m == 3:
                            moments(n + 2, b, i + 1)
                    dve.wait_ge(sq_done, n * 2 + 2)
                    dve.wait_ge(scaled, n)
                    nc.vector.tensor_reduce(ss[:], sq[:].rearrange("p t (h d) -> p t h d", d=HK), AX_X,
                                            ALU.add).then_inc(ss_done, 1)
                    dve.wait_ge(norm_sd, n + 1)
                    nc.vector.reciprocal(rn[:], rn[:]).then_inc(norm_r, 1)
                    dve.wait_ge(norm_r, n * 2 + 1)
                    nc.vector.tensor_scalar(rn[:, :, 0:H], rn[:, :, 0:H], HK ** -0.5, None, ALU.mult
                                            ).then_inc(norm_r, 1)
                    normalise(n + 2, b)
                    beta_out(n + 1, 1 - b)
            gates_out()




def delta_stage(nc, a, s):
    with ExitStack() as ctx:
        sb = lambda n, shape: ctx.enter_context(nc.sbuf_tensor(n, shape, F32))
        bank = lambda n: ctx.enter_context(nc.psum_tensor(n, [P, 512], F32))
        sem = ctx.enter_context(stage_semaphores(nc))
        G = range(BATCH)
        per = lambda n, shape: [sb(f"{n}{b}", shape) for b in G]

        con = s["con"]
        w_o = sb("w_o", [P, H, D])
        norm_w = sb("norm_w", [P, 1])
        eps = sb("eps2", [P, 1])
        qk = per("qk", [P, 2 * DK])
        vb = per("vb", [P, DV])
        gt = per("gt", [P, DV])
        gbt = per("gbt", [P, 2 * H])
        xr = per("xr", [P, D])
        gam = per("gam", [P, 3 * H])
        gC2 = per("gC2", [P, 2])
        nbg = per("nbg", [P, H])
        g_gt = per("g_gt", [P, H, P])
        E = per("E", [P, H, P])
        Em = per("Em", [P, H, P])
        Eb = per("Eb", [P, H, P])
        qg = per("qg", [P, DK])
        ke = per("ke", [P, DK])
        qkT = per("qkT", [P, 4, P])
        qgT = per("qgT", [P, 2, P])
        PT = per("PT", [P, H, P])
        Y = per("Y", [P, H, P])
        bb = per("bb", [P, H, P])
        u = per("u", [P, H, P])
        S = per("S", [P, 2, HV])
        ssum = per("ssum", [P, H])
        stats = per("stats2_", [P, 6])
        mv = per("mv2_", [P, 2])
        rstd = per("rstd2_", [P, 1])
        x1t = per("x1t", [P, D])
        X, Qs, Pm, Am, og, ogT = g_gt, E, Em, Eb, bb, u

        A = [bank(f"psA{b}") for b in G]
        B = [bank(f"psB{b}") for b in G]

        weights_in = sem("weights_in2")
        qk_in = [sem(f"qk_in{b}") for b in G]
        v_in = [sem(f"v_in{b}") for b in G]
        gx_in = [sem(f"gx_in{b}") for b in G]
        x1_out = [sem(f"x1_out{b}") for b in G]
        names = ("set_up g_gt_done cum_done gam_done D_done E_done Em_done Eb_done nbg_done qg_done ke_done "
                 "qkT_done qkT_sb qgT_done qgT_sb kkqk_done am_done pm_done x0_half x0_done pT_done pT_sb y0_done "
                 "y0_sb lev_q lev_qs lev_y lev_ys lev_x lev_xs ks_done bb_done u_done u_sb o_done s_done "
                 "sq_done rs_sd rs_done og_done ogT_done ogT_sb wo_done y_done st_done st_seen mv_done sd_done "
                 "r_done x1_done").split()
        (set_up, g_gt_done, cum_done, gam_done, D_done, E_done, Em_done, Eb_done, nbg_done, qg_done, ke_done,
         qkT_done, qkT_sb, qgT_done, qgT_sb, kkqk_done, am_done, pm_done, x0_half, x0_done, pT_done, pT_sb, y0_done,
         y0_sb, lev_q, lev_qs, lev_y, lev_ys, lev_x, lev_xs, ks_done, bb_done, u_done, u_sb, o_done, s_done,
         sq_done, rs_sd, rs_done, og_done, ogT_done, ogT_sb, wo_done, y_done, st_done, st_seen, mv_done, sd_done,
         r_done, x1_done) = [sem(f"d_{n}") for n in names]

        block = ctx.enter_context(nc.Block())
        MERGES = range(1, LEVELS)
        NL = LEVELS - 1
        head = lambda slot: 2 * (slot % 2) + slot // 2
        ident = con[:, C_ID:C_ID + P]
        rows = lambda slot: slice(HK * (slot // 2), HK * (slot // 2) + HK)
        by_slot = lambda t: t.rearrange("p (t r) -> p r t", r=2)
        mask4 = lambda lo: con[:, lo:lo + P].unsqueeze(1).broadcast_to([P, H, P])
        HP = P // 2
        right = lambda t, lev: t[:].rearrange("p k (m w j) -> p k m w j", w=2, j=2 ** lev)[:, :, :, 1, :]
        split = lambda t: t[:].rearrange("p (r t) j -> p r t j", r=2)

        @block.sync
        def _(sp):
            sp.dma_start(w_o[:], a["L0_attn_Wo"].rearrange("(h p) n -> p h n", p=P)).then_inc(weights_in, 16)
            sp.dma_start(norm_w[:], a["L0_attn_norm_w"].rearrange("(p a) -> p a", a=1)).then_inc(weights_in, 16)
            for b in G:
                sp.dma_start(gbt[b][:], s["gb"][b * CHUNKS]).then_inc(qk_in[b], 16)
                sp.dma_start(qk[b][:], s["qkvg"][b * CHUNKS, :, 0:2 * DK]).then_inc(qk_in[b], 16)
            with sp.Fori(0, CHUNKS) as c:
                sp.wait_ge(bb_done, c * BATCH)
                for b in G:
                    sp.dma_start(vb[b][:], s["qkvg"][c + b * CHUNKS, :, 2 * DK:QKV]).then_inc(v_in[b], 16)
                sp.wait_ge(og_done, c * BATCH)
                sp.wait_ge(y_done, c * BATCH)
                for b in G:
                    sp.dma_start(gt[b][:], s["qkvg"][c + b * CHUNKS, :, QKV:QKV + DV]).then_inc(gx_in[b], 16)
                    sp.dma_start(xr[b][:], a["x"].rearrange("b (c p) d -> b c p d", p=P)[b, c]).then_inc(gx_in[b], 16)
                sp.wait_ge(Eb_done, (c + 1) * BATCH)
                sp.wait_ge(ke_done, (c + 1) * BATCH)
                sp.wait_ge(nbg_done, (c + 1) * BATCH)
                sp.wait_ge(qkT_done, (c + 1) * BATCH)
                for b in G:
                    sp.dma_start(gbt[b][:], s["gb"][(c + 1) % CHUNKS + b * CHUNKS]).then_inc(qk_in[b], 16)
                    sp.dma_start(qk[b][:], s["qkvg"][(c + 1) % CHUNKS + b * CHUNKS, :, 0:2 * DK]
                                 ).then_inc(qk_in[b], 16)

        @block.gpsimd
        def _(pool):
            nc.gpsimd.memset(eps[:], EPS).then_inc(set_up, 1)
            for b in G:
                nc.gpsimd.memset(S[b][:], 0.0).then_inc(set_up, 1)
            pool.wait_ge(weights_in, 32)

            def masked_decays(b, c):
                pool.wait_ge(qk_in[b], c * 32 + 32)
                pool.wait_ge(lev_y, c * NL * BATCH)
                nc.gpsimd.tensor_tensor(split(g_gt[b]),
                                        by_slot(gbt[b][:, 0:H]).unsqueeze(3).broadcast_to([P, 2, 2, P]),
                                        con[:, C_GT:C_GT + P].unsqueeze(1).unsqueeze(1).broadcast_to([P, 2, 2, P]),
                                        ALU.mult).then_inc(g_gt_done, 1)

            for b in G:
                masked_decays(b, 0)
            with pool.Fori(0, CHUNKS) as c:
                for b in G:
                    pool.wait_ge(gam_done, c * BATCH + b + 1)
                    pool.wait_ge(qgT_done, c * BATCH)
                    nc.gpsimd.tensor_tensor(qg[b][:].rearrange("p (h d) -> p h d", d=HK),
                                            qk[b][:, 0:DK].rearrange("p (h d) -> p h d", d=HK),
                                            gam[b][:, 0:H].unsqueeze(2).broadcast_to([P, H, HK]),
                                            ALU.mult).then_inc(qg_done, 1)
                for b in G:
                    pool.wait_ge(E_done, c * BATCH + b + 1)
                    pool.wait_ge(lev_q, c * NL * BATCH)
                    nc.gpsimd.tensor_tensor(split(Eb[b]), split(E[b]),
                                            by_slot(gbt[b][:, H:2 * H]).unsqueeze(3).broadcast_to([P, 2, 2, P]),
                                            ALU.mult).then_inc(Eb_done, 1)
                for b in G:
                    pool.wait_ge(am_done, c * BATCH + b + 1)
                    nc.gpsimd.tensor_tensor(X[b][:], Am[b][:], mask4(C_NM0), ALU.mult).then_inc(x0_half, 1)
                for b in G:
                    pool.wait_ge(o_done, c * BATCH)
                    nc.gpsimd.tensor_tensor(ke[b][:].rearrange("p (h d) -> p h d", d=HK),
                                            qk[b][:, DK:2 * DK].rearrange("p (h d) -> p h d", d=HK),
                                            gam[b][:, H:2 * H].unsqueeze(2).broadcast_to([P, H, HK]),
                                            ALU.mult).then_inc(ke_done, 1)
                for b in G:
                    masked_decays(b, c + 1)
                for b in G:
                    pool.wait_ge(x1_done, c * BATCH + b + 1)
                    pool.dma_start(s["x1"][c + b * CHUNKS], x1t[b][:]).then_inc(x1_out[b], 16)
            for b in G:
                pool.wait_ge(x1_out[b], 16 * CHUNKS)

        @block.tensor
        def _(pe):
            pe.wait_ge(weights_in, 32)
            pe.wait_ge(set_up, 1 + BATCH)

            def decay_sums(b, c):
                pe.wait_ge(g_gt_done, c * BATCH + b + 1)
                pe.wait_ge(ogT_sb, (c - 1) * BATCH + b + 1) if not isinstance(c, int) else None
                pe.matmul(A[b][:], con[:, C_LE:C_LE + P], g_gt[b][:], start=True, stop=True).then_inc(D_done, 1)

            for b in G:
                decay_sums(b, 0)
            with pe.Fori(0, CHUNKS) as c:
                at = lambda b: c * BATCH + b + 1
                for b in G:
                    pe.wait_ge(qk_in[b], c * 32 + 32)
                    pe.wait_ge(y_done, c * BATCH)
                    for k, lo in enumerate((C_LE, C_GT, C_ONE)):
                        mm = pe.matmul(B[b][:, k * H:(k + 1) * H], con[:, lo:lo + P], gbt[b][:, 0:H],
                                       start=True, stop=True)
                    mm.then_inc(cum_done, 1)
                for b in G:
                    pe.wait_ge(gam_done, at(b))
                    for k in range(4):
                        mm = pe.transpose(B[b][:, k * P:(k + 1) * P], qk[b][:, k * P:(k + 1) * P], ident)
                    mm.then_inc(qkT_done, 1)
                for b in G:
                    pe.wait_ge(E_done, at(b))
                    pe.wait_ge(qg_done, at(b))
                    for k in range(2):
                        mm = pe.transpose(A[b][:, k * P:(k + 1) * P], qg[b][:, k * P:(k + 1) * P], ident)
                    mm.then_inc(qgT_done, 1)
                for b in G:
                    pe.wait_ge(qkT_sb, at(b))
                    pe.wait_ge(qgT_sb, at(b))
                    for w in (2, 0):
                        for t in range(2):
                            for r, bk in enumerate((A[b], B[b])):
                                lo = (t if w else 2 + t) * P
                                mm = pe.matmul(bk[:, lo:lo + P], qkT[b][rows(2 * r), w + t, :],
                                               qkT[b][rows(2 * r), 2 + t, :], start=True, stop=True)
                    mm.then_inc(kkqk_done, 1)
                for b in G:
                    pe.wait_ge(pm_done, at(b))
                    for k in range(H):
                        mm = pe.transpose(B[b][:, k * P:(k + 1) * P], Pm[b][:, k, :], ident)
                    mm.then_inc(pT_done, 1)
                for b in G:
                    pe.wait_ge(x0_done, at(b))
                    for k in range(H):
                        mm = pe.transpose(A[b][:, k * P:(k + 1) * P], X[b][:, k, :], ident)
                    mm.then_inc(y0_done, 1)
                for lev in MERGES:
                    lat = lambda b, lev=lev: (c * NL + (lev - 1)) * BATCH + b + 1
                    for b in G:
                        if lev == 1:
                            pe.wait_ge(y0_sb, at(b))
                        else:
                            pe.wait_ge(lev_ys, lat(b) - BATCH)
                            pe.wait_ge(lev_xs, (c * (NL - 1) + (lev - 2)) * BATCH + b + 1)
                        for k in range(H):
                            mm = pe.matmul(A[b][:, k * P:(k + 1) * P], Am[b][:, k, :], Y[b][:, k, :],
                                           start=True, stop=True)
                        mm.then_inc(lev_q, 1)
                    for b in G:
                        pe.wait_ge(lev_qs, lat(b))
                        if lev == 1:
                            pe.wait_ge(pT_sb, at(b))
                        for k in range(H):
                            mm = pe.matmul(B[b][:, k * HP:(k + 1) * HP], X[b][:, k, :], Qs[b][:, k, 0:HP],
                                           start=True, stop=True)
                        mm.then_inc(lev_y, 1)
                    if lev < NL:
                        for b in G:
                            pe.wait_ge(lev_ys, lat(b))
                            for k in range(H):
                                mm = pe.transpose(A[b][:, k * P:(k + 1) * P], Y[b][:, k, :], ident)
                            mm.then_inc(lev_x, 1)
                for b in G:
                    pe.wait_ge(lev_ys, (c + 1) * NL * BATCH - BATCH + b + 1)
                    pe.wait_ge(s_done, c * BATCH)
                    for t in range(2):
                        for r, bk in enumerate((A[b], B[b])):
                            mm = pe.matmul(bk[:, t * P:(t + 1) * P], qkT[b][rows(2 * r), 2 + t, :],
                                           S[b][rows(2 * r), t, :], start=True, stop=True)
                    mm.then_inc(ks_done, 1)
                for b in G:
                    pe.wait_ge(bb_done, at(b))
                    for k in range(H):
                        mm = pe.matmul(A[b][:, k * P:(k + 1) * P], Y[b][:, k, :], bb[b][:, k, :],
                                       start=True, stop=True)
                    mm.then_inc(u_done, 1)
                for b in G:
                    pe.wait_ge(u_sb, at(b))
                    pe.wait_ge(ke_done, at(b))
                    for t in range(2):
                        for r, bk in enumerate((A[b], B[b])):
                            pe.matmul(bk[:, t * P:(t + 1) * P], qgT[b][rows(2 * r), t, :],
                                      S[b][rows(2 * r), t, :], start=True, stop=False)
                            pe.matmul(bk[:, t * P:(t + 1) * P], PT[b][:, 2 * r + t, :], u[b][:, 2 * r + t, :],
                                      start=False, stop=True)
                    for t in range(2):
                        for r in range(2):
                            h = 2 * t + r
                            mm = pe.matmul(B[b][rows(2 * r), 2 * P + t * P:2 * P + (t + 1) * P],
                                           ke[b][:, h * HK:(h + 1) * HK], u[b][:, 2 * r + t, :],
                                           start=True, stop=True)
                    mm.then_inc(o_done, 1)
                for b in G:
                    pe.wait_ge(og_done, at(b))
                    for k in range(H):
                        mm = pe.transpose(A[b][:, k * P:(k + 1) * P], og[b][:, k, :], ident)
                    mm.then_inc(ogT_done, 1)
                for b in G:
                    pe.wait_ge(ogT_sb, at(b))
                    for k in range(H):
                        mm = pe.matmul(B[b][:, 0:D], ogT[b][:, k, :], w_o[:, head(k), :],
                                       start=k == 0, stop=k == H - 1)
                    mm.then_inc(wo_done, 1)
                    decay_sums(b, c + 1)

        @block.scalar
        def _(act):
            act.wait_ge(weights_in, 32)
            act.wait_ge(set_up, 1 + BATCH)
            with act.Fori(0, CHUNKS) as c:
                at = lambda b: c * BATCH + b + 1
                flat = lambda t: t[:].rearrange("p k j -> p (k j)")
                for b in G:
                    act.wait_ge(cum_done, at(b))
                    act.wait_ge(ke_done, c * BATCH)
                    act.wait_ge(s_done, c * BATCH)
                    nc.scalar.activation(gam[b][:], B[b][:, 0:3 * H], ACT.Exp)
                    tot = B[b][:, 2 * H:3 * H].rearrange("p (t r) -> p r t", r=2)
                    for r in range(2):
                        e = nc.scalar.activation(gC2[b][rows(2 * r), :], tot[rows(2 * r), r, :], ACT.Exp)
                    e.then_inc(gam_done, 1)
                for b in G:
                    act.wait_ge(D_done, at(b))
                    nc.scalar.activation(flat(E[b]), A[b][:], ACT.Exp).then_inc(E_done, 1)
                for b in G:
                    act.wait_ge(qkT_done, at(b))
                    nc.scalar.activation(flat(qkT[b]), B[b][:], ACT.Copy).then_inc(qkT_sb, 1)
                for b in G:
                    act.wait_ge(qgT_done, at(b))
                    nc.scalar.activation(flat(qgT[b]), A[b][:, 0:2 * P], ACT.Copy).then_inc(qgT_sb, 1)
                for b in G:
                    act.wait_ge(pT_done, at(b))
                    nc.scalar.activation(flat(PT[b]), B[b][:], ACT.Copy).then_inc(pT_sb, 1)
                for b in G:
                    act.wait_ge(y0_done, at(b))
                    nc.scalar.activation(flat(Y[b]), A[b][:], ACT.Copy).then_inc(y0_sb, 1)
                for lev in range(1, NL):
                    for b in G:
                        act.wait_ge(lev_x, (c * (NL - 1) + (lev - 1)) * BATCH + b + 1)
                        nc.scalar.activation(flat(X[b]), A[b][:], ACT.Copy).then_inc(lev_xs, 1)
                for b in G:
                    act.wait_ge(u_done, at(b))
                    nc.scalar.activation(flat(u[b]), A[b][:], ACT.Copy).then_inc(u_sb, 1)
                for b in G:
                    act.wait_ge(o_done, at(b))
                    act.wait_ge(s_done, at(b))
                    for k in range(H):
                        bk = (A, B)[k // 2][b]
                        q = nc.scalar.activation(og[b][:, k, :], bk[:, (k % 2) * P:(k % 2 + 1) * P], ACT.Square,
                                                 accum_out=ssum[b][:, k:k + 1])
                    q.then_inc(sq_done, 1)
                    act.wait_ge(sq_done, at(b))
                    nc.scalar.activation(ssum[b][:], ssum[b][:], ACT.Sqrt, bias=eps[:, 0:1], scale=1.0 / HV
                                         ).then_inc(rs_sd, 1)
                for b in G:
                    act.wait_ge(ogT_done, at(b))
                    nc.scalar.activation(flat(ogT[b]), A[b][:], ACT.Copy, scale=norm_w[:, 0:1]).then_inc(ogT_sb, 1)
                for b in G:
                    act.wait_ge(mv_done, at(b))
                    nc.scalar.activation(rstd[b][:], mv[b][:, 1:2], ACT.Sqrt, bias=eps[:, 0:1]).then_inc(sd_done, 1)

        @block.vector
        def _(dve):
            dve.wait_ge(weights_in, 32)
            with dve.Fori(0, CHUNKS) as c:
                at = lambda b: c * BATCH + b + 1
                for b in G:
                    dve.wait_ge(gam_done, at(b))
                    nc.vector.scalar_tensor_tensor(nbg[b][:], gam[b][:, 0:H], -1.0, gbt[b][:, H:2 * H],
                                                   ALU.mult, ALU.mult).then_inc(nbg_done, 1)
                for b in G:
                    dve.wait_ge(E_done, at(b))
                    dve.wait_ge(pT_done, c * BATCH)
                    nc.vector.tensor_tensor(Em[b][:], E[b][:], mask4(C_GE), ALU.mult).then_inc(Em_done, 1)
                for b in G:
                    dve.wait_ge(kkqk_done, at(b))
                    dve.wait_ge(Eb_done, at(b))
                    for r, bk in enumerate((A[b], B[b])):
                        m = nc.vector.tensor_tensor(Am[b][:, 2 * r:2 * r + 2, :],
                                                    bk[:, 0:2 * P].rearrange("p (t j) -> p t j", t=2),
                                                    Eb[b][:, 2 * r:2 * r + 2, :], ALU.mult)
                    m.then_inc(am_done, 1)
                    dve.wait_ge(Em_done, at(b))
                    for r, bk in enumerate((A[b], B[b])):
                        m = nc.vector.tensor_tensor(Pm[b][:, 2 * r:2 * r + 2, :],
                                                    bk[:, 2 * P:4 * P].rearrange("p (t j) -> p t j", t=2),
                                                    Em[b][:, 2 * r:2 * r + 2, :], ALU.mult)
                    m.then_inc(pm_done, 1)
                for b in G:
                    dve.wait_ge(x0_half, at(b))
                    nc.vector.tensor_tensor(X[b][:], X[b][:], mask4(C_ID), ALU.add).then_inc(x0_done, 1)
                for lev in MERGES:
                    lat = lambda b, lev=lev: (c * NL + (lev - 1)) * BATCH + b + 1
                    for b in G:
                        dve.wait_ge(lev_q, lat(b))
                        m = C_LEV + (lev - 1) * HP
                        nc.vector.tensor_tensor(Qs[b][:, :, 0:HP].rearrange("p k (m j) -> p k m j", j=2 ** lev),
                                                A[b][:].rearrange("p (k m w j) -> p k m w j", k=H, w=2,
                                                                  j=2 ** lev)[:, :, :, 1, :],
                                                con[:, m:m + HP].rearrange("p (m j) -> p m j", j=2 ** lev).unsqueeze(1)
                                                .broadcast_to([P, H, HP // 2 ** lev, 2 ** lev]), ALU.mult
                                                ).then_inc(lev_qs, 1)
                    for b in G:
                        dve.wait_ge(lev_y, lat(b))
                        y = right(Y[b], lev)
                        nc.vector.tensor_tensor(y, y, B[b][:, 0:H * HP].rearrange("p (k m j) -> p k m j", k=H,
                                                                                 j=2 ** lev),
                                                ALU.subtract).then_inc(lev_ys, 1)
                for b in G:
                    dve.wait_ge(ks_done, at(b))
                    dve.wait_ge(v_in[b], c * 16 + 16)
                    dve.wait_ge(ogT_done, c * BATCH)
                    dve.wait_ge(nbg_done, at(b))
                    for k in range(H):
                        bk, h = (A, B)[k // 2][b], head(k)
                        m = nc.vector.scalar_tensor_tensor(bb[b][:, k, :], bk[:, (k % 2) * P:(k % 2 + 1) * P],
                                                           nbg[b][:, h:h + 1], vb[b][:, h * HV:(h + 1) * HV],
                                                           ALU.mult, ALU.add)
                    m.then_inc(bb_done, 1)

                def new_state(b):
                    dve.wait_ge(o_done, at(b))
                    for t in range(2):
                        m = nc.vector.scalar_tensor_tensor(S[b][:, t, :], S[b][:, t, :], gC2[b][:, t:t + 1],
                                                           B[b][:, 2 * P + t * P:2 * P + (t + 1) * P],
                                                           ALU.mult, ALU.add)
                    m.then_inc(s_done, 1)

                new_state(0)
                for b in G:
                    if b < BATCH - 1:
                        new_state(b + 1)
                    dve.wait_ge(rs_sd, at(b))
                    nc.vector.reciprocal(ssum[b][:], ssum[b][:]).then_inc(rs_done, 1)
                    dve.wait_ge(rs_done, at(b))
                    dve.wait_ge(gx_in[b], c * 32 + 32)
                    for k in range(H):
                        bk, h = (A, B)[k // 2][b], head(k)
                        m = nc.vector.scalar_tensor_tensor(og[b][:, k, :], bk[:, (k % 2) * P:(k % 2 + 1) * P],
                                                           ssum[b][:, k:k + 1], gt[b][:, h * HV:(h + 1) * HV],
                                                           ALU.mult, ALU.mult)
                    m.then_inc(og_done, 1)
                for step in range(BATCH + 2):
                    if step < BATCH:
                        b = step
                        dve.wait_ge(wo_done, at(b))
                        dve.wait_ge(x1_out[b], c * 16)
                        nc.vector.scalar_tensor_tensor(x1t[b][:], xr[b][:], 2.0, B[b][:, 0:D], ALU.mult, ALU.add
                                                       ).then_inc(y_done, 1)
                    if 1 <= step <= BATCH:
                        b = step - 1
                        dve.wait_ge(y_done, at(b))
                        nc.vector.bn_stats(stats[b][:], x1t[b][:]).then_inc(st_done, 1)
                    if step >= 2:
                        b = step - 2
                        dve.wait_ge(st_done, at(b))
                        nc.vector.sem_inc(st_seen, 1)
                        nc.vector.bn_aggr(mv[b][:], stats[b][:]).then_inc(mv_done, 1)
                for step in range(BATCH + 1):
                    if step < BATCH:
                        b = step
                        dve.wait_ge(sd_done, at(b))
                        nc.vector.reciprocal(rstd[b][:], rstd[b][:]).then_inc(r_done, 1)
                    if step > 0:
                        b = step - 1
                        dve.wait_ge(r_done, at(b))
                        nc.vector.tensor_scalar(x1t[b][:], x1t[b][:], mv[b][:, 0:1], rstd[b][:, 0:1],
                                                ALU.subtract, ALU.mult).then_inc(x1_done, 1)


def context_stage(nc, a, s):
    with ExitStack() as ctx:
        sb = lambda n, shape: ctx.enter_context(nc.sbuf_tensor(n, shape, F32))
        bank = lambda n: ctx.enter_context(nc.psum_tensor(n, [P, 512], F32))
        sem = ctx.enter_context(stage_semaphores(nc))
        XJ = XW // P
        G = range(BATCH)
        per = lambda n, shape: [sb(f"{n}{b}", shape) for b in G]
        con = s["con"]
        w_k = sb("xw_k", [P, KD, XW])
        w_v = sb("xw_v", [P, KD, XW])
        nw = sb("xnw", [P, 2])
        eps = sb("eps3", [P, 1])
        cx = sb("cx", [P, BATCH, D])
        cxT = sb("cxT", [P, BATCH, KD, CTX])
        k_sb = per("k_sb", [P, XW])
        k_sq = sb("k_sq", [P, XW])
        v_sb = per("v_sb", [P, XW])
        ss = per("ss3_", [P, XH])
        kT = per("kT3_", [P, XJ, 2, KC])
        ctx_len = ctx.enter_context(nc.sbuf_tensor("ctx_len", [P, BATCH], I32))
        len_f = sb("len_f", [P, BATCH])
        valid = sb("valid", [P, BATCH])
        madd = sb("madd3", [P, BATCH, CTX])
        ps_c = [bank(f"ps_c{h}") for h in range(2)]
        ps_k = [bank(f"ps_k{h}") for h in range(2)]
        ps_v = [bank(f"ps_v{h}") for h in range(2)]
        ps_kT = [bank(f"ps_kT{h}") for h in range(2)]
        (ctx_in, weights_in, wv_in, set_up, nw_done, cxT_done, cxT_sb, k_done, v_done, k_out, sq_done, ss_done,
         sd_done, r_done, rm_done, len_done, valid_done, m_half, madd_done, k_scaled, kT_done, kT_sb, v_sb_done,
         stored) = [
            sem(f"c_{n}") for n in
            ("ctx_in weights_in wv_in set_up nw_done cxT_done cxT_sb k_done v_done k_out sq_done ss_done sd_done "
             "r_done rm_done len_done valid_done m_half madd_done k_scaled kT_done kT_sb v_sb_done stored").split()]
        block = ctx.enter_context(nc.Block())

        @block.sync
        def _(sp):
            sp.dma_start(cx[0:CTX], a["ctx_1024"].rearrange("b p d -> p b d")).then_inc(ctx_in, 16)
            sp.dma_start(w_k[:], a["L0_xattn_Wk"].rearrange("(k p) n -> p k n", p=P)).then_inc(weights_in, 16)
            sp.dma_start(ctx_len[:], a["_lenS2"].rearrange("(a b) -> a b", a=1).broadcast_to([P, BATCH])
                         ).then_inc(weights_in, 16)
            for k, w in enumerate((a["L0_xattn_q_norm_w"], a["L0_xattn_k_norm_w"])):
                for r in range(2):
                    sp.dma_start(nw[r * XD:(r + 1) * XD, k:k + 1], w.rearrange("(p a) -> p a", a=1)
                                 ).then_inc(weights_in, 16)
            sp.dma_start(w_v[:], a["L0_xattn_Wv"].rearrange("(k p) n -> p k n", p=P)).then_inc(wv_in, 16)
            sp.wait_ge(madd_done, 1)
            sp.dma_start(s["madd"].rearrange("b p c -> p b c"), madd[:]).then_inc(stored, 16)
            for b in G:
                sp.wait_ge(v_sb_done, 2 * b + 2)
                sp.dma_start(s["v"][b], v_sb[b][0:CTX, :]).then_inc(stored, 16)
            for b in G:
                sp.wait_ge(kT_sb, 2 * b + 2)
                sp.dma_start(s["kT"][b], kT[b][:]).then_inc(stored, 16)
            sp.wait_ge(stored, 16 * (1 + 2 * BATCH))

        @block.gpsimd
        def _(pool):
            nc.gpsimd.memset(eps[:], EPS).then_inc(set_up, 1)
            for b in G:
                nc.gpsimd.memset(kT[b][:], 0.0).then_inc(set_up, 1)

        @block.tensor
        def _(pe):
            pe.wait_ge(ctx_in, 16)
            for b in G:
                for c in range(KD):
                    lo = ((b % 2) * KD + c) * P
                    mm = pe.transpose(ps_c[b // 2][:, lo:lo + CTX], cx[0:CTX, b, c * P:(c + 1) * P],
                                      con[0:CTX, C_ID:C_ID + CTX])
                if b % 2:
                    mm.then_inc(cxT_done, 1)
            pe.wait_ge(weights_in, 16 * 6)
            pe.wait_ge(cxT_sb, 2)
            for b in G:
                if b:
                    pe.wait_ge(k_out, 2 * b)
                for h in range(2):
                    for c in range(KD):
                        mm = pe.matmul(ps_k[h][0:CTX, :], cxT[:, b, c, :], w_k[:, c, h * 512:(h + 1) * 512],
                                       start=c == 0, stop=c == KD - 1)
                mm.then_inc(k_done, 1)
                if b == 0:
                    pe.wait_ge(wv_in, 16)
                else:
                    pe.wait_ge(v_sb_done, 2 * b)
                for h in range(2):
                    for c in range(KD):
                        mm = pe.matmul(ps_v[h][0:CTX, :], cxT[:, b, c, :], w_v[:, c, h * 512:(h + 1) * 512],
                                       start=c == 0, stop=c == KD - 1)
                mm.then_inc(v_done, 1)
            for b in G:
                pe.wait_ge(k_scaled, b + 1)
                if b:
                    pe.wait_ge(kT_sb, 2 * b)
                for j in range(XJ):
                    mm = pe.transpose(ps_kT[j // 4][:, (j % 4) * P:(j % 4) * P + CTX],
                                      k_sb[b][0:CTX, j * P:(j + 1) * P], con[0:CTX, C_ID:C_ID + CTX])
                mm.then_inc(kT_done, 1)

        @block.scalar
        def _(act):
            act.wait_ge(set_up, 1 + BATCH)
            act.wait_ge(nw_done, 1)
            for h in range(2):
                act.wait_ge(cxT_done, h + 1)
                nc.scalar.activation(cxT[:, 2 * h:2 * h + 2],
                                     ps_c[h][:].rearrange("p (b c j) -> p b c j", b=2, c=KD)[:, :, :, 0:CTX],
                                     ACT.Copy).then_inc(cxT_sb, 1)
            for b in G:
                act.wait_ge(k_done, b + 1)
                for h in range(2):
                    nc.scalar.activation(k_sb[b][0:CTX, h * 512:(h + 1) * 512], ps_k[h][0:CTX, :], ACT.Copy
                                         ).then_inc(k_out, 1)
                act.wait_ge(k_out, 2 * b + 2)
                if b:
                    act.wait_ge(ss_done, b)
                nc.scalar.activation(k_sq[0:CTX, :], k_sb[b][0:CTX, :], ACT.Square).then_inc(sq_done, 1)
                act.wait_ge(v_done, b + 1)
                for h in range(2):
                    nc.scalar.activation(v_sb[b][0:CTX, h * 512:(h + 1) * 512], ps_v[h][0:CTX, :], ACT.Copy
                                         ).then_inc(v_sb_done, 1)
                act.wait_ge(ss_done, b + 1)
                nc.scalar.activation(ss[b][0:CTX, :], ss[b][0:CTX, :], ACT.Sqrt, bias=eps[0:CTX, 0:1], scale=1.0 / XD
                                     ).then_inc(sd_done, 1)
            for b in G:
                act.wait_ge(kT_done, b + 1)
                for h in range(2):
                    for r in range(2):
                        rows = slice(r * XD, (r + 1) * XD)
                        y = nc.scalar.activation(kT[b][rows, 4 * h:4 * h + 4, r, 0:CTX],
                                                 ps_kT[h][rows, :].rearrange("p (c j) -> p c j", c=4)[:, :, 0:CTX],
                                                 ACT.Copy, scale=nw[rows, 0:1])
                    y.then_inc(kT_sb, 1)

        @block.vector
        def _(dve):
            dve.wait_ge(weights_in, 16 * 6)
            nc.vector.tensor_tensor(nw[:, 0:1], nw[:, 0:1], nw[:, 1:2], ALU.mult).then_inc(nw_done, 1)
            nc.vector.tensor_scalar(len_f[:], ctx_len[:], 1.0, None, ALU.mult).then_inc(len_done, 1)
            dve.wait_ge(len_done, 1)
            nc.vector.tensor_tensor(valid[:], con[:, C_COL:C_COL + 1].broadcast_to([P, BATCH]), len_f[:], ALU.is_lt
                                    ).then_inc(valid_done, 1)
            for b in G:
                nc.vector.tensor_scalar(madd[:, b], con[:, C_IOTA:C_IOTA + CTX], len_f[:, b:b + 1], None, ALU.is_lt
                                        ).then_inc(m_half, 1)
            dve.wait_ge(m_half, BATCH)
            nc.vector.tensor_scalar(madd[:], madd[:], -1.0, 1e30, ALU.add, ALU.mult).then_inc(madd_done, 1)
            dve.wait_ge(valid_done, 1)

            def scaled(b):
                dve.wait_ge(sd_done, b + 1)
                nc.vector.reciprocal(ss[b][0:CTX, :], ss[b][0:CTX, :]).then_inc(r_done, 1)
                dve.wait_ge(r_done, b + 1)
                nc.vector.tensor_scalar(ss[b][0:CTX, :], ss[b][0:CTX, :], valid[0:CTX, b:b + 1], None, ALU.mult
                                        ).then_inc(rm_done, 1)
                dve.wait_ge(rm_done, b + 1)
                v = k_sb[b][0:CTX, :].rearrange("p (h d) -> p h d", d=XD)
                nc.vector.tensor_tensor(v, v, ss[b][0:CTX, :].unsqueeze(2).broadcast_to([CTX, XH, XD]), ALU.mult
                                        ).then_inc(k_scaled, 1)

            for b in G:
                dve.wait_ge(sq_done, b + 1)
                nc.vector.tensor_reduce(ss[b][0:CTX, :], k_sq[0:CTX, :].rearrange("p (h d) -> p h d", d=XD), AX_X,
                                        ALU.add).then_inc(ss_done, 1)
                scaled(b)


def cross_stage(nc, a, s):
    with ExitStack() as ctx:
        sb = lambda n, shape: ctx.enter_context(nc.sbuf_tensor(n, shape, F32))
        bank = lambda n: ctx.enter_context(nc.psum_tensor(n, [P, 512], F32))
        sem = ctx.enter_context(stage_semaphores(nc))
        T, R, W = range(BLK), range(2), range(BLK // 2)
        XJ = XW // P
        two = lambda n, shape: [sb(f"{n}{k}", shape) for k in R]
        x1_v = s["x1"].rearrange("(n t) p d -> n p t d", t=BLK)
        x2_v = s["x2"].rearrange("(n t) p d -> n p t d", t=BLK)
        lg_v = s["lg"].rearrange("(n t) p e -> n p t e", t=BLK)
        con = s["con"]
        w_q = sb("xw_q", [P, KD, XW])
        w_o = sb("xw_o", [P, XJ, D])
        w_r = sb("w_r", [P, KD, NE])
        empty = two("empty", [P, ROW])
        eps = sb("eps4", [P, 2])
        xq = sb("xq", [P, BLK, D])
        xr = sb("xr4", [P, BLK, D])
        kT = sb("kT4", [P, XJ, 2, KC])
        v = sb("v4", [P, XW])
        madd = sb("madd4", [P, CTX])
        x1T = sb("x1T", [P, KD, BT])
        qT = two("qT", [P, XJ, BT])
        q2 = two("q2_", [P, BT])
        ss = sb("ss4", [XH, BT])
        rq = sb("rq", [P, BLK, XH])
        sc = two("sc", [P, BLK, 2, CTX])
        mx = two("mx", [P, BLK, 2])
        nb = two("nb", [P, BLK, 2])
        den = two("den", [P, BLK, 2])
        aT = two("aT", [P, 2, BT])
        oT = sb("oT", [P, XJ, BT])
        x2t = sb("x2t", [P, BLK, D])
        x2T = sb("x2T", [P, BLK, KD, P])
        lg = sb("lg4", [P, BLK, NE])
        stats = sb("stats4", [P, BLK, 6])
        mv = sb("mv4", [P, BLK, 2])
        rstd = sb("rstd4", [P, BLK])
        S = [bank(f"xS{r}") for r in R]
        TB = [bank(f"xT{r}") for r in R]
        V, Q, SS, X = bank("xV"), bank("xQ"), bank("xSS"), bank("xX")
        weights_in = sem("x_weights_in")
        wo_in = sem("x_wo_in")
        q2_done = [sem(f"x_q2_done{k}") for k in R]
        ss_done = [sem(f"x_ss_done{k}") for k in R]
        names = ("set_up xq_in xr_in kv_in zero_out x2_out lg_out x1T_done x1T_sb q_done q_sb ss_sb ss_seen ssT_done "
                 "rq_done sc_done added mx_done nb_done exp_done den_done scaled tr_done tr_a tr_b pv_done o_sb "
                 "wo_done y_done st_done st_seen mv_done sd_done r_done x2_done x2T_done x2T_sb lg_done lg_sb").split()
        (set_up, xq_in, xr_in, kv_in, zero_out, x2_out, lg_out, x1T_done, x1T_sb, q_done, q_sb, ss_sb, ss_seen, ssT_done,
         rq_done, sc_done, added, mx_done, nb_done, exp_done, den_done, scaled, tr_done, tr_a, tr_b, pv_done, o_sb,
         wo_done, y_done, st_done, st_seen, mv_done, sd_done, r_done, x2_done, x2T_done, x2T_sb, lg_done, lg_sb) = [
            sem(f"x_{n}") for n in names]
        block = ctx.enter_context(nc.Block())
        ident = con[:, C_ID:C_ID + P]
        HX = XJ // 2
        X2T_STEP, LG_STEP = 2, 5

        def blocks(eng, turn):
            turn(0, 0, 0, True, False)
            with eng.Fori(0, BATCH - 1) as i:
                turn(i * 2 + 1, i, 1, False, False)
                turn(i * 2 + 2, i + 1, 0, False, False)
            turn(BLOCKS - 1, BATCH - 1, 1, False, True)

        @block.sync
        def _(sp):
            sp.dma_start(xq[:], x1_v[0]).then_inc(xq_in, 16)
            sp.dma_start(w_q[:], a["L0_xattn_Wq"].rearrange("(k p) n -> p k n", p=P)).then_inc(weights_in, 16)
            sp.dma_start(w_o[:], a["L0_xattn_Wo"].rearrange("(k p) n -> p k n", p=P)).then_inc(wo_in, 16)
            for c in range(KD):
                sp.dma_start(w_r[:, c, :], a["L0_ffn_router_w"].rearrange("e (k p) -> p k e", p=P)[:, c, :],
                             allow_slow_non_contiguous=True).then_inc(wo_in, 16)

            def load_kv(i):
                sp.dma_start(kT[:], s["kT"][i]).then_inc(kv_in, 16)
                sp.dma_start(v[0:CTX, :], s["v"][i]).then_inc(kv_in, 16)
                sp.dma_start(madd[:], s["madd"][i]).then_inc(kv_in, 16)

            load_kv(0)
            sp.wait_ge(set_up, 6)
            for k in R:
                sp.dma_start(s["xs"].rearrange("(m k) p d -> k p m d", k=2)[k],
                             empty[k][:].unsqueeze(1).broadcast_to([P, (FT + 1) // 2, ROW])).then_inc(zero_out, 16)
            sp.wait_ge(x1T_done, 1)
            sp.dma_start(xq[:], x1_v[1]).then_inc(xq_in, 16)
            load_experts_early(sp, a, s)

            def store(n):
                sp.wait_ge(x2_done, n + 1)
                sp.dma_start(x2_v[n], x2t[:]).then_inc(x2_out, 16)
                sp.wait_ge(lg_sb, n + 1)
                sp.dma_start(lg_v[n], lg[:]).then_inc(lg_out, 16)

            def turn(n, i, half, first, last):
                sp.wait_ge(y_done, n * 2)
                sp.dma_start(xr[:], x1_v[n]).then_inc(xr_in, 16)
                if not last:
                    sp.wait_ge(x1T_done, n + 2)
                    sp.dma_start(xq[:], x1_v[(n + 2) % BLOCKS]).then_inc(xq_in, 16)
                if not first:
                    store(n - 1)
                if half == 1 and not last:
                    sp.wait_ge(pv_done, (n + 1) * XJ)
                    load_kv(i + 1)

            blocks(sp, turn)
            store(BLOCKS - 1)
            sp.wait_ge(zero_out, 32)
            sp.wait_ge(xq_in, 16 * (BLOCKS + 1))
            sp.wait_ge(x2_out, 16 * BLOCKS)
            sp.wait_ge(lg_out, 16 * BLOCKS)

        @block.gpsimd
        def _(pool):
            nc.gpsimd.memset(eps[:, 0:1], EPS).then_inc(set_up, 1)
            nc.gpsimd.memset(eps[:, 1:2], XD * EPS).then_inc(set_up, 1)
            for k in R:
                nc.gpsimd.memset(empty[k][:], 0.0).then_inc(set_up, 1)
            pool.wait_ge(set_up, 4)
            for k in R:
                nc.gpsimd.tensor_scalar(empty[k][:, D + 1:ROW], con[:, C_COL:C_COL + 1], float((2 * TILES + k) * P), None,
                                        ALU.add).then_inc(set_up, 1)

            def squares(m, b):
                for j in range(XJ):
                    pool.wait_ge(q_sb, m * XJ + j + 1)
                    pool.wait_ge(ss_done[j % 2], m * HX + j // 2)
                    nc.gpsimd.tensor_tensor(q2[j % 2][:], qT[b][:, j, :], qT[b][:, j, :], ALU.mult
                                            ).then_inc(q2_done[j % 2], 1)

            def turn(n, i, half, first, last):
                if not last:
                    squares(n + 1, 1 - half)

            squares(0, 0)
            blocks(pool, turn)

        @block.tensor
        def _(pe):
            pe.wait_ge(weights_in, 16)

            def x1_turned(m, first):
                pe.wait_ge(xq_in, m * 16 + 16)
                if not first:
                    pe.wait_ge(q_sb, m * XJ)
                    pe.wait_ge(rq_done, m)
                for c in range(KD):
                    for t in T:
                        mm = pe.transpose((Q, X)[c][:, t * P:(t + 1) * P], xq[:, t, c * P:(c + 1) * P], ident)
                mm.then_inc(x1T_done, 1)

            def queries(m, j):
                if j == 0:
                    pe.wait_ge(x1T_sb, m * KD + KD)
                pe.wait_ge(q_sb, m * XJ + j)
                for c in range(KD):
                    mm = pe.matmul(Q[:], w_q[:, c, j * P:(j + 1) * P], x1T[:, c, :], start=c == 0, stop=c == KD - 1)
                mm.then_inc(q_done, 1)

            def square_sums(m, j):
                pe.wait_ge(q2_done[j % 2], m * HX + j // 2 + 1)
                if j == 0:
                    pe.wait_ge(ss_sb, m)
                pe.matmul(SS[0:XH, :], con[:, C_HEAD + j * XH:C_HEAD + (j + 1) * XH], q2[j % 2][:], start=j == 0,
                          stop=j == XJ - 1).then_inc(ss_done[j % 2], 1)

            def sums_turned(m):
                pe.wait_ge(ss_sb, m + 1)
                nc.tensor.sem_inc(ss_seen, 1)
                for t in T:
                    mm = pe.transpose(X[:, t * XH:(t + 1) * XH], ss[:, t * P:(t + 1) * P],
                                      con[0:XH, C_ID:C_ID + XH])
                mm.then_inc(ssT_done, 1)

            def x2_turned(n, k):
                if k == 0:
                    pe.wait_ge(x2_done, n + 1)
                pe.wait_ge(x2T_sb, n * 2 + k)
                for t in R:
                    for c in range(KD):
                        mm = pe.transpose(X[:, (t * KD + c) * P:(t * KD + c + 1) * P],
                                          x2t[:, 2 * k + t, c * P:(c + 1) * P], ident)
                mm.then_inc(x2T_done, 1)

            def logits(n):
                pe.wait_ge(x2T_sb, n * 2 + 2)
                for t in T:
                    for c in range(KD):
                        mm = pe.matmul(X[:, t * NE:(t + 1) * NE], x2T[:, t, c, :], w_r[:, c, :], start=c == 0,
                                       stop=c == KD - 1)
                mm.then_inc(lg_done, 1)

            def turn(n, i, half, first, last):
                at = lambda j: n * XJ + j + 1

                def scores(j):
                    if j == 0:
                        pe.wait_ge(q_sb, at(XJ - 1))
                        pe.wait_ge(kv_in, i * 48 + 48)
                    pe.wait_ge(added, at(j) - 1)
                    for t in T:
                        lo = (t % 2) * 2 * KC
                        mm = pe.matmul(S[t // 2][:, lo:lo + 2 * KC], qT[half][:, j, t * P:(t + 1) * P],
                                       kT[:, j].rearrange("p r c -> p (r c)"), start=True, stop=True)
                    mm.then_inc(sc_done, 1)

                def weights_turned(j):
                    pe.wait_ge(scaled, at(j))
                    if j == 0 and not first:
                        pe.wait_ge(y_done, n * 2)
                    pe.wait_ge(tr_a, at(j) - 1)
                    pe.wait_ge(tr_b, at(j) - 1)
                    for r in R:
                        for t in T:
                            mm = pe.transpose(TB[r][0:CTX, t * P:(t + 1) * P], sc[j % 2][:, t, r, :], ident)
                    mm.then_inc(tr_done, 1)

                def values(j):
                    pe.wait_ge(o_sb, at(j) - 1)
                    pe.wait_ge(tr_a, at(j))
                    pe.wait_ge(tr_b, at(j))
                    for r in R:
                        h = 2 * j + r
                        mm = pe.matmul(V[r * XD:(r + 1) * XD, :], v[0:CTX, h * XD:(h + 1) * XD],
                                       aT[j % 2][0:CTX, r, :], start=True, stop=True)
                    mm.then_inc(pv_done, 1)

                scores(0)
                if not last:
                    x1_turned(n + 1, False)
                for j in range(XJ):
                    if j < XJ - 1:
                        scores(j + 1)
                    if not last:
                        queries(n + 1, j)
                        if j:
                            square_sums(n + 1, j - 1)
                    weights_turned(j)
                    if j:
                        values(j - 1)
                    if not first and j in (X2T_STEP, X2T_STEP + 1):
                        x2_turned(n - 1, j - X2T_STEP)
                    if not first and j == LG_STEP:
                        logits(n - 1)
                values(XJ - 1)
                if not last:
                    square_sums(n + 1, XJ - 1)
                pe.wait_ge(o_sb, at(XJ - 1))
                pe.wait_ge(tr_a, at(XJ - 1))
                pe.wait_ge(tr_b, at(XJ - 1))
                for t in T:
                    for j in range(XJ):
                        mm = pe.matmul(TB[t // 2][:, (t % 2) * D:(t % 2 + 1) * D], oT[:, j, t * P:(t + 1) * P],
                                       w_o[:, j, :], start=j == 0, stop=j == XJ - 1)
                    if t % 2:
                        mm.then_inc(wo_done, 1)
                if not last:
                    pe.wait_ge(lg_sb, n)
                    sums_turned(n + 1)

            x1_turned(0, True)
            for j in range(XJ):
                queries(0, j)
                if j:
                    square_sums(0, j - 1)
            square_sums(0, XJ - 1)
            sums_turned(0)
            pe.wait_ge(wo_in, 16 * 3)
            blocks(pe, turn)
            for k in R:
                x2_turned(BLOCKS - 1, k)
            logits(BLOCKS - 1)

        @block.scalar
        def _(act):
            def x1_out(m):
                act.wait_ge(x1T_done, m + 1)
                for c in range(KD):
                    nc.scalar.activation(x1T[:, c, :], (Q, X)[c][:], ACT.Copy).then_inc(x1T_sb, 1)

            def query_out(m, b, j):
                act.wait_ge(q_done, m * XJ + j + 1)
                nc.scalar.activation(qT[b][:, j, :], Q[:], ACT.Copy).then_inc(q_sb, 1)

            def sums_out(m):
                act.wait_ge(ss_done[0], m * HX + HX)
                act.wait_ge(ss_done[1], m * HX + HX)
                if not (isinstance(m, int) and m == 0):
                    act.wait_ge(ssT_done, m)
                nc.scalar.activation(ss[:], SS[0:XH, :], ACT.Sqrt, bias=eps[0:XH, 1:2]).then_inc(ss_sb, 1)

            def x2_sd(n):
                act.wait_ge(mv_done, n + 1)
                nc.scalar.activation(rstd[:], mv[:, :, 1], ACT.Sqrt, bias=eps[:, 0:1]).then_inc(sd_done, 1)

            def x2_out_of_psum(n, k):
                act.wait_ge(x2T_done, n * 2 + k + 1)
                nc.scalar.activation(x2T[:, 2 * k:2 * k + 2], X[:].rearrange("p (t c j) -> p t c j", c=KD, j=P),
                                     ACT.Copy).then_inc(x2T_sb, 1)

            def turn(n, i, half, first, last):
                at = lambda j: n * XJ + j + 1

                def exponentials(j):
                    act.wait_ge(nb_done, at(j))
                    for r in R:
                        for t in T:
                            e = nc.scalar.activation(sc[j % 2][:, t, r, :], sc[j % 2][:, t, r, :], ACT.Exp,
                                                     bias=nb[j % 2][:, t, r:r + 1],
                                                     scale=rq[:, t, 2 * j + r:2 * j + r + 1],
                                                     accum_out=den[j % 2][:, t, r:r + 1])
                    e.then_inc(exp_done, 1)

                def out_out(j):
                    act.wait_ge(pv_done, at(j))
                    nc.scalar.activation(oT[:, j, :], V[:], ACT.Copy).then_inc(o_sb, 1)

                if not last:
                    x1_out(n + 1)
                if not first:
                    x2_sd(n - 1)
                exponentials(0)
                for j in range(XJ):
                    if not last:
                        query_out(n + 1, 1 - half, j)
                    if j < XJ - 1:
                        exponentials(j + 1)
                    act.wait_ge(tr_done, at(j))
                    nc.scalar.activation(aT[j % 2][0:CTX, 0, :], TB[0][0:CTX, :], ACT.Copy).then_inc(tr_a, 1)
                    if j:
                        out_out(j - 1)
                    if not first and j in (X2T_STEP, X2T_STEP + 1):
                        x2_out_of_psum(n - 1, j - X2T_STEP)
                out_out(XJ - 1)
                if not last:
                    sums_out(n + 1)

            act.wait_ge(set_up, 3)
            x1_out(0)
            for j in range(XJ):
                query_out(0, 0, j)
            sums_out(0)
            blocks(act, turn)
            x2_sd(BLOCKS - 1)
            for k in R:
                x2_out_of_psum(BLOCKS - 1, k)

        @block.vector
        def _(dve):
            def sums_out(m):
                dve.wait_ge(ssT_done, m + 1)
                nc.vector.reciprocal(rq[:], X[:, 0:BLK * XH].rearrange("p (t h) -> p t h", t=BLK)
                                     ).then_inc(rq_done, 1)

            def norm(n):
                dve.wait_ge(sd_done, n + 1)
                nc.vector.reciprocal(rstd[:], rstd[:]).then_inc(r_done, 1)
                dve.wait_ge(r_done, n + 1)
                for t in T:
                    z = nc.vector.tensor_scalar(x2t[:, t, :], x2t[:, t, :], mv[:, t, 0:1], rstd[:, t:t + 1],
                                                ALU.subtract, ALU.mult)
                z.then_inc(x2_done, 1)

            def logits_out(n):
                dve.wait_ge(lg_out, n * 16)
                dve.wait_ge(lg_done, n + 1)
                nc.vector.tensor_copy(lg[:], X[:, 0:BLK * NE].rearrange("p (t e) -> p t e", e=NE)
                                      ).then_inc(lg_sb, 1)

            def turn(n, i, half, first, last):
                at = lambda j: n * XJ + j + 1

                def masked(j):
                    dve.wait_ge(sc_done, at(j))
                    if j == 0:
                        dve.wait_ge(kv_in, i * 48 + 48)
                    mask = madd[:].unsqueeze(1).unsqueeze(1).broadcast_to([P, 2, 2, CTX])
                    for k in W:
                        pairs = S[k][:, 0:4 * KC].rearrange("p (t r c) -> p t r c", t=2, r=2)[:, :, :, 0:CTX]
                        m = nc.vector.tensor_tensor(sc[j % 2][:, 2 * k:2 * k + 2], pairs, mask, ALU.add)
                    m.then_inc(added, 1)
                    dve.wait_ge(added, at(j))
                    nc.vector.tensor_reduce(mx[j % 2][:], sc[j % 2][:], AX_X, ALU.max).then_inc(mx_done, 1)
                    if j == 0:
                        dve.wait_ge(rq_done, n + 1)
                    dve.wait_ge(mx_done, at(j))
                    nc.vector.scalar_tensor_tensor(nb[j % 2][:], mx[j % 2][:], -1.0, rq[:, :, 2 * j:2 * j + 2],
                                                   ALU.mult, ALU.mult).then_inc(nb_done, 1)

                def normed(j):
                    dve.wait_ge(exp_done, at(j))
                    nc.vector.reciprocal(den[j % 2][:], den[j % 2][:]).then_inc(den_done, 1)
                    dve.wait_ge(den_done, at(j))
                    nc.vector.tensor_tensor(sc[j % 2][:], sc[j % 2][:],
                                            den[j % 2][:].unsqueeze(3).broadcast_to([P, BLK, 2, CTX]), ALU.mult
                                            ).then_inc(scaled, 1)

                masked(0)
                for j in range(XJ):
                    if j < XJ - 1:
                        masked(j + 1)
                    normed(j)
                    if j == 0 and not first:
                        norm(n - 1)
                    dve.wait_ge(tr_done, at(j))
                    nc.vector.tensor_copy(aT[j % 2][0:CTX, 1, :], TB[1][0:CTX, :]).then_inc(tr_b, 1)
                    if not first and j == LG_STEP:
                        logits_out(n - 1)
                dve.wait_ge(xr_in, n * 16 + 16)
                dve.wait_ge(x2_out, n * 16)
                for k in W:
                    dve.wait_ge(wo_done, n * 2 + k + 1)
                    nc.vector.tensor_tensor(x2t[:, 2 * k:2 * k + 2, :], xr[:, 2 * k:2 * k + 2, :],
                                            TB[k][:].rearrange("p (t d) -> p t d", d=D), ALU.add
                                            ).then_inc(y_done, 1)
                    dve.wait_ge(y_done, n * 2 + k + 1)
                    for t in (2 * k, 2 * k + 1):
                        nc.vector.bn_stats(stats[:, t, :], x2t[:, t, :]).then_inc(st_done, 1)
                dve.wait_ge(st_done, n * BLK + BLK)
                nc.vector.sem_inc(st_seen, 1)
                for t in T:
                    ag = nc.vector.bn_aggr(mv[:, t, :], stats[:, t, :])
                ag.then_inc(mv_done, 1)
                if not last:
                    sums_out(n + 1)

            sums_out(0)
            blocks(dve, turn)
            norm(BLOCKS - 1)
            logits_out(BLOCKS - 1)



EARLY_LOADS, LATE_LOADS = 2 * NE + 1, NE + 2


def load_experts_early(eng, a, s):
    for e in range(NE):
        for k, n in enumerate(("L0_ffn_gate_w", "L0_ffn_up_w")):
            eng.dma_start(s["w_gu"][:, e, :, k * FF:(k + 1) * FF], a[n][e].rearrange("(k p) n -> p k n", p=P)
                          ).then_inc(s["early_in"], 16)
    eng.dma_start(s["b_d"][:], a["L0_ffn_down_b"].unsqueeze(0).broadcast_to([P, NE, D])).then_inc(s["early_in"], 16)


def load_experts_late(eng, a, s):
    for k, n in enumerate(("L0_ffn_gate_b", "L0_ffn_up_b")):
        eng.dma_start(s["b_gu"][:, :, k * FF:(k + 1) * FF], a[n].unsqueeze(0).broadcast_to([P, NE, FF])
                      ).then_inc(s["late_in"], 16)
    for e in range(NE):
        eng.dma_start(s["w_d"][:, e], a["L0_ffn_down_w"][e].rearrange("(k p) n -> p k n", p=P)
                      ).then_inc(s["late_in"], 16)


def route_stage(nc, a, s):
    with ExitStack() as ctx:
        sb = lambda n, shape, dt=F32: ctx.enter_context(nc.sbuf_tensor(n, shape, dt))
        sem = ctx.enter_context(stage_semaphores(nc))
        con = s["con"]
        lg = sb("lg5", [P, TILES, NE])
        pr = sb("pr", [P, TILES, NE])
        pick = sb("pick", [P, TILES, NE])
        w = sb("w5", [P, TILES, NE])
        pos = sb("pos", [P, TILES, NE])
        cmp1, cmp2 = [s["x2_sb"][:, 8 * k:8 * k + 8, :].rearrange("p a d -> p (a d)").rearrange(
            "p (t e f) -> p t e f", e=NE, f=NE) for k in range(2)]
        row = sb("row5", [P, TILES])
        tot = sb("tot", [P, TILES, NE])
        cum = sb("cum", [P, NE, TILES])
        k128 = sb("k128", [P, TILES])
        many = sb("many", [P, NE, TILES])
        nt = sb("nt", [P, NE])
        ct = sb("ct", [P, NE])
        base = sb("base", [P, NE])
        of = sb("of", [P, FT, NE])
        off = sb("off", [P, FT])
        posf = sb("posf", [P, 2, TILES])
        R = 8
        wid = sb("wid", [P, TILES, 2, 2])
        xt = [sb(f"xt5_{q}", [P, 2, ROW]) for q in range(R)]
        idx = [sb(f"idx5_{q}", [P, 2], I32) for q in range(R)]
        ps_w = ctx.enter_context(nc.psum_tensor("ps_w", [P, 512], F32))
        ps_t = ctx.enter_context(nc.psum_tensor("ps_t", [P, 512], F32))
        loaded, steps, shifted, exped, picked, counted, tot_done, placed = [
            sem(f"r_{n}") for n in "loaded steps shifted exped picked counted tot_done placed".split()]
        x_in = [sem(f"r_x_in{q}") for q in range(R)]
        idx_done = [sem(f"r_idx_done{q}") for q in range(R)]
        seen = sem("r_seen")
        x_out = [sem(f"r_x_out{q}") for q in range(R)]
        tile_e = s["tile_e"]
        block = ctx.enter_context(nc.Block())
        ex = lambda t: t.unsqueeze(2).broadcast_to([P, TILES, NE])

        @block.sync
        def _(sp):
            sp.dma_start(lg[:], s["lg"].rearrange("t p e -> p t e")).then_inc(loaded, 16)
            with sp.Fori(0, TILES // R) as i:
                for q in range(R):
                    sp.wait_ge(x_out[q], i * 32)
                    sp.dma_start(xt[q][:, :, 0:D], s["x2"][i * R + q].unsqueeze(1).broadcast_to([P, 2, D])
                                 ).then_inc(x_in[q], 16)

        @block.scalar
        def _(act):
            act.wait_ge(shifted, 1)
            nc.scalar.activation(pr[:], pr[:], ACT.Exp).then_inc(exped, 1)
            load_experts_late(act, a, s)

        @block.tensor
        def _(pe):
            pe.wait_ge(loaded, 16)
            pe.wait_ge(picked, 1)
            m = pick[:].rearrange("p t e -> p (t e)")
            pe.matmul(ps_w[:, 0:TILES * NE], con[:, C_LT:C_LT + P], m, start=True, stop=True)
            pe.matmul(ps_t[:, 0:TILES * NE], con[:, C_ONE:C_ONE + P], m, start=True, stop=True).then_inc(counted, 1)

        @block.vector
        def _(dve):
            n = [0]

            def link(ins):
                n[0] += 1
                ins.then_inc(steps, 1)
                dve.wait_ge(steps, n[0])

            V = nc.vector
            dve.wait_ge(loaded, 16)
            link(V.tensor_reduce(row[:], lg[:], AX_X, ALU.max))
            V.tensor_tensor(pr[:], lg[:], ex(row[:]), ALU.subtract).then_inc(shifted, 1)
            link(V.tensor_scalar(k128[:], con[:, C_IOTA:C_IOTA + TILES], float(P), None, ALU.mult))
            dve.wait_ge(exped, 1)
            link(V.tensor_reduce(row[:], pr[:], AX_X, ALU.add))
            link(V.reciprocal(row[:], row[:]))
            link(V.tensor_tensor(pr[:], pr[:], ex(row[:]), ALU.mult))
            one = pr[:].unsqueeze(3).broadcast_to([P, TILES, NE, NE])
            other = pr[:].unsqueeze(2).broadcast_to([P, TILES, NE, NE])
            link(V.tensor_tensor(cmp1, other, one, ALU.is_gt))
            link(V.tensor_tensor(cmp2, other, one, ALU.is_equal))
            lower = con[:, C_LOW:C_LOW + NE * NE].rearrange("p (a b) -> p a b", b=NE)
            link(V.tensor_tensor(cmp2, cmp2, lower.unsqueeze(1).broadcast_to([P, TILES, NE, NE]), ALU.mult))
            link(V.tensor_tensor(cmp1, cmp1, cmp2, ALU.add))
            link(V.tensor_reduce(pick[:], cmp1, AX_X, ALU.add))
            V.tensor_scalar(pick[:], pick[:], 1.5, None, ALU.is_lt).then_inc(picked, 1)
            dve.wait_ge(picked, 1)
            link(V.tensor_tensor(w[:], pr[:], pick[:], ALU.mult))
            link(V.tensor_reduce(row[:], w[:], AX_X, ALU.add))
            link(V.tensor_scalar(row[:], row[:], 1e-9, None, ALU.add))
            link(V.reciprocal(row[:], row[:]))
            link(V.tensor_tensor(w[:], w[:], ex(row[:]), ALU.mult))
            dve.wait_ge(counted, 1)
            link(V.tensor_copy(tot[:], ps_t[:, 0:TILES * NE].rearrange("p (t e) -> p t e", e=NE)))
            for e in range(NE):
                sc = V.tensor_tensor_scan(cum[:, e, :], con[:, C_ONE:C_ONE + TILES], tot[:, :, e], 0.0,
                                          ALU.mult, ALU.add)
            link(sc)
            link(V.tensor_tensor(many[:], cum[:, :, TILES - 1:TILES].broadcast_to([P, NE, TILES]),
                                 k128[:].unsqueeze(1).broadcast_to([P, NE, TILES]), ALU.is_gt))
            link(V.tensor_reduce(nt[:], many[:], AX_X, ALU.add))
            link(V.tensor_tensor_scan(ct[:], con[:, C_ONE:C_ONE + NE], nt[:], 0.0, ALU.mult, ALU.add))
            link(V.tensor_tensor(base[:], ct[:], nt[:], ALU.subtract))
            link(V.tensor_scalar(base[:], base[:], float(P), None, ALU.mult))
            link(V.tensor_tensor(pos[:], cum[:].rearrange("p e t -> p t e"), tot[:], ALU.subtract))
            link(V.tensor_tensor(pos[:], pos[:], ps_w[:, 0:TILES * NE].rearrange("p (t e) -> p t e", e=NE), ALU.add))
            link(V.tensor_tensor(pos[:], pos[:], base[:].unsqueeze(1).broadcast_to([P, TILES, NE]), ALU.add))
            link(V.tensor_tensor(pos[:], pos[:], pick[:], ALU.mult))
            link(V.tensor_reduce(posf[:, 1, :], pos[:], AX_X, ALU.max))
            link(V.tensor_reduce(posf[:, 0, :], pos[:], AX_X, ALU.add))
            link(V.tensor_tensor(posf[:, 0, :], posf[:, 0, :], posf[:, 1, :], ALU.subtract))
            link(V.tensor_tensor(pick[:], pos[:], ex(posf[:, 1, :]), ALU.is_equal))
            link(V.tensor_tensor(pick[:], pick[:], w[:], ALU.mult))
            link(V.tensor_reduce(wid[:, :, 1, 0], pick[:], AX_X, ALU.add))
            link(V.tensor_tensor(w[:], w[:], pick[:], ALU.subtract))
            V.tensor_reduce(wid[:, :, 0, 0], w[:], AX_X, ALU.add)
            for k in range(2):
                ids = V.tensor_scalar(wid[:, :, k, 1], k128[:], con[:, C_COL:C_COL + 1], float(k * TILES * P),
                                      ALU.add, ALU.add)
            link(ids)
            link(V.tensor_tensor(of[:], con[:, C_IOTA:C_IOTA + FT].unsqueeze(2).broadcast_to([P, FT, NE]),
                                 ct[:].unsqueeze(1).broadcast_to([P, FT, NE]), ALU.is_ge))
            link(V.tensor_reduce(off[:], of[:], AX_X, ALU.add))
            link(V.tensor_scalar(off[:], off[:], float(NE - 1), None, ALU.min))
            V.tensor_copy(tile_e[:, 0:FT], off[:]).then_inc(placed, 1)
            with dve.Fori(0, TILES // R) as i:
                for q in range(R):
                    dve.wait_ge(x_out[q], i * 32)
                    V.tensor_scalar(xt[q][:, :, D:ROW], wid[:, i * R + q], 1.0, None, ALU.mult)
                    V.tensor_copy(idx[q][:], posf[:, :, i * R + q]).then_inc(idx_done[q], 1)

        @block.gpsimd
        def _(pool):
            with pool.Fori(0, TILES // R) as i:
                for q in range(R):
                    pool.wait_ge(idx_done[q], i + 1)
                    pool.wait_ge(x_in[q], i * 16 + 16)
                    nc.gpsimd.sem_inc(seen, 1)
                    for k in range(2):
                        nc.gpsimd.indirect_dma_start(
                            out=s["xs"].rearrange("t p d -> (t p) d"),
                            out_offset=bass.IndirectOffsetOnAxis(ap=idx[q][:, k:k + 1], axis=0),
                            in_=xt[q][:, k, :], in_offset=None).then_inc(x_out[q], 16)
            for q in range(R):
                pool.wait_ge(x_out[q], 32 * TILES // R)
            pool.wait_ge(placed, 1)


def expert_stage(nc, a, s):
    with ExitStack() as ctx:
        sb = lambda n, shape, dt=F32: ctx.enter_context(nc.sbuf_tensor(n, shape, dt))
        bank = lambda n: ctx.enter_context(nc.psum_tensor(n, [P, 512], F32))
        sem = ctx.enter_context(stage_semaphores(nc))
        Q = range(2)
        two = lambda n, shape: [sb(f"{n}{q}", shape) for q in Q]
        sems = lambda n: [sem(f"e_{n}{q}") for q in Q]
        FK = FF // P
        ident = s["con"][:, C_ID:C_ID + P]
        w_gu, w_d, b_gu, b_d, early_in, late_in = (s[n] for n in "w_gu w_d b_gu b_d early_in late_in".split())
        xs = two("xs6_", [P, D])
        end = two("end6_", [P, ROW - D])
        idx = [sb(f"idx6_{q}", [P, 1], I32) for q in Q]
        seen = sem("e_seen")
        xsT = two("xsT", [P, KD, P])
        g = two("g6_", [P, FF])
        u = two("u6_", [P, FF])
        hT = two("hT", [P, FK, P])
        o = two("o6_", [P, D])
        pG = [bank(f"pG{q}") for q in Q]
        pU = [bank(f"pU{q}") for q in Q]
        pX, pH = bank("pX6"), bank("pH6")
        pD = [bank(f"pD{q}") for q in Q]
        x2_in = sem("e_x2_in")
        xs_in, xT_done, xT_sb, gu_done, gb_done, ub_done, silu_done, h_done, hT_done, hT_sb, d_done, ob_done, o_done, o_out, end_in = [
            sems(n) for n in ("xs_in xT_done xT_sb gu_done gb_done ub_done silu_done h_done hT_done hT_sb d_done "
                              "ob_done o_done o_out end_in").split()]
        tile_e = s["tile_e"]
        LOOPS = (FT - 3) // 2
        block = ctx.enter_context(nc.Block())

        def turns(eng, turn):
            tile = lambda j: (j % 2, j // 2, j)
            turn(None, None, None, tile(0))
            turn(tile(0), None, None, tile(1))
            turn(tile(1), tile(0), None, tile(2))
            turn(tile(2), tile(1), tile(0), tile(3))
            with eng.Fori(0, LOOPS) as i:
                at = lambda k: (k % 2, i + k // 2, i * 2 + k)
                turn(at(3), at(2), at(1), at(4))
                turn(at(4), at(3), at(2), at(5))
            turn(None, tile(FT - 1), tile(FT - 2), None)
            turn(None, None, tile(FT - 1), None)

        @block.sync
        def _(sp):

            def load(t):
                q, m, j = t
                sp.wait_ge(xT_done[q], m)
                sp.dma_start(xs[q][:], s["xs"][j][:, 0:D]).then_inc(xs_in[q], 16)

            def turn(t, before, earlier, after):
                if after:
                    load(after)

            turns(sp, turn)

        @block.gpsimd
        def _(pool):
            def turn(t, before, earlier, after):
                if earlier:
                    q, m, j = earlier
                    pool.wait_ge(o_done[q], m + 1)
                    nc.gpsimd.sem_inc(seen, 1)
                    nc.gpsimd.indirect_dma_start(
                        out=s["y"].rearrange("t p d -> (t p) d"),
                        out_offset=bass.IndirectOffsetOnAxis(ap=idx[q][:], axis=0),
                        in_=o[q][:], in_offset=None).then_inc(o_out[q], 16)
                if t:
                    q, m, j = t
                    pool.dma_start(end[q][:], s["xs"][j][:, D:ROW]).then_inc(end_in[q], 16)

            turns(pool, turn)
            pool.wait_ge(o_out[0], 16 * ((FT + 1) // 2))
            pool.wait_ge(o_out[1], 16 * (FT // 2))

        @block.tensor
        def _(pe):
            pe.wait_ge(early_in, EARLY_LOADS * 16)
            pe.wait_ge(late_in, LATE_LOADS * 16)

            def x_turned(t):
                q, m, _ = t
                pe.wait_ge(xs_in[q], m * 16 + 16)
                pe.wait_ge(xT_sb[1 - q], m if q == 0 else m + 1)
                for c in range(KD):
                    mm = pe.transpose(pX[:, c * P:(c + 1) * P], xs[q][:, c * P:(c + 1) * P], ident)
                mm.then_inc(xT_done[q], 1)

            def expert(t):
                _, _, j = t
                return pe.value_load(tile_e[0:1, j:j + 1] if isinstance(j, int) else tile_e[0:1, bass.ds(j, 1)],
                                     min_val=0, max_val=NE - 1)

            def gate_up(t, e):
                q, m, j = t
                pe.wait_ge(xT_sb[q], m + 1)
                pe.wait_ge(ub_done[q], m)
                pe.wait_ge(gb_done[q], m)
                for k, bk in enumerate((pG[q], pU[q])):
                    for c in range(KD):
                        mm = pe.matmul(bk[:], xsT[q][:, c, :], w_gu[:, bass.ds(e, 1), c, k * FF:(k + 1) * FF],
                                       start=c == 0, stop=c == KD - 1)
                mm.then_inc(gu_done[q], 1)

            def h_turned(t):
                q, m, j = t
                pe.wait_ge(h_done[q], m + 1)
                pe.wait_ge(hT_sb[1 - q], m if q == 0 else m + 1)
                for k in range(FK):
                    mm = pe.transpose(pH[:, k * P:(k + 1) * P], g[q][:, k * P:(k + 1) * P], ident)
                mm.then_inc(hT_done[q], 1)

            def down(t, e):
                q, m, j = t
                pe.wait_ge(hT_sb[q], m + 1)
                pe.wait_ge(ob_done[q], m)
                for k in range(FK):
                    mm = pe.matmul(pD[q][:, 0:D], hT[q][:, k, :], w_d[:, bass.ds(e, 1), k, :], start=k == 0,
                                   stop=k == FK - 1)
                mm.then_inc(d_done[q], 1)

            def turn(t, before, earlier, after):
                e, e_earlier = t and expert(t), earlier and expert(earlier)
                if t:
                    gate_up(t, e)
                if after:
                    x_turned(after)
                if before:
                    h_turned(before)
                if earlier:
                    down(earlier, e_earlier)

            turns(pe, turn)

        @block.scalar
        def _(act):
            act.dma_start(s["x2_sb"][:], s["x2"].rearrange("t p d -> p t d")).then_inc(x2_in, 16)

            def x_out(t):
                q, m, _ = t
                act.wait_ge(xT_done[q], m + 1)
                act.wait_ge(gu_done[q], m)
                nc.scalar.activation(xsT[q][:], pX[:, 0:D].rearrange("p (c j) -> p c j", c=KD), ACT.Copy
                                     ).then_inc(xT_sb[q], 1)

            def silu(t):
                q, m, _ = t
                act.wait_ge(gb_done[q], m + 1)
                nc.scalar.activation(g[q][:], g[q][:], ACT.Silu).then_inc(silu_done[q], 1)

            def h_out(t):
                q, m, _ = t
                act.wait_ge(hT_done[q], m + 1)
                act.wait_ge(d_done[q], m)
                nc.scalar.activation(hT[q][:], pH[:].rearrange("p (k j) -> p k j", k=FK), ACT.Copy
                                     ).then_inc(hT_sb[q], 1)

            def turn(t, before, earlier, after):
                if after:
                    x_out(after)
                if before:
                    h_out(before)
                if t:
                    silu(t)

            turns(act, turn)
            act.wait_ge(x2_in, 16)

        @block.vector
        def _(dve):
            dve.wait_ge(early_in, EARLY_LOADS * 16)
            dve.wait_ge(late_in, LATE_LOADS * 16)

            def biased(t):
                q, m, j = t
                e = dve.value_load(tile_e[0:1, j:j + 1] if isinstance(j, int) else tile_e[0:1, bass.ds(j, 1)],
                                   min_val=0, max_val=NE - 1)
                dve.wait_ge(gu_done[q], m + 1)
                dve.wait_ge(hT_done[q], m)
                nc.vector.tensor_tensor(g[q][:], pG[q][:], b_gu[:, bass.ds(e, 1), 0:FF], ALU.add
                                        ).then_inc(gb_done[q], 1)
                nc.vector.tensor_tensor(u[q][:], pU[q][:], b_gu[:, bass.ds(e, 1), FF:2 * FF], ALU.add
                                        ).then_inc(ub_done[q], 1)

            def hidden(t):
                q, m, j = t
                dve.wait_ge(silu_done[q], m + 1)
                dve.wait_ge(ub_done[q], m + 1)
                nc.vector.tensor_tensor(g[q][:], g[q][:], u[q][:], ALU.mult).then_inc(h_done[q], 1)

            def out(t):
                q, m, j = t
                e = dve.value_load(tile_e[0:1, j:j + 1] if isinstance(j, int) else tile_e[0:1, bass.ds(j, 1)],
                                   min_val=0, max_val=NE - 1)
                dve.wait_ge(d_done[q], m + 1)
                dve.wait_ge(end_in[q], m * 16 + 16)
                dve.wait_ge(o_out[q], m * 16)
                nc.vector.tensor_copy(idx[q][:], end[q][:, 1:2])
                nc.vector.tensor_tensor(o[q][:], pD[q][:, 0:D], b_d[:, bass.ds(e, 1), :], ALU.add
                                        ).then_inc(ob_done[q], 1)
                dve.wait_ge(ob_done[q], m + 1)
                nc.vector.tensor_scalar(o[q][:], o[q][:], end[q][:, 0:1], None, ALU.mult).then_inc(o_done[q], 1)

            def turn(t, before, earlier, after):
                if t:
                    biased(t)
                if earlier:
                    out(earlier)
                if t:
                    hidden(t)

            turns(dve, turn)


def final_stage(nc, a, s, out):
    with ExitStack() as ctx:
        sb = lambda n, shape, dt=F32: ctx.enter_context(nc.sbuf_tensor(n, shape, dt))
        sem = ctx.enter_context(stage_semaphores(nc))
        R, T = range(4), range(BLK)
        sems = lambda n: [sem(f"f_{n}{q}") for q in R]
        x2 = s["x2_sb"]
        y = [sb(f"y7_{q}", [P, 2, BLK, D]) for q in R]
        z = [sb(f"z7_{q}", [P, BLK, D]) for q in R]
        stats = [sb(f"stats7_{q}", [P, BLK, 6]) for q in R]
        mv = [sb(f"mv7_{q}", [P, BLK, 2]) for q in R]
        rstd = [sb(f"rstd7_{q}", [P, BLK]) for q in R]
        eps = sb("eps7", [P, 1])
        set_up, seen = sem("f_set_up"), sem("f_seen")
        y_in, a_done, b_done, st_done, mv_done, sd_done, r_done, z_done, z_out = [
            sems(n) for n in "y_in a_done b_done st_done mv_done sd_done r_done z_done z_out".split()]
        y_v = s["y"][0:2 * TILES].rearrange("(k n t) p d -> k n p t d", k=2, t=BLK)
        out_v = out.rearrange("b (c t p) d -> (b c) p t d", p=P, t=BLK)
        USES = BLOCKS // len(R)
        block = ctx.enter_context(nc.Block())

        @block.sync
        def _(sp):
            with sp.Fori(0, USES) as i:
                for q in R:
                    sp.wait_ge(b_done[q], i)
                    for k in range(2):
                        sp.dma_start(y[q][:, k], y_v[k, i * len(R) + q]).then_inc(y_in[q], 16)
            for q in R:
                sp.wait_ge(z_out[q], 16 * USES)

        @block.gpsimd
        def _(pool):
            nc.gpsimd.memset(eps[:], EPS).then_inc(set_up, 1)

        @block.scalar
        def _(act):
            act.wait_ge(set_up, 1)
            with act.Fori(0, USES) as i:
                for q in R:
                    act.wait_ge(mv_done[q], i + 1)
                    nc.scalar.activation(rstd[q][:], mv[q][:, :, 1], ACT.Sqrt, bias=eps[:, 0:1]
                                         ).then_inc(sd_done[q], 1)
                for q in R:
                    act.wait_ge(z_done[q], i + 1)
                    act.dma_start(out_v[i * len(R) + q], z[q][:]).then_inc(z_out[q], 16)

        @block.vector
        def _(dve):
            def finish(q, i):
                dve.wait_ge(sd_done[q], i + 1)
                nc.vector.reciprocal(rstd[q][:], rstd[q][:]).then_inc(r_done[q], 1)
                dve.wait_ge(r_done[q], i + 1)
                for t in T:
                    last = nc.vector.tensor_scalar(z[q][:, t, :], z[q][:, t, :], mv[q][:, t, 0:1],
                                                rstd[q][:, t:t + 1], ALU.subtract, ALU.mult)
                last.then_inc(z_done[q], 1)

            with dve.Fori(0, USES) as i:
                for q in R:
                    dve.wait_ge(y_in[q], i * 32 + 32)
                    dve.wait_ge(z_out[q], i * 16)
                    nc.vector.tensor_tensor(z[q][:], y[q][:, 0], y[q][:, 1], ALU.add).then_inc(b_done[q], 1)
                    dve.wait_ge(b_done[q], i + 1)
                    nc.vector.tensor_tensor(z[q][:], z[q][:], x2[:, bass.ds(i * BLK * len(R) + q * BLK, BLK), :], ALU.add
                                            ).then_inc(a_done[q], 1)
                    dve.wait_ge(a_done[q], i + 1)
                    for t in T:
                        nc.vector.bn_stats(stats[q][:, t, :], z[q][:, t, :]).then_inc(st_done[q], 1)
                    dve.wait_ge(st_done[q], i * BLK + BLK)
                    nc.vector.sem_inc(seen, 1)
                    for t in T:
                        ag = nc.vector.bn_aggr(mv[q][:, t, :], stats[q][:, t, :])
                    ag.then_inc(mv_done[q], 1)
                    if q:
                        finish(q - 1, i)
                finish(len(R) - 1, i)




def build(nc, a, out):
    dram = lambda n, shape: nc.dram_tensor(n, shape, F32, kind="Internal").ap()
    s = {
        "qkvg": dram("qkvg", [TILES, P, QKV + DV]),
        "gb": dram("gb", [TILES, P, 2 * H]),
        "x1": dram("x1", [TILES, P, D]),
        "kT": dram("kT", [BATCH, P, XW // P, 2, KC]),
        "v": dram("v", [BATCH, CTX, XW]),
        "madd": dram("madd", [BATCH, P, CTX]),
        "x2": dram("x2", [TILES, P, D]),
        "y": dram("y", [2 * TILES + 2, P, D]),
        "lg": dram("lg", [TILES, P, NE]),
        "xs": dram("xs", [FT + 1, P, ROW]),
    }
    with ExitStack() as kept, stage_semaphores(nc) as sem:
        sb = lambda ctx, n, shape, dt=F32: ctx.enter_context(nc.sbuf_tensor(n, shape, dt))
        s["con"] = sb(kept, "con", [P, C_N])
        project_stage(nc, a, s)
        delta_stage(nc, a, s)
        context_stage(nc, a, s)
        s["w_gu"] = sb(kept, "w_gu", [P, NE, KD, 2 * FF])
        s["b_d"] = sb(kept, "b_d", [P, NE, D])
        s["early_in"], s["late_in"] = sem("early_in"), sem("late_in")
        cross_stage(nc, a, s)
        s["x2_sb"] = sb(kept, "x2_sb", [P, TILES, D])
        with ExitStack() as experts:
            s["tile_e"] = sb(experts, "tile_e", [P, FT + 1], I32)
            s["w_d"] = sb(experts, "w_d", [P, NE, FF // P, D])
            s["b_gu"] = sb(experts, "b_gu", [P, NE, 2 * FF])
            route_stage(nc, a, s)
            expert_stage(nc, a, s)
        final_stage(nc, a, s, out)


_INS = ['x', 'ctx_1024', '_lenS2', 'L0_attn_ln_w', 'L0_attn_ln_b', 'L0_attn_Wq', 'L0_attn_Wk', 'L0_attn_Wv',
        'L0_attn_conv_q', 'L0_attn_conv_k', 'L0_attn_conv_v', 'L0_attn_Wb', 'L0_attn_Wa', 'L0_attn_A_log',
        'L0_attn_dt_bias', 'L0_attn_Wg', 'L0_attn_norm_w', 'L0_attn_Wo', 'L0_xattn_Wq', 'L0_xattn_Wk',
        'L0_xattn_Wv', 'L0_xattn_Wo', 'L0_xattn_q_norm_w', 'L0_xattn_k_norm_w', 'L0_ffn_router_w',
        'L0_ffn_gate_w', 'L0_ffn_gate_b', 'L0_ffn_up_w', 'L0_ffn_up_b', 'L0_ffn_down_w', 'L0_ffn_down_b']


def kernel(**inputs):
    import concourse.bacc as _bacc
    from concourse.bass_utils import run_bass_kernel_spmd as _run

    nc = _bacc.Bacc("TRN2", target_bir_lowering=False, num_devices=1)
    arrays, aps = {}, {}
    for name in _INS:
        arrays[f"in_{name}"] = np.ascontiguousarray(inputs[name])
    arrays["in_consts"] = constants()
    for name, v in arrays.items():
        aps[name[3:]] = nc.dram_tensor(name, v.shape, mybir.dt.from_np(v.dtype), kind="ExternalInput").ap()
    out = nc.dram_tensor("out", [BATCH, SEQ, D], F32, kind="ExternalOutput").ap()
    build(nc, aps, out)
    r = _run(nc, [arrays], core_ids=[0])
    return r.results[0]["out"]
```
